# Optimizing a Trainium2 kernel written in Bass

```python
import numpy as np
import jax
import jax.numpy as jnp

def _softmax(x, axis=-1):
    return jax.nn.softmax(x, axis=axis)

def _gelu(x):
    return jax.nn.gelu(x, approximate=True)

def _silu(x):
    return jax.nn.silu(x)

def _sigmoid(x):
    return jax.nn.sigmoid(x)

def _layernorm(x, axis=-1, eps=1e-05):
    m = jnp.mean(x, axis=axis, keepdims=True)
    v = jnp.var(x, axis=axis, keepdims=True)
    return (x - m) / jnp.sqrt(v + eps)

def _scatter_add(tgt, idx, src, axis=0):
    return tgt.at[idx].add(src)

def _segment_sum(src, seg, n):
    return jax.ops.segment_sum(src, seg, n)
kernel_name = 'mk_perceiver_d1_seqx_r8_eaae9c'

def setup_inputs(seed: int=0):
    np.random.seed(seed)
    _w = jnp.asarray

    def _rec_inputs():
        import jax
        import jax.numpy as jnp
        _rk = jax.random.key(seed)
        x = 0.0003765 + 1 * jax.random.normal(jax.random.fold_in(_rk, 1), (64, 32, 128), jnp.float32)
        _lenS = 32 - jax.random.randint(jax.random.fold_in(_rk, 7), (64,), 0, max(1, 32 // 4) + 1, jnp.int32)
        _lenS2 = 257 - jax.random.randint(jax.random.fold_in(_rk, 8), (64,), 0, max(1, 257 // 4) + 1, jnp.int32)
        _ctx_1024P = jax.random.normal(jax.random.fold_in(_rk, 11), (64, 16, 128), jnp.float32)
        _ctx_1024c = jax.random.dirichlet(jax.random.fold_in(_rk, 511), 0.3 * jnp.ones((16,), jnp.float32), (64, 257))
        _ctx_1024t = jnp.einsum('bsk,bkd->bsd', _ctx_1024c, _ctx_1024P)
        _ctx_1024t = _ctx_1024t * jax.lax.rsqrt(jnp.mean(jnp.square(_ctx_1024t)) + 1e-12) * 0.953939
        ctx_1024 = -0.000292821 + 1.00034 * (_ctx_1024t + 0.3 * jax.random.normal(jax.random.fold_in(_rk, 611), (64, 257, 128), jnp.float32))
        return (x, ctx_1024)
    x, ctx_1024 = _rec_inputs()

    def _L0_xattn_setup():
        import jax, jax.numpy as jnp
        import numpy as np
        EMBED = 128
        HEADS = 16
        HEAD_DIM = EMBED // HEADS
        key = jax.random.key(seed)
        ks = jax.random.split(key, 8)
        B, S = (2, 256)
        return {'values': jax.random.normal(ks[0], (B, S, EMBED), jnp.float32), 'keys': jax.random.normal(ks[1], (B, S, EMBED), jnp.float32), 'query': jax.random.normal(ks[2], (B, S, EMBED), jnp.float32), 'Wv': jax.random.normal(ks[3], (EMBED, EMBED), jnp.float32) * EMBED ** (-0.5), 'Wk': jax.random.normal(ks[4], (EMBED, EMBED), jnp.float32) * EMBED ** (-0.5), 'Wq': jax.random.normal(ks[5], (EMBED, EMBED), jnp.float32) * EMBED ** (-0.5), 'Wo': jax.random.normal(ks[6], (EMBED, EMBED), jnp.float32) * EMBED ** (-0.5), 'bo': jnp.zeros((EMBED,), jnp.float32)}
    _L0_xattn_all = _L0_xattn_setup()
    _L0_xattn_in = {k: v for k, v in _L0_xattn_all.items() if k in ('Wv', 'Wk', 'Wq', 'Wo', 'bo')}
    del _L0_xattn_all

    def _L0_attn_setup():
        import jax, jax.numpy as jnp
        import numpy as np
        B, L = (2, 128)
        D_MODEL, D_CKV, D_CQ = (128, 32, 64)
        N_HEAD, D_HEAD, D_ROPE = (8, 64, 32)
        N_IDX_HEAD = 4
        K_TS, LW = (96, 64)
        ROPE_BASE = 10000.0

        def _pope(x, angles):
            cos, sin = (jnp.cos(angles), jnp.sin(angles))
            mu1, mu2 = jnp.split(jax.nn.softplus(x), 2, axis=-1)
            return jnp.concatenate([mu1 * cos - mu2 * sin, mu1 * sin + mu2 * cos], axis=-1)

        def _forward(x, W_dkv, W_uk, W_uv, W_dq, W_uq, W_qr, W_kr, W_out, idx_wq, idx_wk, idx_w, raw_delta):
            B_, L_, _ = x.shape
            c_kv = x @ W_dkv
            q_i = (x @ idx_wq).reshape(B_, L_, N_IDX_HEAD, D_HEAD)
            k_i = x @ idx_wk
            s_i = jax.nn.relu(jnp.einsum('bthd,bsd->bths', q_i, k_i))
            I = jnp.einsum('bths,h->bts', s_i, idx_w)
            qpos = jnp.arange(L_)[:, None]
            kpos = jnp.arange(L_)[None, :]
            local = (kpos >= qpos - LW + 1) & (kpos <= qpos)
            causal = kpos > qpos
            I = jnp.where(local[None], jnp.inf, I)
            I = jnp.where(causal[None], -jnp.inf, I)
            kk = min(K_TS, L_)
            _, idx = jax.lax.top_k(I, kk)
            bi = jnp.arange(B_)[:, None, None]
            key_c = (c_kv @ W_uk)[bi, idx].reshape(B_, L_, kk, N_HEAD, D_HEAD)
            value = (c_kv @ W_uv)[bi, idx].reshape(B_, L_, kk, N_HEAD, D_HEAD)
            c_q = x @ W_dq
            query_c = (c_q @ W_uq).reshape(B_, L_, N_HEAD, D_HEAD)
            half = D_ROPE // 2
            theta = 1.0 / ROPE_BASE ** (2.0 * jnp.arange(half, dtype=jnp.float32) / D_ROPE)
            delta = -2.0 * jnp.pi * jax.nn.sigmoid(raw_delta)
            angles_q = jnp.arange(L_, dtype=jnp.float32)[:, None] * theta[None, :] + delta
            query_r = _pope((c_q @ W_qr).reshape(B_, L_, N_HEAD, D_ROPE), angles_q[None, :, None, :])
            kr_sel = (x @ W_kr)[bi, idx]
            angles_k = jnp.arange(kk, dtype=jnp.float32)[:, None] * theta[None, :] + delta
            key_r = _pope(kr_sel, angles_k[None, None, :, :])
            scale = (D_HEAD + D_ROPE) ** (-0.5)
            q_c = query_c.transpose(0, 2, 1, 3)
            q_r = query_r.transpose(0, 2, 1, 3)
            k_c = key_c.transpose(0, 3, 1, 2, 4)
            v = value.transpose(0, 3, 1, 2, 4)
            scores = (jnp.einsum('bhld,bhlkd->bhlk', q_c, k_c) + jnp.einsum('bhld,blkd->bhlk', q_r, key_r)) * scale
            attn = jax.nn.softmax(scores.astype(jnp.float32), axis=-1).astype(v.dtype)
            out = jnp.einsum('bhlk,bhlkd->bhld', attn, v)
            out = out.transpose(0, 2, 1, 3).reshape(B_, L_, N_HEAD * D_HEAD)
            return out @ W_out
        key = jax.random.key(seed)
        ks = jax.random.split(key, 14)

        def w(k, shape, fan_in):
            return jax.random.normal(k, shape, dtype=jnp.float32) * fan_in ** (-0.5)
        return {'x': jax.random.normal(ks[0], (B, L, D_MODEL), dtype=jnp.float32), 'W_dkv': w(ks[1], (D_MODEL, D_CKV), D_MODEL), 'W_uk': w(ks[2], (D_CKV, N_HEAD * D_HEAD), D_CKV), 'W_uv': w(ks[3], (D_CKV, N_HEAD * D_HEAD), D_CKV), 'W_dq': w(ks[4], (D_MODEL, D_CQ), D_MODEL), 'W_uq': w(ks[5], (D_CQ, N_HEAD * D_HEAD), D_CQ), 'W_qr': w(ks[6], (D_CQ, N_HEAD * D_ROPE), D_CQ), 'W_kr': w(ks[7], (D_MODEL, D_ROPE), D_MODEL), 'W_out': w(ks[8], (N_HEAD * D_HEAD, D_MODEL), N_HEAD * D_HEAD), 'idx_wq': w(ks[9], (D_MODEL, N_IDX_HEAD * D_HEAD), D_MODEL), 'idx_wk': w(ks[10], (D_MODEL, D_HEAD), D_MODEL), 'idx_w': jnp.ones((N_IDX_HEAD,), dtype=jnp.float32), 'raw_delta': jax.random.normal(ks[11], (D_ROPE // 2,), dtype=jnp.float32) * 0.1}
    _L0_attn_all = _L0_attn_setup()
    _L0_attn_in = {k: v for k, v in _L0_attn_all.items() if k in ('W_dkv', 'W_uk', 'W_uv', 'W_dq', 'W_uq', 'W_qr', 'W_kr', 'W_out', 'idx_wq', 'idx_wk', 'idx_w', 'raw_delta')}
    del _L0_attn_all

    def _L0_ffn_setup():
        import jax, jax.numpy as jnp
        import numpy as np
        TOP_K = 2
        key = jax.random.key(seed)
        k0, k1, k2, k3, k4 = jax.random.split(key, 5)
        B, S, H, I, E = (4, 256, 128, 352, 8)
        s_h = 1.0 / np.sqrt(H)
        s_i = 1.0 / np.sqrt(I)
        return {'x': jax.random.normal(k0, (B, S, H), jnp.float32), 'w_router': jax.random.normal(k1, (E, H), jnp.float32) * s_h, 'w_gate': jax.random.normal(k2, (E, I, H), jnp.float32) * s_h, 'w_up': jax.random.normal(k3, (E, I, H), jnp.float32) * s_h, 'w_down': jax.random.normal(k4, (E, H, I), jnp.float32) * s_i}
    _L0_ffn_all = _L0_ffn_setup()
    _L0_ffn_in = {k: v for k, v in _L0_ffn_all.items() if k in ('w_router', 'w_gate', 'w_up', 'w_down')}
    del _L0_ffn_all
    return {'x': x, 'ctx_1024': ctx_1024, 'L0_xattn_Wv': _L0_xattn_in['Wv'], 'L0_xattn_Wk': _L0_xattn_in['Wk'], 'L0_xattn_Wq': _L0_xattn_in['Wq'], 'L0_xattn_Wo': _L0_xattn_in['Wo'], 'L0_xattn_bo': _L0_xattn_in['bo'], 'L0_attn_W_dkv': _L0_attn_in['W_dkv'], 'L0_attn_W_uk': _L0_attn_in['W_uk'], 'L0_attn_W_uv': _L0_attn_in['W_uv'], 'L0_attn_W_dq': _L0_attn_in['W_dq'], 'L0_attn_W_uq': _L0_attn_in['W_uq'], 'L0_attn_W_qr': _L0_attn_in['W_qr'], 'L0_attn_W_kr': _L0_attn_in['W_kr'], 'L0_attn_W_out': _L0_attn_in['W_out'], 'L0_attn_idx_wq': _L0_attn_in['idx_wq'], 'L0_attn_idx_wk': _L0_attn_in['idx_wk'], 'L0_attn_idx_w': _L0_attn_in['idx_w'], 'L0_attn_raw_delta': _L0_attn_in['raw_delta'], 'L0_ffn_w_router': _L0_ffn_in['w_router'], 'L0_ffn_w_gate': _L0_ffn_in['w_gate'], 'L0_ffn_w_up': _L0_ffn_in['w_up'], 'L0_ffn_w_down': _L0_ffn_in['w_down']}

def reference(x, ctx_1024, L0_xattn_Wv, L0_xattn_Wk, L0_xattn_Wq, L0_xattn_Wo, L0_xattn_bo, L0_attn_W_dkv, L0_attn_W_uk, L0_attn_W_uv, L0_attn_W_dq, L0_attn_W_uq, L0_attn_W_qr, L0_attn_W_kr, L0_attn_W_out, L0_attn_idx_wq, L0_attn_idx_wk, L0_attn_idx_w, L0_attn_raw_delta, L0_ffn_w_router, L0_ffn_w_gate, L0_ffn_w_up, L0_ffn_w_down):
    import jax
    import jax.numpy as jnp

    def _L0_xattn_ref(values, keys, query, Wv, Wk, Wq, Wo, bo):
        import jax, jax.numpy as jnp
        import numpy as np
        EMBED = 128
        HEADS = 16
        HEAD_DIM = EMBED // HEADS
        N, Q, _ = query.shape
        v = (values @ Wv.T).reshape(N, -1, HEADS, HEAD_DIM)
        k = (keys @ Wk.T).reshape(N, -1, HEADS, HEAD_DIM)
        q = (query @ Wq.T).reshape(N, -1, HEADS, HEAD_DIM)
        energy = jnp.einsum('nqhd,nkhd->nhqk', q, k)
        attn = jax.nn.softmax(energy / HEAD_DIM ** 0.5, axis=-1)
        out = jnp.einsum('nhqk,nkhd->nqhd', attn, v).reshape(N, Q, EMBED)
        return out @ Wo.T + bo

    def _L0_attn_ref(x, W_dkv, W_uk, W_uv, W_dq, W_uq, W_qr, W_kr, W_out, idx_wq, idx_wk, idx_w, raw_delta):
        import jax, jax.numpy as jnp
        import numpy as np
        B, L = (2, 128)
        D_MODEL, D_CKV, D_CQ = (128, 32, 64)
        N_HEAD, D_HEAD, D_ROPE = (8, 64, 32)
        N_IDX_HEAD = 4
        K_TS, LW = (96, 64)
        ROPE_BASE = 10000.0

        def _pope(x, angles):
            cos, sin = (jnp.cos(angles), jnp.sin(angles))
            mu1, mu2 = jnp.split(jax.nn.softplus(x), 2, axis=-1)
            return jnp.concatenate([mu1 * cos - mu2 * sin, mu1 * sin + mu2 * cos], axis=-1)

        def _forward(x, W_dkv, W_uk, W_uv, W_dq, W_uq, W_qr, W_kr, W_out, idx_wq, idx_wk, idx_w, raw_delta):
            B_, L_, _ = x.shape
            c_kv = x @ W_dkv
            q_i = (x @ idx_wq).reshape(B_, L_, N_IDX_HEAD, D_HEAD)
            k_i = x @ idx_wk
            s_i = jax.nn.relu(jnp.einsum('bthd,bsd->bths', q_i, k_i))
            I = jnp.einsum('bths,h->bts', s_i, idx_w)
            qpos = jnp.arange(L_)[:, None]
            kpos = jnp.arange(L_)[None, :]
            local = (kpos >= qpos - LW + 1) & (kpos <= qpos)
            causal = kpos > qpos
            I = jnp.where(local[None], jnp.inf, I)
            I = jnp.where(causal[None], -jnp.inf, I)
            kk = min(K_TS, L_)
            _, idx = jax.lax.top_k(I, kk)
            bi = jnp.arange(B_)[:, None, None]
            key_c = (c_kv @ W_uk)[bi, idx].reshape(B_, L_, kk, N_HEAD, D_HEAD)
            value = (c_kv @ W_uv)[bi, idx].reshape(B_, L_, kk, N_HEAD, D_HEAD)
            c_q = x @ W_dq
            query_c = (c_q @ W_uq).reshape(B_, L_, N_HEAD, D_HEAD)
            half = D_ROPE // 2
            theta = 1.0 / ROPE_BASE ** (2.0 * jnp.arange(half, dtype=jnp.float32) / D_ROPE)
            delta = -2.0 * jnp.pi * jax.nn.sigmoid(raw_delta)
            angles_q = jnp.arange(L_, dtype=jnp.float32)[:, None] * theta[None, :] + delta
            query_r = _pope((c_q @ W_qr).reshape(B_, L_, N_HEAD, D_ROPE), angles_q[None, :, None, :])
            kr_sel = (x @ W_kr)[bi, idx]
            angles_k = jnp.arange(kk, dtype=jnp.float32)[:, None] * theta[None, :] + delta
            key_r = _pope(kr_sel, angles_k[None, None, :, :])
            scale = (D_HEAD + D_ROPE) ** (-0.5)
            q_c = query_c.transpose(0, 2, 1, 3)
            q_r = query_r.transpose(0, 2, 1, 3)
            k_c = key_c.transpose(0, 3, 1, 2, 4)
            v = value.transpose(0, 3, 1, 2, 4)
            scores = (jnp.einsum('bhld,bhlkd->bhlk', q_c, k_c) + jnp.einsum('bhld,blkd->bhlk', q_r, key_r)) * scale
            attn = jax.nn.softmax(scores.astype(jnp.float32), axis=-1).astype(v.dtype)
            out = jnp.einsum('bhlk,bhlkd->bhld', attn, v)
            out = out.transpose(0, 2, 1, 3).reshape(B_, L_, N_HEAD * D_HEAD)
            return out @ W_out
        return _forward(x, W_dkv, W_uk, W_uv, W_dq, W_uq, W_qr, W_kr, W_out, idx_wq, idx_wk, idx_w, raw_delta)

    def _L0_ffn_ref(x, w_router, w_gate, w_up, w_down):
        import jax, jax.numpy as jnp
        import numpy as np
        TOP_K = 2
        B, S, H = x.shape
        E = w_router.shape[0]
        xf = x.reshape(-1, H)
        logits = jnp.einsum('th,eh->te', xf, w_router)
        probs = jax.nn.softmax(logits, axis=-1)
        topw, topi = jax.lax.top_k(probs, TOP_K)
        topw = topw / jnp.sum(topw, axis=-1, keepdims=True)
        onehot = (topi[..., None] == jnp.arange(E)).astype(x.dtype)
        combine = jnp.einsum('tk,tke->te', topw, onehot)
        gate = jax.nn.silu(jnp.einsum('th,eih->eti', xf, w_gate))
        up = jnp.einsum('th,eih->eti', xf, w_up)
        down = jnp.einsum('eti,ehi->eth', gate * up, w_down)
        out = jnp.einsum('eth,te->th', down, combine)
        return out.reshape(B, S, H)
    x = x + _L0_xattn_ref(ctx_1024, ctx_1024, _layernorm(x, axis=-1), L0_xattn_Wv, L0_xattn_Wk, L0_xattn_Wq, L0_xattn_Wo, L0_xattn_bo)
    x = x + _L0_attn_ref(_layernorm(x, axis=-1), L0_attn_W_dkv, L0_attn_W_uk, L0_attn_W_uv, L0_attn_W_dq, L0_attn_W_uq, L0_attn_W_qr, L0_attn_W_kr, L0_attn_W_out, L0_attn_idx_wq, L0_attn_idx_wk, L0_attn_idx_w, L0_attn_raw_delta)
    x = x + _L0_ffn_ref(_layernorm(x, axis=-1), L0_ffn_w_router, L0_ffn_w_gate, L0_ffn_w_up, L0_ffn_w_down)
    return x

_drawn_inputs = setup_inputs


def setup_inputs(seed=0):
    import zlib

    import numpy as np

    out = dict(_drawn_inputs(seed))
    spreads = {'L0_xattn_bo': (0.0, 0.1), 'L0_attn_idx_w': (1.0, 0.2)}
    factors = {}
    for name, (base, spread) in spreads.items():
        noise = np.random.default_rng([zlib.crc32(name.encode()), seed]).standard_normal(out[name].shape)
        drawn = base * np.exp(spread * noise) if base else spread * noise
        out[name] = jnp.asarray(drawn.astype(out[name].dtype))
    for name, factor in factors.items():
        out[name] = (out[name] * factor).astype(out[name].dtype)
    return out
```

```python
import concourse.bass as bass
from concourse import mybir
from contextlib import ExitStack
import math

F32 = mybir.dt.float32
F32R = mybir.dt.float32r
ALU = mybir.AluOpType
ACT = mybir.ActivationFunctionType
AX = mybir.AxisListType

B, L, D = 64, 32, 128
S = 257
SP = 258
KC = SP // 3
XH, XD = 16, 8
G = 4
T = B * L // 128
NH, DH, DR = 8, 64, 32
CKV, CQ = 32, 64
E, I = 8, 352
CH = [(0, 128), (128, 128), (256, 96)]
NC = len(CH)
TB = 4
EPS = 1e-5
BIG = 3.0e38


def bc(ap, shape):
    return ap.broadcast_to(shape)


def f(ap):
    return ap.bitcast(F32)


def counts(value):
    return not isinstance(value, int) or value > 0


def build(nc, x, ctxT, wq, wk, wv, wo, bo, w_dq, w_kv, w_uqT, w_ukT, w_uvT, w_qr, w_out, raw_delta,
          w_router, w_gate, w_up, w_down, ident, head_mask, cos_pos, sin_pos, expert_rank, expert_sel, out):
    held = ExitStack()
    with held:
        def sb(name, shape, dt=F32, stack=held):
            return stack.enter_context(nc.sbuf_tensor(name, shape, dt))

        def sem(name):
            return held.enter_context(nc.semaphore(name))

        X = sb("X", [128, T, D])
        I128 = sb("I128", [128, 128])
        mean = sb("mean", [128, T])
        var = sb("var", [128, T])
        rstd = sb("rstd", [128, T])
        std = sb("std", [128, T])
        WkvS = sb("WkvS", [128, CKV + DR])
        WdqS = sb("WdqS", [128, CQ])
        WA = sb("WA", [CQ, NH, 2, 32])
        Wvo = sb("Wvo", [128, 2, D])
        cosT = sb("cosT", [128, 16])
        sinT = sb("sinT", [128, 16])
        wrT = sb("wrT", [128, E])
        rank = sb("rank", [128, E])
        SELr = sb("SELr", [2 * E, E, 128], F32R)
        GW = sb("GW", [128, E, I])
        UW = sb("UW", [128, E, I])
        DW = sb("DW", [128, E * NC, D])
        GH, GL = sb("GH", [128, E, I], F32R), sb("GL", [128, E, I], F32R)
        UH, UL = sb("UH", [128, E, I], F32R), sb("UL", [128, E, I], F32R)
        WH, WL = sb("WH", [128, E * NC, D], F32R), sb("WL", [128, E * NC, D], F32R)

        first = ExitStack()
        XL = sb("XL", [128, T, D], F32, first)
        XLT = sb("XLT", [128, T * 128], F32, first)
        SQ = XLT[:, 0:512].rearrange("p (t d) -> p t d", t=4)
        QH = sb("QH", [128, T * 128], F32R, first)
        QL = sb("QL", [128, T * 128], F32R, first)
        CR = sb("CR", [128, 4, S], F32, first)
        CHi = sb("CHi", [128, 4, SP], F32R, first)
        CLo = sb("CLo", [128, 4, SP], F32R, first)
        KH = sb("KH", [128, 2, SP], F32R, first)
        KL = sb("KL", [128, 2, SP], F32R, first)
        V = sb("V", [KC, 4, 3, D], F32, first)
        QMH = sb("QMH", [128, 4, G, L], F32R, first)
        QML = sb("QML", [128, 4, G, L], F32R, first)
        PR = sb("PR", [128, 2, G, SP], F32, first)
        PT = sb("PT", [KC, 3, 512], F32, first)
        nmax = sb("nmax", [128, G], F32, first)
        rsum = sb("rsum", [128, G], F32, first)
        rinv = sb("rinv", [128, G], F32, first)
        OM = sb("OM", [128, G, L], F32, first)
        OT = sb("OT", [128, 128], F32, first)
        WqS, WkS, WvS, WoS = (sb(n, [128, 128], F32, first) for n in ("WqS", "WkS", "WvS", "WoS"))
        WkH, WkL = sb("WkH", [128, 128], F32R, first), sb("WkL", [128, 128], F32R, first)
        WvH, WvL = sb("WvH", [128, 128], F32R, first), sb("WvL", [128, 128], F32R, first)
        boB = sb("boB", [128, D], F32, first)
        HM = sb("HM", [128, G], F32, first)
        small = sb("small", [128, 6, 16], F32, first)
        cpos, spos = sb("cpos", [128, 16], F32, first), sb("spos", [128, 16], F32, first)
        uqT = sb("uqT", [DH, NH, CQ], F32, first)
        ukT = sb("ukT", [DH, NH, CKV], F32, first)
        uvT = sb("uvT", [DH, NH, CKV], F32, first)
        woutS = PT[0:DH, 0:2, :].rearrange("p a n -> p (a n)").rearrange("p (h d) -> p h d", h=NH)
        SEL = sb("SEL", [2 * E, E, 128], F32, first)
        first.close()

        SQ2 = sb("SQ2", [128, 4, D])
        OUT = sb("OUT", [128, 4, D])
        second = ExitStack()
        xl = sb("xl", [128, 2, 128], F32, second)
        xlT = sb("xlT", [128, 2, 128], F32, second)
        cqT = sb("cqT", [CQ, 2, 128], F32, second)
        RR = sb("RR", [128, 2, 9, 32], F32, second)
        AB = sb("AB", [128, 2, 9, 32], F32, second)
        EX = sb("EX", [128, 2, 9, 32], F32, second)
        LG = sb("LG", [128, 2, 9, 32], F32, second)
        SPL = sb("SPL", [128, 2, 9, 2, 16], F32, second)
        MC = sb("MC", [128, 2, 9, 2, 16], F32, second)
        MS = sb("MS", [128, 2, 9, 2, 16], F32, second)
        TT = sb("TT", [128, 2, 10, 2, 32], F32, second)
        XT = sb("XT", [128, 2, 5, 128], F32, second)
        SS = sb("SS", [128, 2, 8, 32], F32, second)
        SD = sb("SD", [128, 2, 8, 32], F32, second)
        SE = sb("SE", [128, 2, 8, 32], F32, second)
        SN = sb("SN", [128, 2, 8, 32], F32, second)
        PTb = sb("PTb", [128, 2, 8, 32], F32, second)
        nm8 = sb("nm8", [128, 2, 8], F32, second)
        s8 = sb("s8", [128, 2, 8], F32, second)
        r8 = sb("r8", [128, 2, 8], F32, second)
        OS = sb("OS", [128, 2, 2, 128], F32, second)
        second.close()
        xe = sb("xe", [128, 4, 128])
        xeT = sb("xeT", [128, 512])
        xeH, xeL = sb("xeH", [128, 512], F32R), sb("xeL", [128, 512], F32R)
        tk = sb("tk", [128, 12, 4, E])
        tm = sb("tm", [128, 8, 4])
        cHi = sb("cHi", [128, 4, E], F32R)
        comb = sb("comb", [128, 4, 2 * E])
        CT = sb("CT", [2 * E, 512], F32R)
        CB = sb("CB", [128, 2, 512])
        sg = sb("sg", [128, 2, 512])
        hu = sb("hu", [128, 2, 512])
        hc = sb("hc", [128, 2, 512])
        hH, hL = sb("hH", [128, 4, 512], F32R), sb("hL", [128, 4, 512], F32R)
        YS = sb("YS", [128, 512])

        PS = held.enter_context(nc.psum_tensor("PS", [128, 8, 512], F32))
        bank = [PS[:, i, :] for i in range(8)]

        in_x, in_ident, in_sa, in_wqk, in_attn, in_moe, in_rot = (sem("in_" + n) for n in ("x", "ident", "sa", "wqk", "attn", "moe", "rot"))
        in_ctx = [sem(f"in_ctx{j}") for j in range(4)]
        ln_step, std_ready, ln_out = sem("ln_step"), sem("std_ready"), sem("ln_out")
        sq_ready = sem("sq_ready")
        ln_turned, ln_copied = sem("ln_turned"), sem("ln_copied")
        q_ready, q_scaled, q_hi, q_lo = sem("q_ready"), sem("q_scaled"), sem("q_hi"), sem("q_lo")
        w_split, pad_set = sem("w_split"), sem("pad_set")
        x_biased = sem("x_biased")
        rot_step, rot_act = sem("rot_step"), sem("rot_act")
        absorbed, absorbed_out = sem("absorbed"), sem("absorbed_out")
        sel_ready, wqr_in = sem("sel_ready"), sem("wqr_in")
        ctx_hi, ctx_lo, qm_hi, qm_lo = sem("ctx_hi"), sem("ctx_lo"), sem("qm_hi"), sem("qm_lo")
        k_proj, v_proj, k_hi, k_lo, v_copied = sem("k_proj"), sem("v_proj"), sem("k_hi"), sem("k_lo"), sem("v_copied")
        scores, max_ready, exped, sums_inv, normed = sem("scores"), sem("max_ready"), sem("exped"), sem("sums_inv"), sem("normed")
        p_turned, pt_act, pt_dve = sem("p_turned"), sem("pt_act"), sem("pt_dve")
        pv_done, o_masked, o_summed, wo_done, x1_ready = sem("pv_done"), sem("o_masked"), sem("o_summed"), sem("wo_done"), sem("x1_ready")

        b = {n: sem("b_" + n) for n in (
            "xl", "turned", "xlT", "cqT", "kv", "q", "rr", "abs", "exp", "ln", "copied", "sp", "mc", "ms",
            "rot", "dup", "T", "xt_a", "xt_v", "s", "ss", "max", "sub", "se", "sum", "inv", "norm", "pt", "pv",
            "os", "o", "x2", "pe_ready", "kr")}
        c = {n: sem("c_" + n) for n in (
            "xe", "turned", "xeT", "xeH", "xeL", "logits", "tk", "e2", "comb", "combT", "ct", "cbm", "cb",
            "gate", "up", "silu", "hu", "hc", "hH", "hL", "down", "ys", "yT", "out", "w_hi", "w_lo")}
        stored, out_free = sem("stored"), sem("out_free")

        def ln_stats_vector(v, t0, dst, n0, m0):
            s = slice(t0, t0 + 4)
            v.tensor_reduce(var[:, s], X[:, s, :], AX.X, ALU.add).then_inc(ln_step, 1)
            v.wait_ge(ln_step, n0 + 1)
            v.tensor_scalar(mean[:, s], var[:, s], 1.0 / D, None, ALU.mult).then_inc(ln_step, 1)
            v.wait_ge(ln_step, n0 + 2)
            v.tensor_tensor(dst, X[:, s, :], bc(mean[:, s].unsqueeze(2), [128, 4, D]), ALU.subtract).then_inc(ln_step, 1)
            v.wait_ge(sq_ready, m0 + 1)
            v.tensor_reduce(var[:, s], (SQ if m0 < 4 else SQ2[:, :, :]), AX.X, ALU.add).then_inc(ln_step, 1)

        def ln_squares_scalar(a, src, sq, n0, m0):
            a.wait_ge(ln_step, n0 + 3)
            a.activation(sq, src, ACT.Square).then_inc(sq_ready, 1)

        def XC2(n):
            return OUT[:, :, :]

        block = held.enter_context(nc.Block())

        @block.sync
        def _(sp):
            sp.dma_start(X[:, :, :], x.rearrange("(t p) d -> p t d", p=128)).then_inc(in_x, 16)
            sp.dma_start(I128[:, :], ident).then_inc(in_ident, 16)
            for dst, src in ((WqS, wq), (WkS, wk), (WvS, wv), (WoS, wo), (HM, head_mask)):
                sp.dma_start(dst[:, :], src).then_inc(in_wqk, 16)
            sp.dma_start(boB[:, :], bc(bo.unsqueeze(0), [128, D])).then_inc(in_wqk, 16)

            def load_ctx(k, j):
                if not isinstance(k, int) or k >= 4:
                    sp.wait_ge(ctx_lo, k - 3)
                sp.dma_start(CR[:, j, :], ctxT[:, bass.ds(k * S, S)]).then_inc(in_ctx[j], 16)

            for j in range(4):
                load_ctx(j, j)
            for dst, src in ((cpos, cos_pos), (spos, sin_pos)):
                sp.dma_start(dst[:, :], src).then_inc(in_rot, 16)
            sp.dma_start(small[:, 0, :], bc(raw_delta.unsqueeze(0), [128, 16])).then_inc(in_rot, 16)
            for dst, src in ((uqT[:, :, :], w_uqT), (ukT[:, :, :], w_ukT), (uvT[:, :, :], w_uvT), (woutS, w_out)):
                sp.dma_start(dst, src).then_inc(in_attn, 16)
            sp.dma_start(WA[:, :, 1, :], w_qr).then_inc(wqr_in, 16)
            sp.dma_start(WkvS[:, :], w_kv).then_inc(in_attn, 16)
            sp.dma_start(WdqS[:, :], w_dq).then_inc(in_attn, 16)
            sp.dma_start(SEL[:, :, :], expert_sel).then_inc(in_attn, 16)
            for j in range(4):
                load_ctx(4 + j, j)
            sp.dma_start(GW[:, :, :], w_gate).then_inc(in_moe, 16)
            sp.dma_start(UW[:, :, :], w_up).then_inc(in_moe, 16)
            for n, (c0, m) in enumerate(CH):
                sp.dma_start(DW[0:m, n::NC, :], w_down[c0:c0 + m, :, :]).then_inc(in_moe, 16)
            sp.dma_start(wrT[:, :], w_router).then_inc(in_moe, 16)
            sp.dma_start(rank[:, :], expert_rank).then_inc(in_moe, 16)
            with sp.Fori(2, T) as i:
                for j in range(4):
                    load_ctx(4 * i + j, j)
            sp.sem_inc(out_free, 1)
            with sp.Fori(0, TB) as tb:
                sp.wait_ge(c["out"], 4 * tb + 4)
                sp.dma_start(out[bass.ds(tb * 512, 512), :].rearrange("(t p) d -> p t d", p=128), OUT[:, :, :]).then_inc(stored, 16)
                sp.wait_ge(stored, 16 * tb + 16)
                sp.sem_inc(out_free, 1)

        @block.gpsimd
        def _(g):
            g.memset(f(CHi[:, :, S:SP]), 0.0).then_inc(pad_set, 1)
            g.memset(f(CLo[:, :, S:SP]), 0.0).then_inc(pad_set, 1)
            g.memset(PR[:, :, :, S:SP], 0.0).then_inc(pad_set, 1)

            def prepare(i, j):
                k = 4 * i + j
                if isinstance(i, int) and k == 0:
                    g.wait_ge(q_lo, 4)
                g.wait_ge(in_ctx[j], 16 * i + 16)
                if counts(k - 3):
                    g.wait_ge(v_proj, k - 3)
                if counts(4 * k - 12):
                    g.wait_ge(scores, 4 * k - 12)
                mask = bc(HM[:, :].unsqueeze(2), [128, G, L])
                g.tensor_tensor(QMH[:, j, :, :], bc(f(QH[:, bass.ds(k * L, L)]).unsqueeze(1), [128, G, L]), mask,
                                ALU.mult).then_inc(qm_hi, 1)
                g.tensor_tensor(QML[:, j, :, :], bc(f(QL[:, bass.ds(k * L, L)]).unsqueeze(1), [128, G, L]), mask,
                                ALU.mult).then_inc(qm_lo, 1)
                g.tensor_copy(CHi[:, j, 0:S], CR[:, j, :]).then_inc(ctx_hi, 1)
                g.wait_ge(ctx_hi, k + 1)
                g.tensor_tensor(CLo[:, j, 0:S], CR[:, j, :], f(CHi[:, j, 0:S]), ALU.subtract).then_inc(ctx_lo, 1)

            g.wait_ge(in_wqk, 96)
            for j in range(4):
                prepare(0, j)
            with g.Fori(1, T) as i:
                for j in range(4):
                    prepare(i, j)

            g.wait_ge(c["w_hi"], 3)
            g.tensor_tensor(GL[:, :, :], GW[:, :, :], f(GH[:, :, :]), ALU.subtract).then_inc(c["w_lo"], 1)
            g.tensor_tensor(UL[:, :, :], UW[:, :, :], f(UH[:, :, :]), ALU.subtract).then_inc(c["w_lo"], 1)
            for n, (c0, m) in enumerate(CH):
                g.tensor_tensor(WL[0:m, n::NC, :], DW[0:m, n::NC, :], f(WH[0:m, n::NC, :]), ALU.subtract).then_inc(c["w_lo"], 1)

            with g.Fori(0, TB) as tb:
                for n in range(E * NC):
                    e, m = n // NC, CH[n % NC][1]
                    at = E * NC * tb + n
                    g.wait_ge(c["cb"], E * tb + e + 1)
                    g.wait_ge(c["hu"], at + 1)
                    if n >= 2:
                        g.wait_ge(c["hL"], at - 1)
                    g.tensor_tensor(hc[0:m, n % 2, :], hu[0:m, n % 2, :], CB[0:m, e % 2, :], ALU.mult).then_inc(c["hc"], 1)

        @block.scalar
        def _(a):
            a.wait_ge(in_x, 16)
            for n in range(4):
                ln_squares_scalar(a, XL[:, 4 * n:4 * n + 4, :], SQ, 4 * n, n)
            a.wait_ge(ln_step, 17)
            a.activation(std[:, :], var[:, :], ACT.Sqrt).then_inc(std_ready, 1)
            a.wait_ge(in_rot, 48)
            a.activation(small[:, 1, :], small[:, 0, :], ACT.Exp, scale=-1.0).then_inc(rot_act, 1)
            for n in range(4):
                a.wait_ge(ln_turned, n + 1)
                a.activation(XLT[:, 512 * n:512 * n + 512], bank[n][:, :], ACT.Copy).then_inc(ln_copied, 1)
            for n in range(4):
                a.wait_ge(q_ready, n + 1)
                a.activation(XL[:, 4 * n:4 * n + 4, :].rearrange("p t d -> p (t d)"), bank[4 + n][:, :], ACT.Copy,
                             scale=XD ** -0.5).then_inc(q_scaled, 1)

            a.wait_ge(rot_step, 5)
            a.activation(small[:, 3, :], small[:, 2, :], ACT.Sin).then_inc(rot_act, 1)
            a.activation(small[:, 5, :], small[:, 4, :], ACT.Sin).then_inc(rot_act, 1)

            def k_high(k, j):
                a.wait_ge(k_proj, k + 1)
                if counts(4 * k - 4):
                    a.wait_ge(scores, 4 * k - 4)
                a.activation(KH[:, j % 2, :], bank[7][:, 0:SP], ACT.Copy).then_inc(k_hi, 1)

            def v_copy(k, j):
                a.wait_ge(v_proj, k + 1)
                if counts(k - 3):
                    a.wait_ge(pv_done, k - 3)
                a.activation(V[:, j, :, :], PS[0:KC, 0:3, 384:512], ACT.Copy).then_inc(v_copied, 1)

            def exps(k, j):
                if counts(3 * k - 3):
                    a.wait_ge(p_turned, 3 * k - 3)
                if counts(4 * k - 4):
                    a.wait_ge(normed, 4 * k - 4)
                for gr in range(G):
                    a.wait_ge(max_ready, 4 * k + gr + 1)
                    if gr == 0:
                        if counts(k):
                            a.wait_ge(sums_inv, k)
                    a.activation(PR[:, j % 2, gr, 0:S], bank[gr][:, 0:S], ACT.Exp, bias=nmax[:, gr:gr + 1],
                                 accum_out=rsum[:, gr:gr + 1]).then_inc(exped, 1)

            def turned_copy(k, ch):
                a.wait_ge(p_turned, 3 * k + ch + 1)
                if counts(k):
                    a.wait_ge(pv_done, k)
                a.activation(PT[:, ch, :], bank[4 + ch][0:KC, :], ACT.Copy).then_inc(pt_act, 1)

            def step(k, j, last=False):
                if not last or k + 2 < B:
                    k_high(k + 2, j + 2)
                if not isinstance(k, int) or k >= 1:
                    turned_copy(k - 1, 2)
                if not last or k + 1 < B:
                    exps(k + 1, j + 1)
                turned_copy(k, 0)
                if not last or k + 2 < B:
                    v_copy(k + 2, (j + 2) % 4)

            for k in range(2):
                k_high(k, k)
                v_copy(k, k)
            exps(0, 0)
            for k in range(4):
                step(k, k)
            with a.Fori(1, T - 1) as i:
                for j in range(4):
                    step(4 * i + j, j)
            for k in range(B - 4, B):
                step(k, k % 4, True)
            turned_copy(B - 1, 2)

            a.wait_ge(in_moe, 16 * 7)
            a.activation(GH[:, :, :], GW[:, :, :], ACT.Copy).then_inc(c["w_hi"], 1)
            a.activation(UH[:, :, :], UW[:, :, :], ACT.Copy).then_inc(c["w_hi"], 1)
            for n, (c0, m) in enumerate(CH):
                ins = a.activation(WH[0:m, n::NC, :], DW[0:m, n::NC, :], ACT.Copy)
            ins.then_inc(c["w_hi"], 1)

            for n in range(4):
                ln_squares_scalar(a, XC2(n), SQ2[:, :, :], 17 + 4 * n, 4 + n)
            a.wait_ge(ln_step, 34)
            a.activation(std[:, :], var[:, :], ACT.Sqrt).then_inc(std_ready, 1)
            with a.Fori(0, T // 2) as i:
                for s in range(2):
                    w = 2 * i + s + 1
                    a.wait_ge(b["turned"], w)
                    a.activation(xlT[:, s, :], bank[4 * s][:, 0:128], ACT.Copy).then_inc(b["xlT"], 1)
                for s in range(2):
                    w = 2 * i + s + 1
                    q = bank[4 * s + 1][:, :].rearrange("p (h c d) -> p h c d", c=2, d=32)
                    a.wait_ge(b["q"], w)
                    a.activation(RR[:, s, 0:8, :], q[:, :, 1, :], ACT.Copy).then_inc(b["rr"], 1)
                    a.activation(TT[:, s, 0:8, 0, :], q[:, :, 0, :], ACT.Copy).then_inc(b["copied"], 1)
                for s in range(2):
                    w = 2 * i + s + 1
                    a.wait_ge(b["rr"], w)
                    a.wait_ge(b["kr"], w)
                    a.activation(AB[:, s, :, :], RR[:, s, :, :], ACT.Abs).then_inc(b["abs"], 1)
                    a.wait_ge(b["abs"], w)
                    a.activation(EX[:, s, :, :], AB[:, s, :, :], ACT.Exp, scale=-1.0).then_inc(b["exp"], 1)
                for s in range(2):
                    w = 2 * i + s + 1
                    a.wait_ge(b["exp"], w)
                    a.activation(LG[:, s, :, :], EX[:, s, :, :], ACT.Ln, bias=1.0).then_inc(b["ln"], 1)
                for s in range(2):
                    w = 2 * i + s + 1
                    a.wait_ge(b["T"], w)
                    a.activation(XT[:, s, 0:4, :].rearrange("p a n -> p (a n)"), bank[4 * s + 2][:, :], ACT.Copy).then_inc(b["xt_a"], 1)
                for s in range(2):
                    w = 2 * i + s + 1
                    a.wait_ge(b["sub"], w)
                    a.activation(SE[:, s, :, :], SD[:, s, :, :], ACT.Exp, scale=(DH + DR) ** -0.5).then_inc(b["se"], 1)
                for s in range(2):
                    w = 2 * i + s + 1
                    a.wait_ge(b["pv"], w)
                    a.activation(OS[:, s, :, :].rearrange("p r (j q) -> p j r q", j=4),
                                 PS[:, 4 * s:4 * s + 4, 0:64].rearrange("p j (r q) -> p j r q", r=2), ACT.Copy).then_inc(b["os"], 1)

            for n in range(4):
                ln_squares_scalar(a, XC2(n), SQ2[:, :, :], 34 + 4 * n, 8 + n)
            a.wait_ge(ln_step, 51)
            a.activation(std[:, :], var[:, :], ACT.Sqrt).then_inc(std_ready, 1)
            with a.Fori(0, TB) as tb:
                a.wait_ge(c["turned"], tb + 1)
                a.activation(xeT[:, :], bank[0][:, :], ACT.Copy).then_inc(c["xeT"], 1)
                a.activation(xeH[:, :], bank[0][:, :], ACT.Copy).then_inc(c["xeH"], 1)
                a.wait_ge(c["tk"], 12 * tb + 11)
                a.activation(tm[:, 5, :], tm[:, 4, :], ACT.Exp).then_inc(c["e2"], 1)
                a.wait_ge(c["combT"], tb + 1)
                a.activation(CT[:, :], bank[3][0:2 * E, :], ACT.Copy).then_inc(c["ct"], 1)
                for n in range(E * NC + 2):
                    at = E * NC * tb + n
                    if n < E * NC:
                        e, m = n // NC, CH[n % NC][1]
                        if n % NC == 0:
                            a.wait_ge(c["cbm"], E * tb + e + 1)
                            if e >= 2:
                                a.wait_ge(c["hc"], at - NC)
                            a.activation(CB[:, e % 2, :], bank[7][:, :], ACT.Copy).then_inc(c["cb"], 1)
                        a.wait_ge(c["gate"], at + 1)
                        if n >= 2:
                            a.wait_ge(c["hu"], at - 1)
                        a.activation(sg[0:m, n % 2, :], bank[n % 2][0:m, :], ACT.Silu).then_inc(c["silu"], 1)
                    if n >= 2:
                        m = CH[(n - 2) % NC][1]
                        a.wait_ge(c["hc"], at - 1)
                        if n - 2 >= 4:
                            a.wait_ge(c["down"], at - 5)
                        a.activation(hH[0:m, (n - 2) % 4, :], hc[0:m, n % 2, :], ACT.Copy).then_inc(c["hH"], 1)
                a.wait_ge(c["down"], E * NC * tb + E * NC)
                a.activation(YS[:, :], bank[6][:, :], ACT.Copy).then_inc(c["ys"], 1)

        @block.vector
        def _(v):
            def finish_stats(n0, s0):
                v.wait_ge(ln_step, n0)
                v.tensor_scalar(var[:, :], var[:, :], 1.0 / D, EPS, ALU.mult, ALU.add).then_inc(ln_step, 1)
                v.wait_ge(std_ready, s0 + 1)
                v.reciprocal(rstd[:, :], std[:, :]).then_inc(std_ready, 1)
                v.wait_ge(std_ready, s0 + 2)

            v.wait_ge(in_x, 16)
            for n in range(4):
                ln_stats_vector(v, 4 * n, XL[:, 4 * n:4 * n + 4, :], 4 * n, n)
            finish_stats(16, 0)
            for n in range(4):
                s = slice(4 * n, 4 * n + 4)
                v.tensor_tensor(XL[:, s, :], XL[:, s, :], bc(rstd[:, s].unsqueeze(2), [128, 4, D]), ALU.mult).then_inc(ln_out, 1)
            v.wait_ge(in_wqk, 96)
            v.tensor_copy(WkH[:, :], WkS[:, :]).then_inc(w_split, 1)
            v.tensor_copy(WvH[:, :], WvS[:, :]).then_inc(w_split, 1)
            v.wait_ge(w_split, 2)
            v.tensor_tensor(WkL[:, :], WkS[:, :], f(WkH[:, :]), ALU.subtract).then_inc(w_split, 1)
            v.tensor_tensor(WvL[:, :], WvS[:, :], f(WvH[:, :]), ALU.subtract).then_inc(w_split, 1)
            for n in range(4):
                v.wait_ge(q_scaled, n + 1)
                qs = XL[:, 4 * n:4 * n + 4, :].rearrange("p t d -> p (t d)")
                v.tensor_copy(QH[:, 512 * n:512 * n + 512], qs).then_inc(q_hi, 1)
                v.wait_ge(q_hi, n + 1)
                v.tensor_tensor(QL[:, 512 * n:512 * n + 512], qs, f(QH[:, 512 * n:512 * n + 512]), ALU.subtract).then_inc(q_lo, 1)

            def k_low(k, j):
                v.wait_ge(k_hi, k + 1)
                v.tensor_tensor(KL[:, j % 2, :], bank[7][:, 0:SP], f(KH[:, j % 2, :]), ALU.subtract).then_inc(k_lo, 1)

            def maxima(k):
                if counts(4 * k):
                    v.wait_ge(exped, 4 * k)
                for gr in range(G):
                    v.wait_ge(scores, 4 * k + gr + 1)
                    v.tensor_reduce(nmax[:, gr:gr + 1], bank[gr][:, 0:S], AX.X, ALU.max, negate=True).then_inc(max_ready, 1)

            def normalise(k, j):
                v.wait_ge(exped, 4 * k + 4)
                if counts(4 * k):
                    v.wait_ge(normed, 4 * k)
                v.reciprocal(rinv[:, :], rsum[:, :]).then_inc(sums_inv, 1)
                v.wait_ge(sums_inv, k + 1)
                for gr in range(G):
                    v.tensor_scalar(PR[:, j % 2, gr, 0:S], PR[:, j % 2, gr, 0:S], rinv[:, gr:gr + 1], None,
                                    ALU.mult).then_inc(normed, 1)

            def turned_copy(k):
                v.wait_ge(p_turned, 3 * k + 2)
                if counts(k):
                    v.wait_ge(pv_done, k)
                v.tensor_copy(PT[:, 1, :], bank[5][0:KC, :]).then_inc(pt_dve, 1)

            def own_blocks(k, j, unit):
                v.wait_ge(pv_done, k + 1)
                if counts(k):
                    v.wait_ge(o_summed, k)
                o = bank[7][:, 384:512].rearrange("p (h q) -> p h q", h=G)
                v.tensor_tensor(OM[:, :, :], o, bc(HM[:, :].unsqueeze(2), [128, G, L]), ALU.mult).then_inc(o_masked, 1)
                v.wait_ge(o_masked, k + 1)
                if j == 0:
                    if counts(unit):
                        v.wait_ge(wo_done, unit)
                v.tensor_reduce(OT[:, L * j:L * j + L], OM[:, :, :].rearrange("p h q -> p q h"), AX.X, ALU.add).then_inc(o_summed, 1)

            def residual(unit):
                v.wait_ge(wo_done, unit + 1)
                xt = X[:, bass.ds(unit, 1), :].rearrange("p t d -> p (t d)")
                v.tensor_tensor(xt, bank[3][:, 384:512], xt, ALU.add).then_inc(x1_ready, 1)

            v.wait_ge(ln_step, 17)
            for n in range(4):
                s = slice(4 * n, 4 * n + 4)
                v.tensor_tensor(X[:, s, :], X[:, s, :], bc(boB[:, :].unsqueeze(1), [128, 4, D]), ALU.add).then_inc(x_biased, 1)
            v.wait_ge(rot_act, 1)
            sm = lambda n: small[:, n, :]
            v.tensor_scalar(sm(1), sm(1), 1.0, None, ALU.add).then_inc(rot_step, 1)
            v.wait_ge(rot_step, 1)
            v.reciprocal(sm(2), sm(1)).then_inc(rot_step, 1)
            v.wait_ge(rot_step, 2)
            v.tensor_scalar(sm(2), sm(2), -math.pi, math.pi / 2, ALU.mult, ALU.add).then_inc(rot_step, 1)
            v.wait_ge(rot_step, 3)
            v.scalar_tensor_tensor(out=sm(4), in0=sm(2), scalar=-1.0, in1=sm(2), op0=ALU.mult, op1=ALU.max).then_inc(rot_step, 1)
            v.wait_ge(rot_step, 4)
            v.tensor_scalar(sm(4), sm(4), -1.0, math.pi / 2, ALU.mult, ALU.add).then_inc(rot_step, 1)
            v.wait_ge(rot_act, 3)
            v.scalar_tensor_tensor(out=sm(1), in0=sm(3), scalar=-2.0, in1=sm(5), op0=ALU.mult, op1=ALU.mult).then_inc(rot_step, 1)
            v.scalar_tensor_tensor(out=sm(2), in0=sm(3), scalar=2.0, in1=sm(3), op0=ALU.mult, op1=ALU.mult).then_inc(rot_step, 1)
            v.wait_ge(rot_step, 7)
            v.tensor_scalar(sm(2), sm(2), 1.0, None, ALU.subtract).then_inc(rot_step, 1)
            v.wait_ge(rot_step, 8)
            v.tensor_tensor(cosT[:, :], cpos[:, :], sm(2), ALU.mult).then_inc(rot_step, 1)
            v.tensor_tensor(sm(0), spos[:, :], sm(1), ALU.mult).then_inc(rot_step, 1)
            v.tensor_tensor(sinT[:, :], spos[:, :], sm(2), ALU.mult).then_inc(rot_step, 1)
            v.tensor_tensor(sm(3), cpos[:, :], sm(1), ALU.mult).then_inc(rot_step, 1)
            v.wait_ge(rot_step, 12)
            v.tensor_tensor(cosT[:, :], cosT[:, :], sm(0), ALU.subtract).then_inc(rot_step, 1)
            v.tensor_tensor(sinT[:, :], sinT[:, :], sm(3), ALU.add).then_inc(rot_step, 1)
            v.wait_ge(absorbed, 1)
            v.tensor_copy(WA[:, :, 0, :], bank[5][0:CQ, 0:NH * 32].rearrange("p (h d) -> p h d", h=NH)).then_inc(absorbed_out, 1)
            v.wait_ge(absorbed, 2)
            v.tensor_copy(Wvo[:, :, :].rearrange("p r n -> p (r n)"), bank[6][:, 0:256]).then_inc(absorbed_out, 1)
            v.wait_ge(in_attn, 16 * 7)
            v.tensor_copy(SELr[:, :, :], SEL[:, :, :]).then_inc(sel_ready, 1)

            def step(k, j, unit, last=False):
                if not last or k + 2 < B:
                    k_low(k + 2, j + 2)
                if not last or k + 1 < B:
                    maxima(k + 1)
                if not isinstance(k, int) or k >= 1:
                    own_blocks(k - 1, (j - 1) % 4, unit - (j == 0))
                if not last or k + 1 < B:
                    normalise(k + 1, j + 1)
                turned_copy(k)
                if j == 0 and (not isinstance(unit, int) or unit >= 1):
                    residual(unit - 1)

            k_low(0, 0)
            k_low(1, 1)
            maxima(0)
            normalise(0, 0)
            for k in range(4):
                step(k, k, 0)
            with v.Fori(1, T - 1) as i:
                for j in range(4):
                    step(4 * i + j, j, i)
            for k in range(B - 4, B):
                step(k, k % 4, T - 1, True)
            own_blocks(B - 1, 3, T - 1)
            residual(T - 1)

            v.wait_ge(x1_ready, T)
            for n in range(4):
                ln_stats_vector(v, 4 * n, XC2(n), 17 + 4 * n, 4 + n)
            finish_stats(33, 2)
            with v.Fori(0, T // 2) as i:
                def w(s):
                    return 2 * i + s + 1
                for s in range(2):
                    t = 2 * i + s
                    v.tensor_scalar(xl[:, s, :], X[:, bass.ds(t, 1), :].rearrange("p t d -> p (t d)"),
                                    mean[:, bass.ds(t, 1)], rstd[:, bass.ds(t, 1)], ALU.subtract, ALU.mult).then_inc(b["xl"], 1)
                for s in range(2):
                    v.wait_ge(b["kv"], w(s))
                    v.tensor_copy(cqT[:, s, :], bank[4 * s][0:CQ, 128:256]).then_inc(b["cqT"], 1)
                for s in range(2):
                    v.tensor_copy(RR[:, s, 8, :], bank[4 * s][:, 256 + CKV:256 + CKV + DR]).then_inc(b["kr"], 1)
                    v.tensor_copy(TT[:, s, 8:10, 0, :], bc(bank[4 * s][:, 256:256 + CKV].unsqueeze(1), [128, 2, 32])).then_inc(b["copied"], 1)
                for s in range(2):
                    v.wait_ge(b["ln"], w(s))
                    v.scalar_tensor_tensor(out=SPL[:, s, :, :, :].rearrange("p h a d -> p h (a d)"), in0=RR[:, s, :, :], scalar=0.0,
                                           in1=LG[:, s, :, :], op0=ALU.max, op1=ALU.add).then_inc(b["sp"], 1)
                    v.wait_ge(b["sp"], w(s))
                    full = [128, 9, 2, 16]
                    v.tensor_tensor(MC[:, s, :, :, :], SPL[:, s, :, :, :], bc(cosT[:, :].unsqueeze(1).unsqueeze(1), full), ALU.mult).then_inc(b["mc"], 1)
                    v.tensor_tensor(MS[:, s, :, :, :], SPL[:, s, :, :, :], bc(sinT[:, :].unsqueeze(1).unsqueeze(1), full), ALU.mult).then_inc(b["ms"], 1)
                    v.wait_ge(b["mc"], w(s))
                    v.wait_ge(b["ms"], w(s))
                    v.tensor_tensor(TT[:, s, 0:9, 1, 0:16], MC[:, s, :, 0, :], MS[:, s, :, 1, :], ALU.subtract).then_inc(b["rot"], 1)
                    v.tensor_tensor(TT[:, s, 0:9, 1, 16:32], MS[:, s, :, 0, :], MC[:, s, :, 1, :], ALU.add).then_inc(b["rot"], 1)
                    v.wait_ge(b["rot"], 4 * i + 2 * s + 2)
                    v.tensor_copy(TT[:, s, 9, 1, :], TT[:, s, 8, 1, :]).then_inc(b["dup"], 1)
                for s in range(2):
                    v.wait_ge(b["T"], w(s))
                    v.tensor_copy(XT[:, s, 4, :], bank[4 * s][:, 384:512]).then_inc(b["xt_v"], 1)
                for s in range(2):
                    v.wait_ge(b["s"], w(s))
                    for r in range(2):
                        v.transpose(SS[:, s, 4 * r:4 * r + 4, :].rearrange("p h k -> p (h k)"), bank[4 * s + 3 - 2 * r][:, 0:128]).then_inc(b["ss"], 1)
                    v.wait_ge(b["ss"], 4 * i + 2 * s + 2)
                    v.tensor_reduce(nm8[:, s, :], SS[:, s, :, :], AX.X, ALU.max).then_inc(b["max"], 1)
                    v.wait_ge(b["max"], w(s))
                    v.tensor_tensor(SD[:, s, :, :], SS[:, s, :, :], bc(nm8[:, s, :].unsqueeze(2), [128, 8, 32]), ALU.subtract).then_inc(b["sub"], 1)
                for s in range(2):
                    v.wait_ge(b["se"], w(s))
                    v.tensor_reduce(s8[:, s, :], SE[:, s, :, :], AX.X, ALU.add).then_inc(b["sum"], 1)
                    v.wait_ge(b["sum"], w(s))
                    v.reciprocal(r8[:, s, :], s8[:, s, :]).then_inc(b["inv"], 1)
                    v.wait_ge(b["inv"], w(s))
                    v.tensor_tensor(SN[:, s, :, :], SE[:, s, :, :], bc(r8[:, s, :].unsqueeze(2), [128, 8, 32]), ALU.mult).then_inc(b["norm"], 1)
                    v.wait_ge(b["norm"], w(s))
                    v.transpose(PTb[:, s, :, :].rearrange("p h k -> p (h k)"), SN[:, s, :, :].rearrange("p h k -> p (h k)")).then_inc(b["pt"], 1)
                for s in range(2):
                    v.wait_ge(b["o"], w(s))
                    xt = X[:, bass.ds(2 * i + s, 1), :].rearrange("p t d -> p (t d)")
                    v.tensor_tensor(xt, bank[4 * s][:, 0:128], xt, ALU.add).then_inc(b["x2"], 1)

            v.wait_ge(b["x2"], T)
            for n in range(4):
                ln_stats_vector(v, 4 * n, XC2(n), 34 + 4 * n, 8 + n)
            finish_stats(50, 4)
            with v.Fori(0, TB) as tb:
                for n in range(4):
                    t = 4 * tb + n
                    v.tensor_scalar(xe[:, n, :], X[:, bass.ds(t, 1), :].rearrange("p t d -> p (t d)"),
                                    mean[:, bass.ds(t, 1)], rstd[:, bass.ds(t, 1)], ALU.subtract, ALU.mult).then_inc(c["xe"], 1)
                v.wait_ge(c["xeH"], tb + 1)
                v.tensor_tensor(xeL[:, :], bank[0][:, :], f(xeH[:, :]), ALU.subtract).then_inc(c["xeL"], 1)
                n = [0]

                def did(ins):
                    n[0] += 1
                    ins.then_inc(c["tk"], 1)
                    return 12 * tb + n[0]

                def small_step(ins):
                    v.wait_ge(c["tk"], did(ins))

                lg = bank[2][:, 0:4 * E].rearrange("p (t e) -> p t e", t=4)
                rk = bc(rank[:, :].unsqueeze(1), [128, 4, E])
                wide = lambda ap: bc(ap.unsqueeze(2), [128, 4, E])
                K = lambda m: tk[:, m, :, :]
                v.wait_ge(c["logits"], tb + 1)
                small_step(v.tensor_reduce(tm[:, 0, :], lg, AX.X, ALU.max))
                small_step(v.tensor_tensor(K(0), lg, wide(tm[:, 0, :]), ALU.is_equal))
                small_step(v.tensor_tensor(K(1), K(0), rk, ALU.mult))
                small_step(v.tensor_reduce(tm[:, 1, :], K(1), AX.X, ALU.max))
                small_step(v.tensor_tensor(K(2), K(1), wide(tm[:, 1, :]), ALU.is_equal))
                small_step(v.scalar_tensor_tensor(out=K(3), in0=K(2), scalar=-BIG, in1=lg, op0=ALU.mult, op1=ALU.add))
                small_step(v.tensor_reduce(tm[:, 2, :], K(3), AX.X, ALU.max))
                small_step(v.tensor_tensor(K(4), K(3), wide(tm[:, 2, :]), ALU.is_equal))
                small_step(v.tensor_tensor(K(5), K(4), rk, ALU.mult))
                small_step(v.tensor_reduce(tm[:, 3, :], K(5), AX.X, ALU.max))
                did(v.tensor_tensor(tm[:, 4, :], tm[:, 2, :], tm[:, 0, :], ALU.subtract))
                small_step(v.tensor_tensor(K(6), K(5), wide(tm[:, 3, :]), ALU.is_equal))
                m = [0]

                def comb_step(ins):
                    m[0] += 1
                    ins.then_inc(c["comb"], 1)
                    v.wait_ge(c["comb"], 8 * tb + m[0])

                v.wait_ge(c["e2"], tb + 1)
                comb_step(v.tensor_scalar(tm[:, 6, :], tm[:, 5, :], 1.0, None, ALU.add))
                comb_step(v.reciprocal(tm[:, 7, :], tm[:, 6, :]))
                comb_step(v.tensor_tensor(tm[:, 6, :], tm[:, 5, :], tm[:, 7, :], ALU.mult))
                comb_step(v.tensor_tensor(K(7), K(2), wide(tm[:, 7, :]), ALU.mult))
                comb_step(v.tensor_tensor(K(8), K(6), wide(tm[:, 6, :]), ALU.mult))
                comb_step(v.tensor_tensor(K(9), K(7), K(8), ALU.add))
                comb_step(v.tensor_copy(cHi[:, :, :], K(9)))
                v.tensor_copy(comb[:, :, 0:E], f(cHi[:, :, :])).then_inc(c["xeL"], 1)
                comb_step(v.tensor_tensor(comb[:, :, E:2 * E], K(9), f(cHi[:, :, :]), ALU.subtract))
                for n in range(E * NC + 2):
                    at = E * NC * tb + n
                    if n < E * NC:
                        m = CH[n % NC][1]
                        v.wait_ge(c["silu"], at + 1)
                        v.wait_ge(c["up"], at + 1)
                        if n >= 2:
                            v.wait_ge(c["hc"], at - 1)
                        v.tensor_tensor(hu[0:m, n % 2, :], bank[2 + n % 2][0:m, :], sg[0:m, n % 2, :], ALU.mult).then_inc(c["hu"], 1)
                    if n >= 2:
                        m = CH[(n - 2) % NC][1]
                        v.wait_ge(c["hH"], at - 1)
                        v.tensor_tensor(hL[0:m, (n - 2) % 4, :], hc[0:m, n % 2, :], f(hH[0:m, (n - 2) % 4, :]), ALU.subtract).then_inc(c["hL"], 1)
                v.wait_ge(c["yT"], tb + 1)
                v.wait_ge(out_free, tb + 1)
                for n in range(4):
                    v.tensor_tensor(OUT[:, n, :], bank[5][:, 128 * n:128 * n + 128],
                                    X[:, bass.ds(4 * tb + n, 1), :].rearrange("p t d -> p (t d)"), ALU.add).then_inc(c["out"], 1)

        @block.tensor
        def _(t):
            t.wait_ge(in_ident, 16)
            for n in range(4):
                t.wait_ge(ln_out, n + 1)
                for m in range(4):
                    ins = t.transpose(bank[n][:, 128 * m:128 * m + 128], XL[:, 4 * n + m, :], I128[:, :])
                ins.then_inc(ln_turned, 1)
            t.wait_ge(in_wqk, 96)
            for n in range(4):
                t.wait_ge(ln_copied, n + 1)
                t.matmul(bank[4 + n][:, :], WqS[:, :], XLT[:, 512 * n:512 * n + 512], start=True, stop=True).then_inc(q_ready, 1)
            t.wait_ge(in_attn, 16 * 7)
            t.wait_ge(q_scaled, 4)
            for h in range(NH):
                ins = t.matmul(bank[5][0:CQ, 32 * h:32 * h + 32], uqT[:, h, :], ukT[:, h, :], start=True, stop=True)
            ins.then_inc(absorbed, 1)
            for h in range(NH):
                hp, r = h // 2, h % 2
                ins = t.matmul(bank[6][32 * hp:32 * hp + 32, 128 * r:128 * r + 128], uvT[:, h, :], woutS[:, h, :], start=True, stop=True)
            ins.then_inc(absorbed, 1)
            t.wait_ge(absorbed_out, 2)

            def project_keys(k, j):
                t.wait_ge(ctx_hi, k + 1)
                t.wait_ge(ctx_lo, k + 1)
                if counts(k):
                    t.wait_ge(k_lo, k)
                if counts(k - 3):
                    t.wait_ge(o_masked, k - 3)
                hi, lo = CHi[:, j, :], CLo[:, j, :]
                for n, (w, c_) in enumerate(((WkH, hi), (WkL, hi), (WkH, lo))):
                    ins = t.matmul(bank[7][:, 0:SP], w[:, :], c_, start=(n == 0), stop=(n == 2))
                ins.then_inc(k_proj, 1)

            def project_values(k, j, scored=True):
                hi, lo = CHi[:, j, :], CLo[:, j, :]
                if counts(k):
                    t.wait_ge(v_copied, k)
                for ch in range(3):
                    s = slice(KC * ch, KC * ch + KC)
                    if scored:
                        t.wait_ge(exped, 4 * k - 3 + ch)
                    for n, (w, c_) in enumerate(((WvH, hi), (WvL, hi), (WvH, lo))):
                        ins = t.matmul(bank[ch][0:KC, 384:512], c_[:, s], w[:, :], start=(n == 0), stop=(n == 2))
                ins.then_inc(v_proj, 1)

            def score(k, j, done=0):
                t.wait_ge(qm_hi, k + 1)
                t.wait_ge(qm_lo, k + 1)
                t.wait_ge(k_lo, k + 1)
                t.wait_ge(v_copied, 2 if isinstance(k, int) and k == 0 else k + 1)
                for gr in range(G):
                    rows = slice(32 * gr, 32 * gr + 32)
                    if counts(4 * k - 3 + gr):
                        t.wait_ge(exped, 4 * k - 3 + gr)
                    if gr == 3 and counts(done):
                        t.wait_ge(x1_ready, done)
                    qh, ql = (q[rows, j % 4, :, :].rearrange("p h q -> p (h q)") for q in (QMH, QML))
                    kh, kl = KH[rows, j % 2, :], KL[rows, j % 2, :]
                    for n, (q, kk) in enumerate(((qh, kh), (ql, kh), (qh, kl))):
                        ins = t.matmul(bank[gr][:, 0:SP], q, kk, start=(n == 0), stop=(n == 2))
                    ins.then_inc(scores, 1)

            def turn(k, j, ch):
                if ch == 1:
                    if counts(k):
                        t.wait_ge(pt_dve, k)
                else:
                    if counts(2 * k - 1 + ch // 2):
                        t.wait_ge(pt_act, 2 * k - 1 + ch // 2)
                for gr in range(G):
                    if ch == 0:
                        t.wait_ge(normed, 4 * k + gr + 1)
                    ins = t.transpose(bank[4 + ch][0:KC, 128 * gr:128 * gr + 128],
                                      PR[:, j % 2, gr, KC * ch:KC * ch + KC], I128[:, :])
                ins.then_inc(p_turned, 1)

            def weigh(k, j):
                t.wait_ge(k_lo, min(k + 4, B) if isinstance(k, int) else k + 4)
                if counts(k):
                    t.wait_ge(o_masked, k)
                for ch in range(3):
                    if ch == 1:
                        t.wait_ge(pt_dve, k + 1)
                    else:
                        t.wait_ge(pt_act, 2 * k + 1 + ch // 2)
                    for gr in range(G):
                        ins = t.matmul(bank[7][32 * gr:32 * gr + 32, 384:512], V[:, j, ch, 32 * gr:32 * gr + 32],
                                       PT[:, ch, 128 * gr:128 * gr + 128], start=(ch == 0), stop=(ch == 2))
                ins.then_inc(pv_done, 1)

            def project_out(unit):
                t.wait_ge(o_summed, 4 * unit + 4)
                t.wait_ge(exped, min(16 * unit + 24, 4 * B) if isinstance(unit, int) else 16 * unit + 24)
                t.matmul(bank[3][:, 384:512], OT[:, :], WoS[:, :], start=True, stop=True).then_inc(wo_done, 1)

            def step(k, j, unit, last=False):
                if not last or k + 2 < B:
                    project_keys(k + 2, (j + 2) % 4)
                if not last or k + 1 < B:
                    score(k + 1, j + 1, done=unit if j == 1 else 0)
                if not isinstance(k, int) or k >= 1:
                    weigh(k - 1, (j - 1) % 4)
                turn(k, j, 0)
                turn(k, j, 1)
                if not last or k + 2 < B:
                    project_values(k + 2, (j + 2) % 4)
                turn(k, j, 2)
                if j == 0 and (not isinstance(unit, int) or unit >= 1):
                    project_out(unit - 1)

            t.wait_ge(w_split, 4)
            t.wait_ge(pad_set, 3)
            for k in range(2):
                project_keys(k, k)
                project_values(k, k, False)
            score(0, 0)
            for k in range(4):
                step(k, k, 0)
            with t.Fori(1, T - 1) as i:
                for j in range(4):
                    step(4 * i + j, j, i)
            for k in range(B - 4, B):
                step(k, k % 4, T - 1, True)
            weigh(B - 1, 3)
            project_out(T - 1)

            t.wait_ge(wqr_in, 16)
            t.wait_ge(x1_ready, T)
            with t.Fori(0, T // 2) as i:
                def w(s):
                    return 2 * i + s + 1
                for s in range(2):
                    t.wait_ge(b["xl"], w(s))
                    t.transpose(bank[4 * s][:, 0:128], xl[:, s, :], I128[:, :]).then_inc(b["turned"], 1)
                for s in range(2):
                    t.wait_ge(b["xlT"], w(s))
                    t.matmul(bank[4 * s][0:CQ, 128:256], WdqS[:, :], xlT[:, s, :], start=True, stop=True)
                    t.matmul(bank[4 * s][:, 256:256 + CKV + DR], xlT[:, s, :], WkvS[:, :], start=True, stop=True).then_inc(b["kv"], 1)
                for s in range(2):
                    t.wait_ge(b["cqT"], w(s))
                    t.matmul(bank[4 * s + 1][:, :], cqT[:, s, :], WA[:, :, :, :].rearrange("p h c d -> p (h c d)"),
                             start=True, stop=True).then_inc(b["q"], 1)
                for s in range(2):
                    t.wait_ge(b["dup"], w(s))
                    t.wait_ge(b["copied"], 4 * i + 2 * s + 2)
                    for n in range(5):
                        src = TT[:, s, 2 * n:2 * n + 2, :, :].rearrange("p h c d -> p (h c d)")
                        dst = bank[4 * s + 2][:, 128 * n:128 * n + 128] if n < 4 else bank[4 * s][:, 384:512]
                        ins = t.transpose(dst, src, I128[:, :])
                    ins.then_inc(b["T"], 1)
                for s in range(2):
                    t.wait_ge(b["xt_a"], w(s))
                    t.wait_ge(b["xt_v"], w(s))
                    t.sem_inc(b["pe_ready"], 1)
                    for j in range(4):
                        for r in range(2):
                            rows, q = slice(64 * r, 64 * r + 64), slice(32 * j, 32 * j + 32)
                            ins = t.matmul(bank[4 * s + 3 - 2 * r][32 * j:32 * j + 32, 0:128],
                                           XT[rows, s, 4, q], XT[rows, s, 0:4, q], start=True, stop=True)
                    ins.then_inc(b["s"], 1)
                for s in range(2):
                    t.wait_ge(b["pt"], w(s))
                    t.wait_ge(b["copied"], 4 * i + 2 * s + 2)
                    t.sem_inc(b["pe_ready"], 1)
                    for j in range(4):
                        for hp in range(4):
                            rows = slice(32 * j, 32 * j + 32)
                            dst = bank[4 * s + j][32 * hp:32 * hp + 32, 0:64]
                            probs = PTb[rows, s, :, :].rearrange("p (r h) q -> p r h q", r=2)[:, :, hp, :]
                            ins = t.matmul(dst, TT[rows, s, 8, 0, :], probs, start=True, stop=True)
                    ins.then_inc(b["pv"], 1)
                for s in range(2):
                    t.wait_ge(b["os"], w(s))
                    for r in range(2):
                        ins = t.matmul(bank[4 * s][:, 0:128], OS[:, s, r, :], Wvo[:, r, :], start=(r == 0), stop=(r == 1))
                    ins.then_inc(b["o"], 1)

            t.wait_ge(c["w_lo"], 5)
            t.wait_ge(sel_ready, 1)
            with t.Fori(0, TB) as tb:
                t.wait_ge(c["xe"], 4 * tb + 4)
                for n in range(4):
                    ins = t.transpose(bank[0][:, 128 * n:128 * n + 128], xe[:, n, :], I128[:, :])
                ins.then_inc(c["turned"], 1)
                t.wait_ge(c["xeT"], tb + 1)
                for n in range(4):
                    ins = t.matmul(bank[2][:, E * n:E * n + E], xeT[:, 128 * n:128 * n + 128], wrT[:, :], start=True, stop=True)
                ins.then_inc(c["logits"], 1)
                t.wait_ge(c["comb"], 8 * tb + 8)
                t.wait_ge(c["xeL"], 2 * tb + 2)
                for n in range(4):
                    ins = t.transpose(bank[3][0:2 * E, 128 * n:128 * n + 128], comb[:, n, :], I128[:, :])
                ins.then_inc(c["combT"], 1)
                t.wait_ge(c["ct"], tb + 1)
                for n in range(E * NC + 3):
                    at = E * NC * tb + n
                    if n < E * NC:
                        e, (c0, m) = n // NC, CH[n % NC]
                        if n % NC == 0:
                            if e:
                                t.wait_ge(c["cb"], E * tb + e)
                            t.matmul(bank[7][:, :], SELr[:, e, :], CT[:, :], start=True, stop=True).then_inc(c["cbm"], 1)
                        for name, wh, wl, bk in (("gate", GH, GL, n % 2), ("up", UH, UL, 2 + n % 2)):
                            if n >= 2:
                                t.wait_ge(c["silu"] if name == "gate" else c["hu"], at - 1)
                            s = slice(c0, c0 + m)
                            for q, (w_, x_) in enumerate(((wh, xeH), (wl, xeH), (wh, xeL))):
                                ins = t.matmul(bank[bk][0:m, :], w_[:, e, s], x_[:, :], start=(q == 0), stop=(q == 2))
                            ins.then_inc(c[name], 1)
                    if n >= 3:
                        o = n - 3
                        m = CH[o % NC][1]
                        t.wait_ge(c["hH"], at - 2)
                        t.wait_ge(c["hL"], at - 2)
                        for q, (w_, h_) in enumerate(((WH, hH), (WL, hH), (WH, hL))):
                            ins = t.matmul(bank[6][:, :], w_[0:m, o, :], h_[0:m, o % 4, :], start=(o == 0 and q == 0),
                                           stop=(o == E * NC - 1 and q == 2))
                        ins.then_inc(c["down"], 1)
                t.wait_ge(c["ys"], tb + 1)
                for n in range(4):
                    ins = t.transpose(bank[5][:, 128 * n:128 * n + 128], YS[:, 128 * n:128 * n + 128], I128[:, :])
                ins.then_inc(c["yT"], 1)


def kernel(x, ctx_1024, L0_xattn_Wv, L0_xattn_Wk, L0_xattn_Wq, L0_xattn_Wo, L0_xattn_bo, L0_attn_W_dkv, L0_attn_W_uk,
           L0_attn_W_uv, L0_attn_W_dq, L0_attn_W_uq, L0_attn_W_qr, L0_attn_W_kr, L0_attn_W_out, L0_attn_idx_wq,
           L0_attn_idx_wk, L0_attn_idx_w, L0_attn_raw_delta, L0_ffn_w_router, L0_ffn_w_gate, L0_ffn_w_up, L0_ffn_w_down):
    import numpy as np
    import concourse.bacc as bacc
    from concourse.bass_utils import run_bass_kernel_spmd

    a = lambda v: np.asarray(v)
    p = np.arange(128)
    angle = (p[:, None] % L) * (1.0 / 10000.0 ** (2.0 * np.arange(16) / DR))[None, :]
    chosen = np.zeros((2, E, E, 128), np.float32)
    for e in range(E):
        chosen[:, e, e, :] = 1.0
    arrays = {
        "x": a(x).reshape(B * L, D),
        "ctxT": a(ctx_1024).transpose(2, 0, 1).reshape(D, B * S),
        "wq": a(L0_xattn_Wq).T, "wk": a(L0_xattn_Wk).T, "wv": a(L0_xattn_Wv).T, "wo": a(L0_xattn_Wo).T,
        "bo": a(L0_xattn_bo),
        "w_dq": a(L0_attn_W_dq),
        "w_kv": np.concatenate([a(L0_attn_W_dkv), a(L0_attn_W_kr)], axis=1),
        "w_uqT": a(L0_attn_W_uq).reshape(CQ, NH, DH).transpose(2, 1, 0),
        "w_ukT": a(L0_attn_W_uk).reshape(CKV, NH, DH).transpose(2, 1, 0),
        "w_uvT": a(L0_attn_W_uv).reshape(CKV, NH, DH).transpose(2, 1, 0),
        "w_qr": a(L0_attn_W_qr).reshape(CQ, NH, DR),
        "w_out": a(L0_attn_W_out).reshape(NH, DH, D).transpose(1, 0, 2),
        "raw_delta": a(L0_attn_raw_delta),
        "w_router": a(L0_ffn_w_router).T,
        "w_gate": a(L0_ffn_w_gate).transpose(2, 0, 1),
        "w_up": a(L0_ffn_w_up).transpose(2, 0, 1),
        "w_down": a(L0_ffn_w_down).transpose(2, 0, 1),
        "ident": np.eye(128, dtype=np.float32),
        "head_mask": ((p[:, None] // XD) % G == np.arange(G)[None, :]).astype(np.float32),
        "cos_pos": np.cos(angle).astype(np.float32),
        "sin_pos": np.sin(angle).astype(np.float32),
        "expert_rank": np.tile(E - np.arange(E, dtype=np.float32), (128, 1)),
        "expert_sel": chosen.reshape(2 * E, E, 128),
    }
    arrays = {n: np.ascontiguousarray(v) for n, v in arrays.items()}
    nc = bacc.Bacc("TRN2", target_bir_lowering=False, num_devices=1)
    aps = {n: nc.dram_tensor(n, v.shape, mybir.dt.from_np(v.dtype), kind="ExternalInput").ap() for n, v in arrays.items()}
    aps["out"] = nc.dram_tensor("out", (B * L, D), F32, kind="ExternalOutput").ap()
    build(nc, **aps)
    r = run_bass_kernel_spmd(nc, [arrays], core_ids=[0])
    return r.results[0]["out"].reshape(B, L, D)
```

```python
import concourse.bass as bass
from concourse import mybir
from contextlib import ExitStack
import math

F32 = mybir.dt.float32
F32R = mybir.dt.float32r
ALU = mybir.AluOpType
ACT = mybir.ActivationFunctionType
AX = mybir.AxisListType

B, L, D = 64, 32, 128
S = 257
SP = 258
KC = SP // 3
XH, XD = 16, 8
G = 4
T = B * L // 128
NH, DH, DR = 8, 64, 32
CKV, CQ = 32, 64
E, I = 8, 352
PARTS = 4
CH = [(0, 128), (128, 128), (256, 96)]
NC = len(CH)
TB = 4
U = E * NC
EPS = 1e-5
BIG = 3.0e38


def bc(ap, shape):
    return ap.broadcast_to(shape)


def f(ap):
    return ap.bitcast(F32)


def counts(value):
    return not isinstance(value, int) or value > 0


def build(nc, x, ctxT, wq, wk, wv, wo, bo, w_dq, w_kv, w_uqT, w_ukT, w_uvT, w_qr, w_out, raw_delta,
          w_router, w_gate, w_up, w_down, ident, head_mask, cos_pos, sin_pos, own_sequence, expert_rank, expert_sel, out):
    held = ExitStack()
    with held:
        def sb(name, shape, dt=F32, stack=held):
            return stack.enter_context(nc.sbuf_tensor(name, shape, dt))

        def sem(name):
            return held.enter_context(nc.semaphore(name))

        X = sb("X", [128, T, D])
        I128 = sb("I128", [128, 128])
        mean = sb("mean", [128, T])
        var = sb("var", [128, T])
        rstd = sb("rstd", [128, T])
        std = sb("std", [128, T])
        ST = sb("ST", [128, T, 6])
        lnt = sb("lnt", [128, 4, T])
        WkvS = sb("WkvS", [128, CKV + DR])
        WdqS = sb("WdqS", [128, CQ])
        WA = sb("WA", [CQ, NH, 2, 32])
        Wvo = sb("Wvo", [128, 2, D])
        cosT = sb("cosT", [128, 16])
        sinT = sb("sinT", [128, 16])
        BM = sb("BM", [128, 4])
        wrT = sb("wrT", [128, E])
        rank = sb("rank", [128, E])
        SELr = sb("SELr", [32, E, 128], F32R)
        GW = sb("GW", [128, E, I])
        UW = sb("UW", [128, E, I])
        DW = sb("DW", [128, E * NC, D])
        GH, GL = sb("GH", [128, E, I], F32R), sb("GL", [128, E, I], F32R)
        UH, UL = sb("UH", [128, E, I], F32R), sb("UL", [128, E, I], F32R)
        WH, WL = sb("WH", [128, E * NC, D], F32R), sb("WL", [128, E * NC, D], F32R)

        first = ExitStack()
        XL = sb("XL", [128, T, D], F32, first)
        XLT = sb("XLT", [128, T * 128], F32, first)
        QH = sb("QH", [128, T * 128], F32R, first)
        QL = sb("QL", [128, T * 128], F32R, first)
        CR = sb("CR", [128, 4, S], F32, first)
        CHi = sb("CHi", [128, 4, SP], F32R, first)
        CLo = sb("CLo", [128, 4, SP], F32R, first)
        KH = sb("KH", [128, 2, SP], F32R, first)
        KL = sb("KL", [128, 2, SP], F32R, first)
        V = sb("V", [KC, 4, 3, D], F32, first)
        QMH = sb("QMH", [128, 4, G, L], F32R, first)
        QML = sb("QML", [128, 4, G, L], F32R, first)
        PR = sb("PR", [128, 2, G, SP], F32, first)
        PT = sb("PT", [KC, 3, 512], F32, first)
        nmax = sb("nmax", [128, G], F32, first)
        rsum = sb("rsum", [128, G], F32, first)
        rinv = sb("rinv", [128, G], F32, first)
        OM = sb("OM", [128, G, L], F32, first)
        OT = sb("OT", [128, 128], F32, first)
        WqS, WkS, WvS, WoS = (sb(n, [128, 128], F32, first) for n in ("WqS", "WkS", "WvS", "WoS"))
        WkH, WkL = sb("WkH", [128, 128], F32R, first), sb("WkL", [128, 128], F32R, first)
        WvH, WvL = sb("WvH", [128, 128], F32R, first), sb("WvL", [128, 128], F32R, first)
        boB = sb("boB", [128, D], F32, first)
        HM = sb("HM", [128, G], F32, first)
        small = sb("small", [128, 6, 16], F32, first)
        cpos, spos = sb("cpos", [128, 16], F32, first), sb("spos", [128, 16], F32, first)
        uqT = sb("uqT", [DH, NH, CQ], F32, first)
        ukT = sb("ukT", [DH, NH, CKV], F32, first)
        uvT = sb("uvT", [DH, NH, CKV], F32, first)
        woutS = PT[0:DH, 0:2, :].rearrange("p a n -> p (a n)").rearrange("p (h d) -> p h d", h=NH)
        SEL = sb("SEL", [32, E, 128], F32, first)
        first.close()

        OUT = sb("OUT", [128, 4, D])
        second = ExitStack()
        xl = sb("xl", [128, 2, 128], F32, second)
        xlT = sb("xlT", [128, 2, 128], F32, second)
        cqT = sb("cqT", [CQ, 2, 128], F32, second)
        RR = sb("RR", [128, 2, 9, 32], F32, second)
        AB = sb("AB", [128, 2, 9, 32], F32, second)
        EX = sb("EX", [128, 2, 9, 32], F32, second)
        LG = sb("LG", [128, 2, 9, 32], F32, second)
        SPL = sb("SPL", [128, 2, 9, 2, 16], F32, second)
        MC = sb("MC", [128, 2, 9, 2, 16], F32, second)
        MS = sb("MS", [128, 2, 9, 2, 16], F32, second)
        TT = sb("TT", [128, 2, 10, 2, 32], F32, second)
        XT = sb("XT", [128, 2, 5, 128], F32, second)
        SS = sb("SS", [128, 2, 8, 32], F32, second)
        SD = sb("SD", [128, 2, 8, 32], F32, second)
        SE = sb("SE", [128, 2, 8, 32], F32, second)
        SN = sb("SN", [128, 2, 8, 32], F32, second)
        PTb = sb("PTb", [128, 2, 8, 32], F32, second)
        CKB = sb("CKB", [128, 2, 4, 32], F32, second)
        nm8 = sb("nm8", [128, 2, 8], F32, second)
        s8 = sb("s8", [128, 2, 8], F32, second)
        r8 = sb("r8", [128, 2, 8], F32, second)
        OS = sb("OS", [128, 2, 2, 128], F32, second)
        second.close()
        xe = sb("xe", [128, T, 128])
        xeT = sb("xeT", [128, T * 128])
        xeH, xeL = sb("xeH", [128, T * 128], F32R), sb("xeL", [128, T * 128], F32R)
        tk = sb("tk", [128, 10, T, E])
        tm = sb("tm", [128, 8, T])
        cHi = sb("cHi", [128, T, E], F32R)
        comb = sb("comb", [128, T, 32])
        CT = sb("CT", [32, T * 128], F32R)
        CB = sb("CB", [128, 2, 512])
        sg = sb("sg", [128, 2, 512])
        hu = sb("hu", [128, 2, 512])
        hc = sb("hc", [128, 2, 512])
        hH, hL = sb("hH", [128, 4, 512], F32R), sb("hL", [128, 4, 512], F32R)
        YS = sb("YS", [128, 512])

        PS = held.enter_context(nc.psum_tensor("PS", [128, 8, 512], F32))
        bank = [PS[:, i, :] for i in range(8)]

        in_x, in_ident, in_sa, in_wqk, in_attn, in_moe, in_rot = (sem("in_" + n) for n in ("x", "ident", "sa", "wqk", "attn", "moe", "rot"))
        in_ctx = [sem(f"in_ctx{j}") for j in range(4)]
        ln_step, std_ready, ln_out = sem("ln_step"), sem("std_ready"), sem("ln_out")
        x1_stats, x2_stats = sem("x1_stats"), sem("x2_stats")
        ln_turned, ln_copied = sem("ln_turned"), sem("ln_copied")
        q_ready, q_scaled, q_hi, q_lo = sem("q_ready"), sem("q_scaled"), sem("q_hi"), sem("q_lo")
        w_split, pad_set = sem("w_split"), sem("pad_set")
        x_biased = sem("x_biased")
        rot_step, rot_act = sem("rot_step"), sem("rot_act")
        absorbed, absorbed_out = sem("absorbed"), sem("absorbed_out")
        sel_ready, wqr_in = sem("sel_ready"), sem("wqr_in")
        ctx_hi, ctx_lo, qm_hi, qm_lo = sem("ctx_hi"), sem("ctx_lo"), sem("qm_hi"), sem("qm_lo")
        k_proj, v_proj, k_hi, k_lo, v_copied = sem("k_proj"), sem("v_proj"), sem("k_hi"), sem("k_lo"), sem("v_copied")
        scores, max_ready, exped, sums_inv, normed = sem("scores"), sem("max_ready"), sem("exped"), sem("sums_inv"), sem("normed")
        p_turned, pt_act, pt_dve = sem("p_turned"), sem("pt_act"), sem("pt_dve")
        pv_done, o_masked, o_summed, wo_done, x1_ready = sem("pv_done"), sem("o_masked"), sem("o_summed"), sem("wo_done"), sem("x1_ready")

        b = {n: sem("b_" + n) for n in (
            "xl", "turned", "xlT", "cqT", "kv", "q", "rr", "abs", "exp", "ln", "copied", "sp", "mc", "ms",
            "rot", "dup", "T", "xt_a", "xt_v", "s", "ss", "max", "sub", "se", "sum", "inv", "norm", "pt", "pv",
            "os", "o", "x2", "pe_ready", "kr", "ckv", "blocks")}
        c = {n: sem("c_" + n) for n in (
            "xe", "turned", "xeT", "xeH", "xeL", "logits", "tk", "e2", "comb", "combT", "ct", "cbm", "cb",
            "zero", "gate", "up", "silu", "hu", "hc", "hH", "hL", "down", "ys", "yT", "out", "w_hi", "w_lo")}
        stored, out_free = sem("stored"), sem("out_free")

        PAIRS = T // 2

        def first_of(i, s):
            return 2 * i + s + 1

        def second_of(i, s):
            return 2 * i + s - 1

        LN_STEPS = 8

        def finish_norm(v, n):
            done = [LN_STEPS * n]

            def step(ins):
                ins.then_inc(ln_step, 1)
                done[0] += 1
                return done[0]

            half, dif, dev = lnt[:, 0, :], lnt[:, 1, :], lnt[:, 2, :]
            step(v.tensor_tensor(half, ST[:, :, 1], ST[:, :, 4], ALU.add))
            step(v.tensor_tensor(dif, ST[:, :, 1], ST[:, :, 4], ALU.subtract))
            n3 = step(v.tensor_tensor(dev, ST[:, :, 2], ST[:, :, 5], ALU.add))
            v.wait_ge(ln_step, n3)
            step(v.tensor_scalar(mean[:, :], half, 0.5, None, ALU.mult))
            step(v.scalar_tensor_tensor(out=lnt[:, 3, :], in0=dif, scalar=0.25, in1=dif, op0=ALU.mult, op1=ALU.mult))
            n6 = step(v.tensor_scalar(var[:, :], dev, 1.0 / D, EPS, ALU.mult, ALU.add))
            v.wait_ge(ln_step, n6)
            step(v.tensor_tensor(var[:, :], var[:, :], lnt[:, 3, :], ALU.add))
            v.wait_ge(std_ready, n + 1)
            n8 = step(v.reciprocal(rstd[:, :], std[:, :]))
            v.wait_ge(ln_step, n8)

        def root(a, n):
            a.wait_ge(ln_step, LN_STEPS * n + 7)
            a.activation(std[:, :], var[:, :], ACT.Sqrt).then_inc(std_ready, 1)

        block = held.enter_context(nc.Block())

        @block.sync
        def _(sp):
            sp.dma_start(X[:, :, :], x.rearrange("(t p) d -> p t d", p=128)).then_inc(in_x, 16)
            sp.dma_start(I128[:, :], ident).then_inc(in_ident, 16)
            for dst, src in ((WqS, wq), (WkS, wk), (WvS, wv), (WoS, wo), (HM, head_mask)):
                sp.dma_start(dst[:, :], src).then_inc(in_wqk, 16)
            sp.dma_start(boB[:, :], bc(bo.unsqueeze(0), [128, D])).then_inc(in_wqk, 16)

            def load_ctx(k, j):
                if not isinstance(k, int) or k >= 4:
                    sp.wait_ge(ctx_lo, k - 3)
                sp.dma_start(CR[:, j, :], ctxT[:, bass.ds(k * S, S)]).then_inc(in_ctx[j], 16)

            for j in range(4):
                load_ctx(j, j)
            for dst, src in ((cpos, cos_pos), (spos, sin_pos), (BM, own_sequence)):
                sp.dma_start(dst[:, :], src).then_inc(in_rot, 16)
            sp.dma_start(small[:, 0, :], bc(raw_delta.unsqueeze(0), [128, 16])).then_inc(in_rot, 16)
            for dst, src in ((uqT[:, :, :], w_uqT), (ukT[:, :, :], w_ukT), (uvT[:, :, :], w_uvT), (woutS, w_out)):
                sp.dma_start(dst, src).then_inc(in_attn, 16)
            sp.dma_start(WA[:, :, 1, :], w_qr).then_inc(wqr_in, 16)
            sp.dma_start(WkvS[:, :], w_kv).then_inc(in_attn, 16)
            sp.dma_start(WdqS[:, :], w_dq).then_inc(in_attn, 16)
            sp.dma_start(SEL[:, :, :], expert_sel).then_inc(in_attn, 16)
            for j in range(4):
                load_ctx(4 + j, j)
            sp.dma_start(GW[:, :, :], w_gate).then_inc(in_moe, 16)
            sp.dma_start(UW[:, :, :], w_up).then_inc(in_moe, 16)
            for n, (c0, m) in enumerate(CH):
                sp.dma_start(DW[0:m, n::NC, :], w_down[c0:c0 + m, :, :]).then_inc(in_moe, 16)
            sp.dma_start(wrT[:, :], w_router).then_inc(in_moe, 16)
            sp.dma_start(rank[:, :], expert_rank).then_inc(in_moe, 16)
            with sp.Fori(2, T) as i:
                for j in range(4):
                    load_ctx(4 * i + j, j)
            sp.sem_inc(out_free, 1)
            with sp.Fori(0, TB) as tb:
                sp.wait_ge(c["out"], 4 * tb + 4)
                sp.dma_start(out[bass.ds(tb * 512, 512), :].rearrange("(t p) d -> p t d", p=128), OUT[:, :, :]).then_inc(stored, 16)
                sp.wait_ge(stored, 16 * tb + 16)
                sp.sem_inc(out_free, 1)

        @block.gpsimd
        def _(g):
            g.memset(f(CHi[:, :, S:SP]), 0.0).then_inc(pad_set, 1)
            g.memset(f(CLo[:, :, S:SP]), 0.0).then_inc(pad_set, 1)
            g.memset(PR[:, :, :, S:SP], 0.0).then_inc(pad_set, 1)

            def prepare(i, j):
                k = 4 * i + j
                if isinstance(i, int) and k == 0:
                    g.wait_ge(q_lo, 4)
                g.wait_ge(in_ctx[j], 16 * i + 16)
                if counts(k - 3):
                    g.wait_ge(v_proj, k - 3)
                if counts(4 * k - 12):
                    g.wait_ge(scores, 4 * k - 12)
                mask = bc(HM[:, :].unsqueeze(2), [128, G, L])
                g.tensor_tensor(QMH[:, j, :, :], bc(f(QH[:, bass.ds(k * L, L)]).unsqueeze(1), [128, G, L]), mask,
                                ALU.mult).then_inc(qm_hi, 1)
                g.tensor_tensor(QML[:, j, :, :], bc(f(QL[:, bass.ds(k * L, L)]).unsqueeze(1), [128, G, L]), mask,
                                ALU.mult).then_inc(qm_lo, 1)
                g.tensor_copy(CHi[:, j, 0:S], CR[:, j, :]).then_inc(ctx_hi, 1)
                g.wait_ge(ctx_hi, k + 1)
                g.tensor_tensor(CLo[:, j, 0:S], CR[:, j, :], f(CHi[:, j, 0:S]), ALU.subtract).then_inc(ctx_lo, 1)

            g.wait_ge(in_wqk, 96)
            for j in range(4):
                prepare(0, j)
            def split_expert(e, n, hi, lo, w):
                g.tensor_copy(hi, w).then_inc(c["w_hi"], 1)
                g.wait_ge(c["w_hi"], PARTS * e + n)
                g.tensor_tensor(lo, w, f(hi), ALU.subtract).then_inc(c["w_lo"], 1)

            with g.Fori(1, T - E) as i:
                for j in range(4):
                    prepare(i, j)
            g.wait_ge(in_moe, 16 * 7)
            with g.Fori(T - E, T) as i:
                e = i - (T - E)
                for j in range(4):
                    prepare(i, j)
                    if j < 2:
                        w, hi, lo = ((GW, GH, GL), (UW, UH, UL))[j]
                        at = (slice(None), bass.ds(e, 1), slice(None))
                        split_expert(e, j + 1, hi[at], lo[at], w[at])
                    else:
                        rows = slice(0, CH[j - 1][1])
                        first, count = ((0, 2), (2, 1))[j - 2]
                        at = (rows, bass.ds(NC * e + first, count), slice(None))
                        split_expert(e, j + 1, WH[at], WL[at], DW[at])

            def first_stage(i):
                for s in range(2):
                    w = first_of(i, s)
                    g.wait_ge(b["ckv"], w)
                    if counts(w - 2):
                        g.wait_ge(b["pv"], w - 2)
                    g.tensor_tensor(CKB[:, s, :, :], bc(TT[:, s, 8, 0, :].unsqueeze(1), [128, 4, 32]),
                                    bc(BM[:, :].unsqueeze(2), [128, 4, 32]), ALU.mult).then_inc(b["blocks"], 1)
                for s in range(2):
                    w = first_of(i, s)
                    g.wait_ge(b["sp"], w)
                    full = [128, 9, 2, 16]
                    g.tensor_tensor(MS[:, s, :, :, :], SPL[:, s, :, :, :], bc(sinT[:, :].unsqueeze(1).unsqueeze(1), full), ALU.mult).then_inc(b["ms"], 1)

            g.wait_ge(in_rot, 64)
            first_stage(0)
            with g.Fori(1, PAIRS) as i:
                first_stage(i)

            def weighted(tb, n):
                e, m = n // NC, CH[n % NC][1]
                at = U * tb + n
                g.wait_ge(c["cb"], E * tb + e + 1)
                g.wait_ge(c["hu"], at + 1)
                if counts(at - 1):
                    g.wait_ge(c["hL"], at - 1)
                g.tensor_tensor(hc[0:m, n % 2, :], hu[0:m, n % 2, :], CB[0:m, e % 2, :], ALU.mult).then_inc(c["hc"], 1)

            g.wait_ge(b["x2"], T)
            g.memset(comb[:, :, 2 * E:32], 0.0).then_inc(c["zero"], 1)
            for n in range(U):
                weighted(0, n)
            with g.Fori(1, TB) as tb:
                for n in range(U):
                    weighted(tb, n)

        @block.scalar
        def _(a):
            root(a, 0)
            a.wait_ge(in_rot, 64)
            a.activation(small[:, 1, :], small[:, 0, :], ACT.Exp, scale=-1.0).then_inc(rot_act, 1)
            for n in range(4):
                a.wait_ge(ln_turned, n + 1)
                a.activation(XLT[:, 512 * n:512 * n + 512], bank[n][:, :], ACT.Copy).then_inc(ln_copied, 1)
            for n in range(4):
                a.wait_ge(q_ready, n + 1)
                a.activation(XL[:, 4 * n:4 * n + 4, :].rearrange("p t d -> p (t d)"), bank[4 + n][:, :], ACT.Copy,
                             scale=XD ** -0.5).then_inc(q_scaled, 1)

            a.wait_ge(rot_step, 5)
            a.activation(small[:, 3, :], small[:, 2, :], ACT.Sin).then_inc(rot_act, 1)
            a.activation(small[:, 5, :], small[:, 4, :], ACT.Sin).then_inc(rot_act, 1)

            def k_high(k, j):
                a.wait_ge(k_proj, k + 1)
                if counts(4 * k - 4):
                    a.wait_ge(scores, 4 * k - 4)
                a.activation(KH[:, j % 2, :], bank[7][:, 0:SP], ACT.Copy).then_inc(k_hi, 1)

            def v_copy(k, j):
                a.wait_ge(v_proj, k + 1)
                if counts(k - 3):
                    a.wait_ge(pv_done, k - 3)
                a.activation(V[:, j, :, :], PS[0:KC, 0:3, 384:512], ACT.Copy).then_inc(v_copied, 1)

            def exps(k, j):
                if counts(3 * k - 3):
                    a.wait_ge(p_turned, 3 * k - 3)
                if counts(4 * k - 4):
                    a.wait_ge(normed, 4 * k - 4)
                for gr in range(G):
                    a.wait_ge(max_ready, 4 * k + gr + 1)
                    if gr == 0:
                        if counts(k):
                            a.wait_ge(sums_inv, k)
                    a.activation(PR[:, j % 2, gr, 0:S], bank[gr][:, 0:S], ACT.Exp, bias=nmax[:, gr:gr + 1],
                                 accum_out=rsum[:, gr:gr + 1]).then_inc(exped, 1)

            def turned_copy(k, ch):
                a.wait_ge(p_turned, 3 * k + ch + 1)
                if counts(k):
                    a.wait_ge(pv_done, k)
                a.activation(PT[:, ch, :], bank[4 + ch][0:KC, :], ACT.Copy).then_inc(pt_act, 1)

            def step(k, j, last=False):
                if not last or k + 2 < B:
                    k_high(k + 2, j + 2)
                if not isinstance(k, int) or k >= 1:
                    turned_copy(k - 1, 2)
                if not last or k + 1 < B:
                    exps(k + 1, j + 1)
                turned_copy(k, 0)
                if not last or k + 2 < B:
                    v_copy(k + 2, (j + 2) % 4)

            for k in range(2):
                k_high(k, k)
                v_copy(k, k)
            exps(0, 0)
            for k in range(4):
                step(k, k)
            with a.Fori(1, T - 1) as i:
                for j in range(4):
                    step(4 * i + j, j)
            for k in range(B - 4, B):
                step(k, k % 4, True)
            turned_copy(B - 1, 2)

            root(a, 1)

            def normed_turned(i):
                for s in range(2):
                    a.wait_ge(b["turned"], first_of(i, s))
                    a.activation(xlT[:, s, :], bank[s][:, 0:128], ACT.Copy).then_inc(b["xlT"], 1)

            def softmax_exp(i):
                for s in range(2):
                    a.wait_ge(b["sub"], second_of(i, s))
                    a.activation(SE[:, s, :, :], SD[:, s, :, :], ACT.Exp, scale=(DH + DR) ** -0.5).then_inc(b["se"], 1)

            def softplus_log(i):
                for s in range(2):
                    w = first_of(i, s)
                    q = bank[2 + s][:, :].rearrange("p (h c d) -> p h c d", c=2, d=32)
                    a.wait_ge(b["q"], w)
                    a.activation(RR[:, s, 0:8, :], q[:, :, 1, :], ACT.Copy).then_inc(b["rr"], 1)
                    a.wait_ge(b["rr"], w)
                    a.wait_ge(b["kr"], w)
                    a.activation(AB[:, s, :, :], RR[:, s, :, :], ACT.Abs).then_inc(b["abs"], 1)
                    a.wait_ge(b["abs"], w)
                    a.activation(EX[:, s, :, :], AB[:, s, :, :], ACT.Exp, scale=-1.0).then_inc(b["exp"], 1)
                for s in range(2):
                    w = first_of(i, s)
                    a.wait_ge(b["exp"], w)
                    a.activation(LG[:, s, :, :], EX[:, s, :, :], ACT.Ln, bias=1.0).then_inc(b["ln"], 1)
                for s in range(2):
                    q = bank[2 + s][:, :].rearrange("p (h c d) -> p h c d", c=2, d=32)
                    a.activation(TT[:, s, 0:8, 0, :], q[:, :, 0, :], ACT.Copy).then_inc(b["copied"], 1)

            def rotated(i):
                for s in range(2):
                    a.wait_ge(b["T"], first_of(i, s))
                    a.activation(XT[:, s, 0:4, :].rearrange("p a n -> p (a n)"), bank[2 + s][:, :], ACT.Copy).then_inc(b["xt_a"], 1)

            normed_turned(0)
            softplus_log(0)
            rotated(0)
            with a.Fori(1, PAIRS) as i:
                normed_turned(i)
                softmax_exp(i)
                softplus_log(i)
                rotated(i)
            softmax_exp(PAIRS)

            root(a, 2)
            for n in range(4):
                s = slice(512 * n, 512 * n + 512)
                a.wait_ge(c["turned"], n + 1)
                a.activation(xeT[:, s], bank[n][:, :], ACT.Copy).then_inc(c["xeT"], 1)
                a.activation(xeH[:, s], bank[n][:, :], ACT.Copy).then_inc(c["xeH"], 1)
            a.wait_ge(c["tk"], 11)
            a.activation(tm[:, 5, :], tm[:, 4, :], ACT.Exp).then_inc(c["e2"], 1)

            def gated(tb, n):
                at = U * tb + n
                a.wait_ge(c["gate"], at + 1)
                if counts(at - 1):
                    a.wait_ge(c["hu"], at - 1)
                m = CH[n % NC][1]
                a.activation(sg[0:m, n % 2, :], bank[n % 2][0:m, :], ACT.Silu).then_inc(c["silu"], 1)

            def spread(tb, e):
                a.wait_ge(c["cbm"], E * tb + e + 1)
                if counts(U * tb + NC * (e - 1)):
                    a.wait_ge(c["hc"], U * tb + NC * (e - 1))
                a.activation(CB[:, e % 2, :], bank[7][:, :], ACT.Copy).then_inc(c["cb"], 1)

            def hidden_high(tb, n):
                at = U * tb + n
                o = (n - 2) % U
                m = CH[o % NC][1]
                a.wait_ge(c["hc"], at - 1)
                if counts(at - 5):
                    a.wait_ge(c["down"], at - 5)
                a.activation(hH[0:m, o % 4, :], hc[0:m, o % 2, :], ACT.Copy).then_inc(c["hH"], 1)

            def summed(tb):
                a.wait_ge(c["down"], U * tb)
                a.activation(YS[:, :], bank[6][:, :], ACT.Copy).then_inc(c["ys"], 1)

            def block_of(tb, first=False):
                for n in range(U):
                    if n % NC == 0 and not (first and n == 0):
                        spread(tb, n // NC)
                    gated(tb, n)
                    if n == 3 and not first:
                        summed(tb)
                    if first and n == 1:
                        for m in range(4):
                            a.wait_ge(c["combT"], m + 1)
                            a.activation(CT[:, 512 * m:512 * m + 512], bank[4 + m][0:32, :], ACT.Copy).then_inc(c["ct"], 1)
                        spread(tb, 0)
                    if n >= 2 or not first:
                        hidden_high(tb, n)

            block_of(0, True)
            with a.Fori(1, TB) as tb:
                block_of(tb)
            for n in range(2):
                hidden_high(TB, n)
            summed(TB)

        @block.vector
        def _(v):
            v.wait_ge(in_x, 16)
            for t in range(T):
                v.bn_stats(ST[:, t, :], X[:, t, :]).then_inc(x1_stats, 1)
            v.wait_ge(x1_stats, T)
            finish_norm(v, 0)
            for t in range(T):
                v.tensor_scalar(XL[:, t, :], X[:, t, :], mean[:, t:t + 1], rstd[:, t:t + 1], ALU.subtract, ALU.mult).then_inc(ln_out, 1)
            v.wait_ge(in_wqk, 96)
            v.tensor_copy(WkH[:, :], WkS[:, :]).then_inc(w_split, 1)
            v.tensor_copy(WvH[:, :], WvS[:, :]).then_inc(w_split, 1)
            v.wait_ge(w_split, 2)
            v.tensor_tensor(WkL[:, :], WkS[:, :], f(WkH[:, :]), ALU.subtract).then_inc(w_split, 1)
            v.tensor_tensor(WvL[:, :], WvS[:, :], f(WvH[:, :]), ALU.subtract).then_inc(w_split, 1)
            for n in range(4):
                v.wait_ge(q_scaled, n + 1)
                qs = XL[:, 4 * n:4 * n + 4, :].rearrange("p t d -> p (t d)")
                v.tensor_copy(QH[:, 512 * n:512 * n + 512], qs).then_inc(q_hi, 1)
                v.wait_ge(q_hi, n + 1)
                v.tensor_tensor(QL[:, 512 * n:512 * n + 512], qs, f(QH[:, 512 * n:512 * n + 512]), ALU.subtract).then_inc(q_lo, 1)

            def k_low(k, j):
                v.wait_ge(k_hi, k + 1)
                v.tensor_tensor(KL[:, j % 2, :], bank[7][:, 0:SP], f(KH[:, j % 2, :]), ALU.subtract).then_inc(k_lo, 1)

            def maxima(k):
                if counts(4 * k):
                    v.wait_ge(exped, 4 * k)
                for gr in range(G):
                    v.wait_ge(scores, 4 * k + gr + 1)
                    v.tensor_reduce(nmax[:, gr:gr + 1], bank[gr][:, 0:S], AX.X, ALU.max, negate=True).then_inc(max_ready, 1)

            def normalise(k, j):
                v.wait_ge(exped, 4 * k + 4)
                if counts(4 * k):
                    v.wait_ge(normed, 4 * k)
                v.reciprocal(rinv[:, :], rsum[:, :]).then_inc(sums_inv, 1)
                v.wait_ge(sums_inv, k + 1)
                for gr in range(G):
                    v.tensor_scalar(PR[:, j % 2, gr, 0:S], PR[:, j % 2, gr, 0:S], rinv[:, gr:gr + 1], None,
                                    ALU.mult).then_inc(normed, 1)

            def turned_copy(k):
                v.wait_ge(p_turned, 3 * k + 2)
                if counts(k):
                    v.wait_ge(pv_done, k)
                v.tensor_copy(PT[:, 1, :], bank[5][0:KC, :]).then_inc(pt_dve, 1)

            def own_blocks(k, j, unit):
                v.wait_ge(pv_done, k + 1)
                if counts(k):
                    v.wait_ge(o_summed, k)
                o = bank[7][:, 384:512].rearrange("p (h q) -> p h q", h=G)
                v.tensor_tensor(OM[:, :, :], o, bc(HM[:, :].unsqueeze(2), [128, G, L]), ALU.mult).then_inc(o_masked, 1)
                v.wait_ge(o_masked, k + 1)
                if j == 0:
                    if counts(unit):
                        v.wait_ge(wo_done, unit)
                v.tensor_reduce(OT[:, L * j:L * j + L], OM[:, :, :].rearrange("p h q -> p q h"), AX.X, ALU.add).then_inc(o_summed, 1)

            def residual(unit):
                v.wait_ge(wo_done, unit + 1)
                xt = X[:, bass.ds(unit, 1), :].rearrange("p t d -> p (t d)")
                v.tensor_tensor(xt, bank[3][:, 384:512], xt, ALU.add).then_inc(x1_ready, 1)
                v.wait_ge(x1_ready, unit + 1)
                v.bn_stats(ST[:, bass.ds(unit, 1), :].rearrange("p t s -> p (t s)"), xt).then_inc(x1_stats, 1)

            for n in range(4):
                s = slice(4 * n, 4 * n + 4)
                v.tensor_tensor(X[:, s, :], X[:, s, :], bc(boB[:, :].unsqueeze(1), [128, 4, D]), ALU.add).then_inc(x_biased, 1)
            v.wait_ge(rot_act, 1)
            sm = lambda n: small[:, n, :]
            v.tensor_scalar(sm(1), sm(1), 1.0, None, ALU.add).then_inc(rot_step, 1)
            v.wait_ge(rot_step, 1)
            v.reciprocal(sm(2), sm(1)).then_inc(rot_step, 1)
            v.wait_ge(rot_step, 2)
            v.tensor_scalar(sm(2), sm(2), -math.pi, math.pi / 2, ALU.mult, ALU.add).then_inc(rot_step, 1)
            v.wait_ge(rot_step, 3)
            v.scalar_tensor_tensor(out=sm(4), in0=sm(2), scalar=-1.0, in1=sm(2), op0=ALU.mult, op1=ALU.max).then_inc(rot_step, 1)
            v.wait_ge(rot_step, 4)
            v.tensor_scalar(sm(4), sm(4), -1.0, math.pi / 2, ALU.mult, ALU.add).then_inc(rot_step, 1)
            v.wait_ge(rot_act, 3)
            v.scalar_tensor_tensor(out=sm(1), in0=sm(3), scalar=-2.0, in1=sm(5), op0=ALU.mult, op1=ALU.mult).then_inc(rot_step, 1)
            v.scalar_tensor_tensor(out=sm(2), in0=sm(3), scalar=2.0, in1=sm(3), op0=ALU.mult, op1=ALU.mult).then_inc(rot_step, 1)
            v.wait_ge(rot_step, 7)
            v.tensor_scalar(sm(2), sm(2), 1.0, None, ALU.subtract).then_inc(rot_step, 1)
            v.wait_ge(rot_step, 8)
            v.tensor_tensor(cosT[:, :], cpos[:, :], sm(2), ALU.mult).then_inc(rot_step, 1)
            v.tensor_tensor(sm(0), spos[:, :], sm(1), ALU.mult).then_inc(rot_step, 1)
            v.tensor_tensor(sinT[:, :], spos[:, :], sm(2), ALU.mult).then_inc(rot_step, 1)
            v.tensor_tensor(sm(3), cpos[:, :], sm(1), ALU.mult).then_inc(rot_step, 1)
            v.wait_ge(rot_step, 12)
            v.tensor_tensor(cosT[:, :], cosT[:, :], sm(0), ALU.subtract).then_inc(rot_step, 1)
            v.tensor_tensor(sinT[:, :], sinT[:, :], sm(3), ALU.add).then_inc(rot_step, 1)
            v.wait_ge(absorbed, 1)
            v.tensor_copy(WA[:, :, 0, :], bank[5][0:CQ, 0:NH * 32].rearrange("p (h d) -> p h d", h=NH)).then_inc(absorbed_out, 1)
            v.wait_ge(absorbed, 2)
            v.tensor_copy(Wvo[:, :, :].rearrange("p r n -> p (r n)"), bank[6][:, 0:256]).then_inc(absorbed_out, 1)
            v.wait_ge(in_attn, 16 * 7)
            v.tensor_copy(SELr[:, :, :], SEL[:, :, :]).then_inc(sel_ready, 1)

            def step(k, j, unit, last=False):
                if not last or k + 2 < B:
                    k_low(k + 2, j + 2)
                if not last or k + 1 < B:
                    maxima(k + 1)
                if not isinstance(k, int) or k >= 1:
                    own_blocks(k - 1, (j - 1) % 4, unit - (j == 0))
                if not last or k + 1 < B:
                    normalise(k + 1, j + 1)
                turned_copy(k)
                if j == 0 and (not isinstance(unit, int) or unit >= 1):
                    residual(unit - 1)

            k_low(0, 0)
            k_low(1, 1)
            maxima(0)
            normalise(0, 0)
            for k in range(4):
                step(k, k, 0)
            with v.Fori(1, T - 1) as i:
                for j in range(4):
                    step(4 * i + j, j, i)
            for k in range(B - 4, B):
                step(k, k % 4, T - 1, True)
            own_blocks(B - 1, 3, T - 1)
            residual(T - 1)

            v.wait_ge(x1_stats, 2 * T)
            finish_norm(v, 1)

            def normed_tiles(i):
                for s in range(2):
                    t = 2 * i + s
                    v.tensor_scalar(xl[:, s, :], X[:, bass.ds(t, 1), :].rearrange("p t d -> p (t d)"),
                                    mean[:, bass.ds(t, 1)], rstd[:, bass.ds(t, 1)], ALU.subtract, ALU.mult).then_inc(b["xl"], 1)

            def centred_scores(i):
                for s in range(2):
                    w = second_of(i, s)
                    v.wait_ge(b["s"], w)
                    for r in range(2):
                        v.transpose(SS[:, s, 4 * r:4 * r + 4, :].rearrange("p h k -> p (h k)"), bank[4 + 2 * r + s][:, 0:128]).then_inc(b["ss"], 1)
                    v.wait_ge(b["ss"], 2 * w)
                    v.tensor_reduce(nm8[:, s, :], SS[:, s, :, :], AX.X, ALU.max).then_inc(b["max"], 1)
                    v.wait_ge(b["max"], w)
                    v.tensor_tensor(SD[:, s, :, :], SS[:, s, :, :], bc(nm8[:, s, :].unsqueeze(2), [128, 8, 32]), ALU.subtract).then_inc(b["sub"], 1)

            def compressed(i):
                for s in range(2):
                    v.wait_ge(b["kv"], first_of(i, s))
                    v.tensor_copy(cqT[:, s, :], bank[s][0:CQ, 128:256]).then_inc(b["cqT"], 1)
                for s in range(2):
                    v.tensor_copy(RR[:, s, 8, :], bank[s][:, 256 + CKV:256 + CKV + DR]).then_inc(b["kr"], 1)
                    v.tensor_copy(TT[:, s, 8:10, 0, :], bc(bank[s][:, 256:256 + CKV].unsqueeze(1), [128, 2, 32])).then_inc(b["ckv"], 1)

            def probabilities(i):
                for s in range(2):
                    w = second_of(i, s)
                    v.wait_ge(b["se"], w)
                    v.tensor_reduce(s8[:, s, :], SE[:, s, :, :], AX.X, ALU.add).then_inc(b["sum"], 1)
                    v.wait_ge(b["sum"], w)
                    v.reciprocal(r8[:, s, :], s8[:, s, :]).then_inc(b["inv"], 1)
                    v.wait_ge(b["inv"], w)
                    v.tensor_tensor(SN[:, s, :, :], SE[:, s, :, :], bc(r8[:, s, :].unsqueeze(2), [128, 8, 32]), ALU.mult).then_inc(b["norm"], 1)
                    v.wait_ge(b["norm"], w)
                    v.transpose(PTb[:, s, :, :].rearrange("p h k -> p (h k)"), SN[:, s, :, :].rearrange("p h k -> p (h k)")).then_inc(b["pt"], 1)

            def weighted_turned(i):
                for s in range(2):
                    v.wait_ge(b["pv"], second_of(i, s))
                    v.transpose(OS[:, s, :, :].rearrange("p r n -> p (r n)"), bank[4 + s][:, 256:512]).then_inc(b["os"], 1)

            def rotate(i):
                for s in range(2):
                    w = first_of(i, s)
                    v.wait_ge(b["ln"], w)
                    v.scalar_tensor_tensor(out=SPL[:, s, :, :, :].rearrange("p h a d -> p h (a d)"), in0=RR[:, s, :, :], scalar=0.0,
                                           in1=LG[:, s, :, :], op0=ALU.max, op1=ALU.add).then_inc(b["sp"], 1)
                for s in range(2):
                    v.wait_ge(b["sp"], first_of(i, s))
                    full = [128, 9, 2, 16]
                    v.tensor_tensor(MC[:, s, :, :, :], SPL[:, s, :, :, :], bc(cosT[:, :].unsqueeze(1).unsqueeze(1), full), ALU.mult).then_inc(b["mc"], 1)
                for s in range(2):
                    w = first_of(i, s)
                    v.wait_ge(b["mc"], w)
                    v.wait_ge(b["ms"], w)
                    v.tensor_tensor(TT[:, s, 0:9, 1, 0:16], MC[:, s, :, 0, :], MS[:, s, :, 1, :], ALU.subtract).then_inc(b["rot"], 1)
                    v.tensor_tensor(TT[:, s, 0:9, 1, 16:32], MS[:, s, :, 0, :], MC[:, s, :, 1, :], ALU.add).then_inc(b["rot"], 1)
                    v.wait_ge(b["rot"], 2 * w)
                    v.tensor_copy(TT[:, s, 9, 1, :], TT[:, s, 8, 1, :]).then_inc(b["dup"], 1)

            def residual2(i):
                for s in range(2):
                    v.wait_ge(b["o"], second_of(i, s))
                    xt = X[:, bass.ds(2 * i + s - 2, 1), :].rearrange("p t d -> p (t d)")
                    v.tensor_tensor(xt, bank[6 + s][:, 128:256], xt, ALU.add).then_inc(b["x2"], 1)
                for s in range(2):
                    v.wait_ge(b["x2"], second_of(i, s))
                    xt = X[:, bass.ds(2 * i + s - 2, 1), :].rearrange("p t d -> p (t d)")
                    v.bn_stats(ST[:, bass.ds(2 * i + s - 2, 1), :].rearrange("p t s -> p (t s)"), xt).then_inc(x2_stats, 1)

            def rotated_keys(i):
                for s in range(2):
                    v.wait_ge(b["T"], first_of(i, s))
                    v.tensor_copy(XT[:, s, 4, :], bank[s][:, 384:512]).then_inc(b["xt_v"], 1)

            normed_tiles(0)
            compressed(0)
            rotate(0)
            rotated_keys(0)
            with v.Fori(1, PAIRS) as i:
                normed_tiles(i)
                centred_scores(i)
                compressed(i)
                probabilities(i)
                weighted_turned(i)
                rotate(i)
                residual2(i)
                rotated_keys(i)
            centred_scores(PAIRS)
            probabilities(PAIRS)
            weighted_turned(PAIRS)
            residual2(PAIRS)

            v.wait_ge(x2_stats, T)
            finish_norm(v, 2)
            for t in range(T):
                v.tensor_scalar(xe[:, t, :], X[:, t, :], mean[:, t:t + 1], rstd[:, t:t + 1], ALU.subtract, ALU.mult).then_inc(c["xe"], 1)
            for n in range(4):
                s = slice(512 * n, 512 * n + 512)
                v.wait_ge(c["xeH"], n + 1)
                v.tensor_tensor(xeL[:, s], bank[n][:, :], f(xeH[:, s]), ALU.subtract).then_inc(c["xeL"], 1)
            n = [0]

            def did(ins):
                n[0] += 1
                ins.then_inc(c["tk"], 1)
                return n[0]

            def small_step(ins):
                v.wait_ge(c["tk"], did(ins))

            lg = bank[4][:, 0:T * E].rearrange("p (t e) -> p t e", t=T)
            rk = bc(rank[:, :].unsqueeze(1), [128, T, E])
            wide = lambda ap: bc(ap.unsqueeze(2), [128, T, E])
            K = lambda m: tk[:, m, :, :]
            v.wait_ge(c["logits"], 1)
            small_step(v.tensor_reduce(tm[:, 0, :], lg, AX.X, ALU.max))
            small_step(v.tensor_tensor(K(0), lg, wide(tm[:, 0, :]), ALU.is_equal))
            small_step(v.tensor_tensor(K(1), K(0), rk, ALU.mult))
            small_step(v.tensor_reduce(tm[:, 1, :], K(1), AX.X, ALU.max))
            small_step(v.tensor_tensor(K(2), K(1), wide(tm[:, 1, :]), ALU.is_equal))
            small_step(v.scalar_tensor_tensor(out=K(3), in0=K(2), scalar=-BIG, in1=lg, op0=ALU.mult, op1=ALU.add))
            small_step(v.tensor_reduce(tm[:, 2, :], K(3), AX.X, ALU.max))
            small_step(v.tensor_tensor(K(4), K(3), wide(tm[:, 2, :]), ALU.is_equal))
            small_step(v.tensor_tensor(K(5), K(4), rk, ALU.mult))
            small_step(v.tensor_reduce(tm[:, 3, :], K(5), AX.X, ALU.max))
            did(v.tensor_tensor(tm[:, 4, :], tm[:, 2, :], tm[:, 0, :], ALU.subtract))
            small_step(v.tensor_tensor(K(6), K(5), wide(tm[:, 3, :]), ALU.is_equal))
            m = [0]

            def comb_step(ins):
                m[0] += 1
                ins.then_inc(c["comb"], 1)
                v.wait_ge(c["comb"], m[0])

            v.wait_ge(c["e2"], 1)
            comb_step(v.tensor_scalar(tm[:, 6, :], tm[:, 5, :], 1.0, None, ALU.add))
            comb_step(v.reciprocal(tm[:, 7, :], tm[:, 6, :]))
            comb_step(v.tensor_tensor(tm[:, 6, :], tm[:, 5, :], tm[:, 7, :], ALU.mult))
            comb_step(v.tensor_tensor(K(7), K(2), wide(tm[:, 7, :]), ALU.mult))
            comb_step(v.tensor_tensor(K(8), K(6), wide(tm[:, 6, :]), ALU.mult))
            comb_step(v.tensor_tensor(K(9), K(7), K(8), ALU.add))
            comb_step(v.tensor_copy(cHi[:, :, :], K(9)))
            v.tensor_copy(comb[:, :, 0:E], f(cHi[:, :, :])).then_inc(c["xeL"], 1)
            comb_step(v.tensor_tensor(comb[:, :, E:2 * E], K(9), f(cHi[:, :, :]), ALU.subtract))

            def multiplied(tb, n):
                at, m = U * tb + n, CH[n % NC][1]
                v.wait_ge(c["silu"], at + 1)
                v.wait_ge(c["up"], at + 1)
                if counts(at - 1):
                    v.wait_ge(c["hc"], at - 1)
                v.tensor_tensor(hu[0:m, n % 2, :], bank[2 + n % 2][0:m, :], sg[0:m, n % 2, :], ALU.mult).then_inc(c["hu"], 1)

            def hidden_low(tb, n):
                at = U * tb + n
                o = (n - 2) % U
                m = CH[o % NC][1]
                v.wait_ge(c["hH"], at - 1)
                v.tensor_tensor(hL[0:m, o % 4, :], hc[0:m, o % 2, :], f(hH[0:m, o % 4, :]), ALU.subtract).then_inc(c["hL"], 1)

            def result(tb):
                v.wait_ge(c["yT"], tb)
                v.wait_ge(out_free, tb)
                for n in range(4):
                    v.tensor_tensor(OUT[:, n, :], bank[5][:, 128 * n:128 * n + 128],
                                    X[:, bass.ds(4 * (tb - 1) + n, 1), :].rearrange("p t d -> p (t d)"), ALU.add).then_inc(c["out"], 1)

            for n in range(U):
                multiplied(0, n)
                if n >= 2:
                    hidden_low(0, n)
            with v.Fori(1, TB) as tb:
                for n in range(U):
                    multiplied(tb, n)
                    hidden_low(tb, n)
                    if n == 8:
                        result(tb)
            for n in range(2):
                hidden_low(TB, n)
            result(TB)

        @block.tensor
        def _(t):
            t.wait_ge(in_ident, 16)
            for n in range(4):
                for m in range(4):
                    t.wait_ge(ln_out, 4 * n + m + 1)
                    ins = t.transpose(bank[n][:, 128 * m:128 * m + 128], XL[:, 4 * n + m, :], I128[:, :])
                ins.then_inc(ln_turned, 1)
            t.wait_ge(in_wqk, 96)
            for n in range(4):
                t.wait_ge(ln_copied, n + 1)
                t.matmul(bank[4 + n][:, :], WqS[:, :], XLT[:, 512 * n:512 * n + 512], start=True, stop=True).then_inc(q_ready, 1)
            t.wait_ge(in_attn, 16 * 7)
            t.wait_ge(q_scaled, 4)
            for h in range(NH):
                ins = t.matmul(bank[5][0:CQ, 32 * h:32 * h + 32], uqT[:, h, :], ukT[:, h, :], start=True, stop=True)
            ins.then_inc(absorbed, 1)
            for h in range(NH):
                hp, r = h // 2, h % 2
                ins = t.matmul(bank[6][32 * hp:32 * hp + 32, 128 * r:128 * r + 128], uvT[:, h, :], woutS[:, h, :], start=True, stop=True)
            ins.then_inc(absorbed, 1)
            t.wait_ge(absorbed_out, 2)

            def project_keys(k, j):
                t.wait_ge(ctx_hi, k + 1)
                t.wait_ge(ctx_lo, k + 1)
                if counts(k):
                    t.wait_ge(k_lo, k)
                if counts(k - 3):
                    t.wait_ge(o_masked, k - 3)
                hi, lo = CHi[:, j, :], CLo[:, j, :]
                for n, (w, c_) in enumerate(((WkH, hi), (WkL, hi), (WkH, lo))):
                    ins = t.matmul(bank[7][:, 0:SP], w[:, :], c_, start=(n == 0), stop=(n == 2))
                ins.then_inc(k_proj, 1)

            def project_values(k, j, scored=True):
                hi, lo = CHi[:, j, :], CLo[:, j, :]
                if counts(k):
                    t.wait_ge(v_copied, k)
                for ch in range(3):
                    s = slice(KC * ch, KC * ch + KC)
                    if scored:
                        t.wait_ge(exped, 4 * k - 3 + ch)
                    for n, (w, c_) in enumerate(((WvH, hi), (WvL, hi), (WvH, lo))):
                        ins = t.matmul(bank[ch][0:KC, 384:512], c_[:, s], w[:, :], start=(n == 0), stop=(n == 2))
                ins.then_inc(v_proj, 1)

            def score(k, j, done=0):
                t.wait_ge(qm_hi, k + 1)
                t.wait_ge(qm_lo, k + 1)
                t.wait_ge(k_lo, k + 1)
                t.wait_ge(v_copied, 2 if isinstance(k, int) and k == 0 else k + 1)
                for gr in range(G):
                    rows = slice(32 * gr, 32 * gr + 32)
                    if counts(4 * k - 3 + gr):
                        t.wait_ge(exped, 4 * k - 3 + gr)
                    if gr == 3 and counts(done):
                        t.wait_ge(x1_ready, done)
                    qh, ql = (q[rows, j % 4, :, :].rearrange("p h q -> p (h q)") for q in (QMH, QML))
                    kh, kl = KH[rows, j % 2, :], KL[rows, j % 2, :]
                    for n, (q, kk) in enumerate(((qh, kh), (ql, kh), (qh, kl))):
                        ins = t.matmul(bank[gr][:, 0:SP], q, kk, start=(n == 0), stop=(n == 2))
                    ins.then_inc(scores, 1)

            def turn(k, j, ch):
                if ch == 1:
                    if counts(k):
                        t.wait_ge(pt_dve, k)
                else:
                    if counts(2 * k - 1 + ch // 2):
                        t.wait_ge(pt_act, 2 * k - 1 + ch // 2)
                for gr in range(G):
                    if ch == 0:
                        t.wait_ge(normed, 4 * k + gr + 1)
                    ins = t.transpose(bank[4 + ch][0:KC, 128 * gr:128 * gr + 128],
                                      PR[:, j % 2, gr, KC * ch:KC * ch + KC], I128[:, :])
                ins.then_inc(p_turned, 1)

            def weigh(k, j):
                t.wait_ge(k_lo, min(k + 4, B) if isinstance(k, int) else k + 4)
                if counts(k):
                    t.wait_ge(o_masked, k)
                for ch in range(3):
                    if ch == 1:
                        t.wait_ge(pt_dve, k + 1)
                    else:
                        t.wait_ge(pt_act, 2 * k + 1 + ch // 2)
                    for gr in range(G):
                        ins = t.matmul(bank[7][32 * gr:32 * gr + 32, 384:512], V[:, j, ch, 32 * gr:32 * gr + 32],
                                       PT[:, ch, 128 * gr:128 * gr + 128], start=(ch == 0), stop=(ch == 2))
                ins.then_inc(pv_done, 1)

            def project_out(unit):
                t.wait_ge(o_summed, 4 * unit + 4)
                t.wait_ge(exped, min(16 * unit + 24, 4 * B) if isinstance(unit, int) else 16 * unit + 24)
                t.matmul(bank[3][:, 384:512], OT[:, :], WoS[:, :], start=True, stop=True).then_inc(wo_done, 1)

            def step(k, j, unit, last=False):
                if not last or k + 2 < B:
                    project_keys(k + 2, (j + 2) % 4)
                if not last or k + 1 < B:
                    score(k + 1, j + 1, done=unit if j == 1 else 0)
                if not isinstance(k, int) or k >= 1:
                    weigh(k - 1, (j - 1) % 4)
                turn(k, j, 0)
                turn(k, j, 1)
                if not last or k + 2 < B:
                    project_values(k + 2, (j + 2) % 4)
                turn(k, j, 2)
                if j == 0 and (not isinstance(unit, int) or unit >= 1):
                    project_out(unit - 1)

            t.wait_ge(w_split, 4)
            t.wait_ge(pad_set, 3)
            for k in range(2):
                project_keys(k, k)
                project_values(k, k, False)
            score(0, 0)
            for k in range(4):
                step(k, k, 0)
            with t.Fori(1, T - 1) as i:
                for j in range(4):
                    step(4 * i + j, j, i)
            for k in range(B - 4, B):
                step(k, k % 4, T - 1, True)
            weigh(B - 1, 3)
            project_out(T - 1)

            t.wait_ge(wqr_in, 16)
            t.wait_ge(x1_ready, T)

            def turn_normed(i):
                for s in range(2):
                    t.wait_ge(b["xl"], first_of(i, s))
                    t.transpose(bank[s][:, 0:128], xl[:, s, :], I128[:, :]).then_inc(b["turned"], 1)

            def latent_scores(i):
                for s in range(2):
                    w = second_of(i, s)
                    t.wait_ge(b["xt_a"], w)
                    t.wait_ge(b["xt_v"], w)
                    t.sem_inc(b["pe_ready"], 1)
                    for j in range(4):
                        for r in range(2):
                            rows, q = slice(64 * r, 64 * r + 64), slice(32 * j, 32 * j + 32)
                            ins = t.matmul(bank[4 + 2 * r + s][32 * j:32 * j + 32, 0:128],
                                           XT[rows, s, 4, q], XT[rows, s, 0:4, q], start=True, stop=True)
                    ins.then_inc(b["s"], 1)

            def compress(i):
                for s in range(2):
                    t.wait_ge(b["xlT"], first_of(i, s))
                    t.matmul(bank[s][0:CQ, 128:256], WdqS[:, :], xlT[:, s, :], start=True, stop=True)
                    t.matmul(bank[s][:, 256:256 + CKV + DR], xlT[:, s, :], WkvS[:, :], start=True, stop=True).then_inc(b["kv"], 1)

            def queries(i):
                for s in range(2):
                    t.wait_ge(b["cqT"], first_of(i, s))
                    t.matmul(bank[2 + s][:, :], cqT[:, s, :], WA[:, :, :, :].rearrange("p h c d -> p (h c d)"),
                             start=True, stop=True).then_inc(b["q"], 1)

            def weigh_compressed(i):
                for s in range(2):
                    t.wait_ge(b["blocks"], second_of(i, s))
                    t.wait_ge(b["pt"], second_of(i, s))
                    for r in range(2):
                        probs = PTb[:, s, 4 * r:4 * r + 4, :].rearrange("p h q -> p (h q)")
                        ins = t.matmul(bank[4 + s][:, 256 + 128 * r:384 + 128 * r], probs,
                                       CKB[:, s, :, :].rearrange("p j d -> p (j d)"), start=True, stop=True)
                    ins.then_inc(b["pv"], 1)

            def latent_out(i):
                for s in range(2):
                    t.wait_ge(b["os"], second_of(i, s))
                    for r in range(2):
                        ins = t.matmul(bank[6 + s][:, 128:256], OS[:, s, r, :], Wvo[:, r, :], start=(r == 0), stop=(r == 1))
                    ins.then_inc(b["o"], 1)

            def turn_rotated(i):
                for s in range(2):
                    t.wait_ge(b["dup"], first_of(i, s))
                    t.wait_ge(b["copied"], first_of(i, s))
                    for n in range(5):
                        src = TT[:, s, 2 * n:2 * n + 2, :, :].rearrange("p h c d -> p (h c d)")
                        dst = bank[2 + s][:, 128 * n:128 * n + 128] if n < 4 else bank[s][:, 384:512]
                        ins = t.transpose(dst, src, I128[:, :])
                    ins.then_inc(b["T"], 1)

            turn_normed(0)
            compress(0)
            queries(0)
            turn_rotated(0)
            with t.Fori(1, PAIRS) as i:
                turn_normed(i)
                latent_scores(i)
                compress(i)
                queries(i)
                weigh_compressed(i)
                latent_out(i)
                turn_rotated(i)
            latent_scores(PAIRS)
            weigh_compressed(PAIRS)
            latent_out(PAIRS)

            t.wait_ge(b["x2"], T)
            for n in range(4):
                t.wait_ge(c["xe"], 4 * n + 4)
                for m in range(4):
                    ins = t.transpose(bank[n][:, 128 * m:128 * m + 128], xe[:, 4 * n + m, :], I128[:, :])
                ins.then_inc(c["turned"], 1)
            for m in range(T):
                if m % 4 == 0:
                    t.wait_ge(c["xeT"], m // 4 + 1)
                ins = t.matmul(bank[4][:, E * m:E * m + E], xeT[:, 128 * m:128 * m + 128], wrT[:, :], start=True, stop=True)
            ins.then_inc(c["logits"], 1)

            def spread(tb, e):
                if counts(E * tb + e):
                    t.wait_ge(c["cb"], E * tb + e)
                t.sem_inc(b["pe_ready"], 1)
                t.matmul(bank[7][:, :], SELr[:, e, :], CT[:, bass.ds(512 * tb, 512)], start=True, stop=True).then_inc(c["cbm"], 1)

            def gate_and_up(tb, n):
                e, (c0, m) = n // NC, CH[n % NC]
                at = U * tb + n
                xh, xl_ = xeH[:, bass.ds(512 * tb, 512)], xeL[:, bass.ds(512 * tb, 512)]
                for name, wh, wl, bk in (("gate", GH, GL, n % 2), ("up", UH, UL, 2 + n % 2)):
                    if counts(at - 1):
                        t.wait_ge(c["silu"] if name == "gate" else c["hu"], at - 1)
                    s = slice(c0, c0 + m)
                    for q, (w_, x_) in enumerate(((wh, xh), (wl, xh), (wh, xl_))):
                        ins = t.matmul(bank[bk][0:m, :], w_[:, e, s], x_, start=(q == 0), stop=(q == 2))
                    ins.then_inc(c[name], 1)

            def down(tb, n):
                at = U * tb + n
                o = (n - 3) % U
                m = CH[o % NC][1]
                t.wait_ge(c["hH"], at - 2)
                t.wait_ge(c["hL"], at - 2)
                if o == 0 and counts(tb):
                    t.wait_ge(c["ys"], tb)
                for q, (w_, h_) in enumerate(((WH, hH), (WL, hH), (WH, hL))):
                    ins = t.matmul(bank[6][:, :], w_[0:m, o, :], h_[0:m, o % 4, :], start=(o == 0 and q == 0),
                                   stop=(o == U - 1 and q == 2))
                ins.then_inc(c["down"], 1)

            def turn_back(tb):
                t.wait_ge(c["ys"], tb)
                t.wait_ge(out_free, tb)
                for n in range(4):
                    ins = t.transpose(bank[5][:, 128 * n:128 * n + 128], YS[:, 128 * n:128 * n + 128], I128[:, :])
                ins.then_inc(c["yT"], 1)

            def block_of(tb, first=False):
                for n in range(U):
                    if n % NC == 0 and not (first and n == 0):
                        spread(tb, n // NC)
                    gate_and_up(tb, n)
                    if first and n == 1:
                        t.wait_ge(c["comb"], 8)
                        t.wait_ge(c["zero"], 1)
                        for m in range(T):
                            ins = t.transpose(bank[4 + m // 4][0:32, 128 * (m % 4):128 * (m % 4) + 128], comb[:, m, :], I128[:, :])
                            if m % 4 == 3:
                                ins.then_inc(c["combT"], 1)
                        t.wait_ge(c["ct"], 4)
                        spread(tb, 0)
                    if n >= 3 or not first:
                        down(tb, n)
                    if n == 6 and not first:
                        turn_back(tb)

            t.wait_ge(c["w_lo"], PARTS * E)
            t.wait_ge(sel_ready, 1)
            t.wait_ge(c["xeL"], 4)
            block_of(0, True)
            with t.Fori(1, TB) as tb:
                block_of(tb)
            for n in range(3):
                down(TB, n)
            turn_back(TB)


def kernel(x, ctx_1024, L0_xattn_Wv, L0_xattn_Wk, L0_xattn_Wq, L0_xattn_Wo, L0_xattn_bo, L0_attn_W_dkv, L0_attn_W_uk,
           L0_attn_W_uv, L0_attn_W_dq, L0_attn_W_uq, L0_attn_W_qr, L0_attn_W_kr, L0_attn_W_out, L0_attn_idx_wq,
           L0_attn_idx_wk, L0_attn_idx_w, L0_attn_raw_delta, L0_ffn_w_router, L0_ffn_w_gate, L0_ffn_w_up, L0_ffn_w_down):
    import numpy as np
    import concourse.bacc as bacc
    from concourse.bass_utils import run_bass_kernel_spmd

    a = lambda v: np.asarray(v)
    p = np.arange(128)
    angle = (p[:, None] % L) * (1.0 / 10000.0 ** (2.0 * np.arange(16) / DR))[None, :]
    chosen = np.zeros((32 // E, E, E, 128), np.float32)
    for e in range(E):
        chosen[0:2, e, e, :] = 1.0
    arrays = {
        "x": a(x).reshape(B * L, D),
        "ctxT": a(ctx_1024).transpose(2, 0, 1).reshape(D, B * S),
        "wq": a(L0_xattn_Wq).T, "wk": a(L0_xattn_Wk).T, "wv": a(L0_xattn_Wv).T, "wo": a(L0_xattn_Wo).T,
        "bo": a(L0_xattn_bo),
        "w_dq": a(L0_attn_W_dq),
        "w_kv": np.concatenate([a(L0_attn_W_dkv), a(L0_attn_W_kr)], axis=1),
        "w_uqT": a(L0_attn_W_uq).reshape(CQ, NH, DH).transpose(2, 1, 0),
        "w_ukT": a(L0_attn_W_uk).reshape(CKV, NH, DH).transpose(2, 1, 0),
        "w_uvT": a(L0_attn_W_uv).reshape(CKV, NH, DH).transpose(2, 1, 0),
        "w_qr": a(L0_attn_W_qr).reshape(CQ, NH, DR),
        "w_out": a(L0_attn_W_out).reshape(NH, DH, D).transpose(1, 0, 2),
        "raw_delta": a(L0_attn_raw_delta),
        "w_router": a(L0_ffn_w_router).T,
        "w_gate": a(L0_ffn_w_gate).transpose(2, 0, 1),
        "w_up": a(L0_ffn_w_up).transpose(2, 0, 1),
        "w_down": a(L0_ffn_w_down).transpose(2, 0, 1),
        "ident": np.eye(128, dtype=np.float32),
        "head_mask": ((p[:, None] // XD) % G == np.arange(G)[None, :]).astype(np.float32),
        "cos_pos": np.cos(angle).astype(np.float32),
        "sin_pos": np.sin(angle).astype(np.float32),
        "own_sequence": (p[:, None] // L == np.arange(4)[None, :]).astype(np.float32),
        "expert_rank": np.tile(E - np.arange(E, dtype=np.float32), (128, 1)),
        "expert_sel": chosen.reshape(32, E, 128),
    }
    arrays = {n: np.ascontiguousarray(v) for n, v in arrays.items()}
    nc = bacc.Bacc("TRN2", target_bir_lowering=False, num_devices=1)
    aps = {n: nc.dram_tensor(n, v.shape, mybir.dt.from_np(v.dtype), kind="ExternalInput").ap() for n, v in arrays.items()}
    aps["out"] = nc.dram_tensor("out", (B * L, D), F32, kind="ExternalOutput").ap()
    build(nc, **aps)
    r = run_bass_kernel_spmd(nc, [arrays], core_ids=[0])
    return r.results[0]["out"].reshape(B, L, D)
```

```python
import concourse.bass as bass
from concourse import mybir
from contextlib import ExitStack
import math

F32 = mybir.dt.float32
F32R = mybir.dt.float32r
ALU = mybir.AluOpType
ACT = mybir.ActivationFunctionType
AX = mybir.AxisListType

B, L, D = 64, 32, 128
S = 257
SP = 258
KC = SP // 3
XH, XD = 16, 8
G = 4
T = B * L // 128
NH, DH, DR = 8, 64, 32
CKV, CQ = 32, 64
E, I = 8, 352
EPS = 1e-5
BIG = 3.0e38
TB = 4
U = E * I // 128
PARTS = 3
STARTS = [n for n in range(U) if n == 0 or 128 * n // I != (128 * n - 128) // I or (128 * n + 127) // I != (128 * n - 1) // I]
Q = len(STARTS)


def run_of(n):
    return max(q for q in range(Q) if STARTS[q] <= n)


def slot(n):
    return n % 4 if n < U - U % 4 else 4 + n % 4


def bc(ap, shape):
    return ap.broadcast_to(shape)


def f(ap):
    return ap.bitcast(F32)


def counts(value):
    return not isinstance(value, int) or value > 0


def build(nc, x, ctxT, wq, wk, wv, wo, bo, w_dq, w_kv, w_uqT, w_ukT, w_uvT, w_qr, w_out, raw_delta,
          w_router, w_gate, w_up, w_down, ident, head_mask, cos_pos, sin_pos, own_sequence, expert_rank, expert_sel, out):
    held = ExitStack()
    with held:
        def sb(name, shape, dt=F32, stack=held):
            return stack.enter_context(nc.sbuf_tensor(name, shape, dt))

        def sem(name):
            return held.enter_context(nc.semaphore(name))

        X = sb("X", [128, T, D])
        I128 = sb("I128", [128, 128])
        mean = sb("mean", [128, T])
        var = sb("var", [128, T])
        rstd = sb("rstd", [128, T])
        std = sb("std", [128, T])
        ST = sb("ST", [128, T, 6])
        lnt = sb("lnt", [128, 4, T])
        WkvS = sb("WkvS", [128, CKV + DR])
        WdqS = sb("WdqS", [128, CQ])
        WA = sb("WA", [CQ, NH, 2, 32])
        Wvo = sb("Wvo", [128, 2, D])
        cosT = sb("cosT", [128, 16])
        sinT = sb("sinT", [128, 16])
        BM = sb("BM", [128, 4])
        wrT = sb("wrT", [128, E])
        rank = sb("rank", [128, E])
        SELr = sb("SELr", [32, Q, 128], F32R)
        GW = sb("GW", [128, U, 128])
        UW = sb("UW", [128, U, 128])
        DW = sb("DW", [128, U, D])
        GH, GL = sb("GH", [128, U, 128], F32R), sb("GL", [128, U, 128], F32R)
        UH, UL = sb("UH", [128, U, 128], F32R), sb("UL", [128, U, 128], F32R)
        WH, WL = sb("WH", [128, U, D], F32R), sb("WL", [128, U, D], F32R)

        first = ExitStack()
        XL = sb("XL", [128, T, D], F32, first)
        XLT = sb("XLT", [128, T * 128], F32, first)
        QH = sb("QH", [128, T * 128], F32R, first)
        QL = sb("QL", [128, T * 128], F32R, first)
        CR = sb("CR", [128, 4, S], F32, first)
        CHi = sb("CHi", [128, 4, SP], F32R, first)
        CLo = sb("CLo", [128, 4, SP], F32R, first)
        KH = sb("KH", [128, 2, SP], F32R, first)
        KL = sb("KL", [128, 2, SP], F32R, first)
        V = sb("V", [KC, 4, 3, D], F32, first)
        QMH = sb("QMH", [128, 4, G, L], F32R, first)
        QML = sb("QML", [128, 4, G, L], F32R, first)
        PR = sb("PR", [128, 2, G, SP], F32, first)
        PT = sb("PT", [KC, 3, 512], F32, first)
        nmax = sb("nmax", [128, G], F32, first)
        rsum = sb("rsum", [128, G], F32, first)
        rinv = sb("rinv", [128, G], F32, first)
        OM = sb("OM", [128, G, L], F32, first)
        OT = sb("OT", [128, 128], F32, first)
        WqS, WkS, WvS, WoS = (sb(n, [128, 128], F32, first) for n in ("WqS", "WkS", "WvS", "WoS"))
        WkH, WkL = sb("WkH", [128, 128], F32R, first), sb("WkL", [128, 128], F32R, first)
        WvH, WvL = sb("WvH", [128, 128], F32R, first), sb("WvL", [128, 128], F32R, first)
        boB = sb("boB", [128, D], F32, first)
        HM = sb("HM", [128, G], F32, first)
        small = sb("small", [128, 6, 16], F32, first)
        cpos, spos = sb("cpos", [128, 16], F32, first), sb("spos", [128, 16], F32, first)
        uqT = sb("uqT", [DH, NH, CQ], F32, first)
        ukT = sb("ukT", [DH, NH, CKV], F32, first)
        uvT = sb("uvT", [DH, NH, CKV], F32, first)
        woutS = PT[0:DH, 0:2, :].rearrange("p a n -> p (a n)").rearrange("p (h d) -> p h d", h=NH)
        first.close()

        OUT = sb("OUT", [128, 4, D])
        second = ExitStack()
        xl = sb("xl", [128, 2, 128], F32, second)
        xlT = sb("xlT", [128, 2, 128], F32, second)
        cqT = sb("cqT", [CQ, 2, 128], F32, second)
        RR = sb("RR", [128, 2, 9, 32], F32, second)
        AB = sb("AB", [128, 2, 9, 32], F32, second)
        EX = sb("EX", [128, 2, 9, 32], F32, second)
        LG = sb("LG", [128, 2, 9, 32], F32, second)
        SPL = sb("SPL", [128, 2, 9, 2, 16], F32, second)
        MC = sb("MC", [128, 2, 9, 2, 16], F32, second)
        MS = sb("MS", [128, 2, 9, 2, 16], F32, second)
        TT = sb("TT", [128, 2, 10, 2, 32], F32, second)
        XT = sb("XT", [128, 2, 5, 128], F32, second)
        SS = sb("SS", [128, 2, 8, 32], F32, second)
        SD = sb("SD", [128, 2, 8, 32], F32, second)
        SE = sb("SE", [128, 2, 8, 32], F32, second)
        SN = sb("SN", [128, 2, 8, 32], F32, second)
        PTb = sb("PTb", [128, 2, 8, 32], F32, second)
        CKB = sb("CKB", [128, 2, 4, 32], F32, second)
        nm8 = sb("nm8", [128, 2, 8], F32, second)
        s8 = sb("s8", [128, 2, 8], F32, second)
        r8 = sb("r8", [128, 2, 8], F32, second)
        OS = sb("OS", [128, 2, 2, 128], F32, second)
        SEL = sb("SEL", [32, Q, 128], F32, second)
        second.close()
        xe = sb("xe", [128, T, 128])
        xeH, xeL = sb("xeH", [128, T * 128], F32R), sb("xeL", [128, T * 128], F32R)
        tk = sb("tk", [128, 10, T, E])
        tm = sb("tm", [128, 8, T])
        cHi = sb("cHi", [128, T, E], F32R)
        comb = sb("comb", [128, T, 32])
        CT = sb("CT", [32, T * 128], F32R)
        hidden = sb("hidden", [128, 4, 2, 512])
        CB, sg, hu, hc = (hidden[:, n, :, :] for n in range(4))
        xeT = hidden[:, 2:4, :, :].rearrange("p a b n -> p (a b n)")
        hH, hL = sb("hH", [128, 6, 512], F32R), sb("hL", [128, 6, 512], F32R)
        YS = sb("YS", [128, 512])

        PS = held.enter_context(nc.psum_tensor("PS", [128, 8, 512], F32))
        bank = [PS[:, i, :] for i in range(8)]

        in_x = [sem(f"in_x{n}") for n in range(4)]
        in_ident, in_wqk, in_attn, in_moe, in_rot = (sem("in_" + n) for n in ("ident", "wqk", "attn", "moe", "rot"))
        in_ctx = [sem(f"in_ctx{j}") for j in range(4)]
        ln_step, std_ready, ln_out = sem("ln_step"), sem("std_ready"), sem("ln_out")
        x1_stats, x2_stats = sem("x1_stats"), sem("x2_stats")
        ln_turned, ln_copied = sem("ln_turned"), sem("ln_copied")
        q_ready, q_scaled, q_hi, q_lo = sem("q_ready"), sem("q_scaled"), sem("q_hi"), sem("q_lo")
        w_split, pad_set = sem("w_split"), sem("pad_set")
        pool_normed = sem("pool_normed")
        x_biased = sem("x_biased")
        rot_step, rot_act = sem("rot_step"), sem("rot_act")
        absorbed, absorbed_out = sem("absorbed"), sem("absorbed_out")
        in_sel = sem("in_sel")
        sel_ready, wqr_in = sem("sel_ready"), sem("wqr_in")
        ctx_hi, ctx_lo, qm_hi, qm_lo = sem("ctx_hi"), sem("ctx_lo"), sem("qm_hi"), sem("qm_lo")
        k_proj, v_proj, k_hi, k_lo, v_copied = sem("k_proj"), sem("v_proj"), sem("k_hi"), sem("k_lo"), sem("v_copied")
        scores, max_ready, exped, sums_inv, normed = sem("scores"), sem("max_ready"), sem("exped"), sem("sums_inv"), sem("normed")
        p_turned, pt_act, pt_dve = sem("p_turned"), sem("pt_act"), sem("pt_dve")
        pv_done, o_masked, o_summed, wo_done, x1_ready = sem("pv_done"), sem("o_masked"), sem("o_summed"), sem("wo_done"), sem("x1_ready")

        b = {n: sem("b_" + n) for n in (
            "xl", "turned", "xlT", "cqT", "kv", "q", "rr", "abs", "exp", "ln", "copied", "sp", "mc", "ms",
            "rot", "dup", "T", "xt_a", "xt_v", "s", "ss", "max", "sub", "se", "sum", "inv", "norm", "pt", "pv",
            "os", "o", "x2", "pe_ready", "kr", "ckv", "blocks")}
        c = {n: sem("c_" + n) for n in (
            "xe", "turned", "xeT", "xeH", "xeL", "logits", "tk", "pair", "comb", "combT", "ct", "cbm", "cb",
            "zero", "gate", "up", "silu", "hu", "hc", "hH", "hL", "down", "ys", "yT", "out", "w_hi", "w_lo")}
        stored, out_free = sem("stored"), sem("out_free")

        PAIRS = T // 2
        assert PAIRS == E

        def first_of(i, s):
            return 2 * i + s + 1

        def second_of(i, s):
            return 2 * i + s - 1

        LN_STEPS = 8

        def finish_norm(v, n):
            done = [LN_STEPS * n]

            def step(ins):
                ins.then_inc(ln_step, 1)
                done[0] += 1
                return done[0]

            half, dif, dev = lnt[:, 0, :], lnt[:, 1, :], lnt[:, 2, :]
            step(v.tensor_tensor(half, ST[:, :, 1], ST[:, :, 4], ALU.add))
            step(v.tensor_tensor(dif, ST[:, :, 1], ST[:, :, 4], ALU.subtract))
            n3 = step(v.tensor_tensor(dev, ST[:, :, 2], ST[:, :, 5], ALU.add))
            v.wait_ge(ln_step, n3)
            step(v.tensor_scalar(mean[:, :], half, 0.5, None, ALU.mult))
            step(v.scalar_tensor_tensor(out=lnt[:, 3, :], in0=dif, scalar=0.25, in1=dif, op0=ALU.mult, op1=ALU.mult))
            n6 = step(v.tensor_scalar(var[:, :], dev, 1.0 / D, EPS, ALU.mult, ALU.add))
            v.wait_ge(ln_step, n6)
            step(v.tensor_tensor(var[:, :], var[:, :], lnt[:, 3, :], ALU.add))
            v.wait_ge(std_ready, n + 1)
            n8 = step(v.reciprocal(rstd[:, :], std[:, :]))
            v.wait_ge(ln_step, n8)

        def root(a, n):
            a.wait_ge(ln_step, LN_STEPS * n + 7)
            a.activation(std[:, :], var[:, :], ACT.Sqrt).then_inc(std_ready, 1)

        block = held.enter_context(nc.Block())

        @block.sync
        def _(sp):
            sp.dma_start(small[:, 0, :], bc(raw_delta.unsqueeze(0), [128, 16])).then_inc(in_rot, 16)
            for dst, src in ((cpos, cos_pos), (spos, sin_pos), (BM, own_sequence)):
                sp.dma_start(dst[:, :], src).then_inc(in_rot, 16)
            for n in range(4):
                sp.dma_start(X[:, 4 * n:4 * n + 4, :], x[512 * n:512 * n + 512, :].rearrange("(t p) d -> p t d", p=128)).then_inc(in_x[n], 16)
            sp.dma_start(I128[:, :], ident).then_inc(in_ident, 16)
            for dst, src in ((WqS, wq), (WkS, wk), (WvS, wv), (WoS, wo), (HM, head_mask)):
                sp.dma_start(dst[:, :], src).then_inc(in_wqk, 16)
            sp.dma_start(boB[:, :], bc(bo.unsqueeze(0), [128, D])).then_inc(in_wqk, 16)

            def load_ctx(k, j):
                if not isinstance(k, int) or k >= 4:
                    sp.wait_ge(ctx_lo, k - 3)
                sp.dma_start(CR[:, j, :], ctxT[:, bass.ds(k * S, S)]).then_inc(in_ctx[j], 16)

            for j in range(4):
                load_ctx(j, j)
            for dst, src in ((uqT[:, :, :], w_uqT), (ukT[:, :, :], w_ukT), (uvT[:, :, :], w_uvT), (woutS, w_out)):
                sp.dma_start(dst, src).then_inc(in_attn, 16)
            sp.dma_start(WA[:, :, 1, :], w_qr).then_inc(wqr_in, 16)
            sp.dma_start(WkvS[:, :], w_kv).then_inc(in_attn, 16)
            sp.dma_start(WdqS[:, :], w_dq).then_inc(in_attn, 16)
            for j in range(4):
                load_ctx(4 + j, j)
            sp.dma_start(GW[:, :, :], w_gate).then_inc(in_moe, 16)
            sp.dma_start(UW[:, :, :], w_up).then_inc(in_moe, 16)
            sp.dma_start(DW[:, :, :], w_down).then_inc(in_moe, 16)
            sp.dma_start(wrT[:, :], w_router).then_inc(in_moe, 16)
            sp.dma_start(rank[:, :], expert_rank).then_inc(in_moe, 16)
            with sp.Fori(2, T) as i:
                for j in range(4):
                    load_ctx(4 * i + j, j)
            sp.wait_ge(x1_stats, 2 * T)
            sp.dma_start(SEL[:, :, :], expert_sel).then_inc(in_sel, 16)
            sp.sem_inc(out_free, 1)
            with sp.Fori(0, TB) as tb:
                sp.wait_ge(c["out"], 4 * tb + 4)
                sp.dma_start(out[bass.ds(tb * 512, 512), :].rearrange("(t p) d -> p t d", p=128), OUT[:, :, :]).then_inc(stored, 16)
                sp.wait_ge(stored, 16 * tb + 16)
                sp.sem_inc(out_free, 1)

        @block.gpsimd
        def _(g):
            g.memset(f(CHi[:, :, S:SP]), 0.0).then_inc(pad_set, 1)
            g.memset(f(CLo[:, :, S:SP]), 0.0).then_inc(pad_set, 1)
            g.memset(PR[:, :, :, S:SP], 0.0).then_inc(pad_set, 1)

            def split_context(k, j):
                g.tensor_copy(CHi[:, j, 0:S], CR[:, j, :]).then_inc(ctx_hi, 1)
                g.wait_ge(ctx_hi, k + 1)
                g.tensor_tensor(CLo[:, j, 0:S], CR[:, j, :], f(CHi[:, j, 0:S]), ALU.subtract).then_inc(ctx_lo, 1)

            def mask_queries(k, j):
                mask = bc(HM[:, :].unsqueeze(2), [128, G, L])
                g.tensor_tensor(QMH[:, j, :, :], bc(f(QH[:, bass.ds(k * L, L)]).unsqueeze(1), [128, G, L]), mask,
                                ALU.mult).then_inc(qm_hi, 1)
                g.tensor_tensor(QML[:, j, :, :], bc(f(QL[:, bass.ds(k * L, L)]).unsqueeze(1), [128, G, L]), mask,
                                ALU.mult).then_inc(qm_lo, 1)

            def prepare(i, j):
                k = 4 * i + j
                g.wait_ge(in_ctx[j], 16 * i + 16)
                g.wait_ge(v_proj, k - 3)
                g.wait_ge(scores, 4 * k - 12)
                mask_queries(k, j)
                split_context(k, j)

            def normalise(k, j):
                g.wait_ge(sums_inv, k + 1)
                for gr in range(2, G):
                    g.tensor_tensor(PR[:, j % 2, gr, 0:S], PR[:, j % 2, gr, 0:S], bc(rinv[:, gr:gr + 1], [128, S]),
                                    ALU.mult).then_inc(pool_normed, 1)

            for j in range(2):
                g.wait_ge(in_ctx[j], 16)
                split_context(j, j)
            g.wait_ge(in_wqk, 96)
            g.wait_ge(q_lo, 1)
            mask_queries(0, 0)
            for j in range(2, 4):
                g.wait_ge(in_ctx[j], 16)
                split_context(j, j)
            for j in range(1, 4):
                mask_queries(j, j)
            g.wait_ge(ln_out, T)
            for n in range(4):
                s = slice(4 * n, 4 * n + 4)
                g.tensor_tensor(X[:, s, :], X[:, s, :], bc(boB[:, :].unsqueeze(1), [128, 4, D]), ALU.add).then_inc(x_biased, 1)
            g.wait_ge(q_lo, 4)

            with g.Fori(1, T) as i:
                for j in range(4):
                    prepare(i, j)
                    normalise(4 * i - 4 + j, j)
            for j in range(4):
                normalise(B - 4 + j, j)
            g.wait_ge(in_sel, 16)
            g.tensor_copy(SELr[:, :, :], SEL[:, :, :]).then_inc(sel_ready, 1)

            def first_stage(i):
                for s in range(2):
                    w = first_of(i, s)
                    g.wait_ge(b["ckv"], w)
                    if counts(w - 2):
                        g.wait_ge(b["pv"], w - 2)
                    g.tensor_tensor(CKB[:, s, :, :], bc(TT[:, s, 8, 0, :].unsqueeze(1), [128, 4, 32]),
                                    bc(BM[:, :].unsqueeze(2), [128, 4, 32]), ALU.mult).then_inc(b["blocks"], 1)
                for s in range(2):
                    w = first_of(i, s)
                    g.wait_ge(b["sp"], w)
                    full = [128, 9, 2, 16]
                    g.tensor_tensor(MS[:, s, :, :, :], SPL[:, s, :, :, :], bc(sinT[:, :].unsqueeze(1).unsqueeze(1), full), ALU.mult).then_inc(b["ms"], 1)

            def split_part(e, n, hi, lo, w):
                g.tensor_copy(hi, w).then_inc(c["w_hi"], 1)
                g.wait_ge(c["w_hi"], PARTS * e + n)
                g.tensor_tensor(lo, w, f(hi), ALU.subtract).then_inc(c["w_lo"], 1)

            def split_expert(e):
                for n, (w, hi, lo) in enumerate(((GW, GH, GL), (UW, UH, UL), (DW, WH, WL))):
                    at = bass.ds(I * e, I)
                    flat = lambda ap: ap[:, :, :].rearrange("p u d -> p (u d)")[:, at]
                    split_part(e, n + 1, flat(hi), flat(lo), flat(w))

            g.wait_ge(in_rot, 64)
            g.wait_ge(in_moe, 16 * 5)
            first_stage(0)
            split_expert(0)
            with g.Fori(1, PAIRS) as i:
                first_stage(i)
                split_expert(i)

            def weighted(tb, n):
                q = run_of(n)
                at = U * tb + n
                g.wait_ge(c["cb"], Q * tb + q + 1)
                g.wait_ge(c["hu"], at + 1)
                if counts(at - 1):
                    g.wait_ge(c["hL"], at - 1)
                g.tensor_tensor(hc[:, n % 2, :], hu[:, n % 2, :], CB[:, q % 2, :], ALU.mult).then_inc(c["hc"], 1)

            g.wait_ge(b["x2"], T)
            g.memset(comb[:, :, 2 * E:32], 0.0).then_inc(c["zero"], 1)
            for n in range(U):
                weighted(0, n)
            with g.Fori(1, TB) as tb:
                for n in range(U):
                    weighted(tb, n)

        @block.scalar
        def _(a):
            a.wait_ge(in_rot, 64)
            a.activation(small[:, 1, :], small[:, 0, :], ACT.Exp, scale=-1.0).then_inc(rot_act, 1)
            a.wait_ge(rot_step, 5)
            a.activation(small[:, 3, :], small[:, 2, :], ACT.Sin).then_inc(rot_act, 1)
            a.activation(small[:, 5, :], small[:, 4, :], ACT.Sin).then_inc(rot_act, 1)
            a.wait_ge(in_wqk, 96)
            a.activation(WkH[:, :], WkS[:, :], ACT.Copy).then_inc(w_split, 1)
            a.activation(WvH[:, :], WvS[:, :], ACT.Copy).then_inc(w_split, 1)
            root(a, 0)

            def normed_out(n):
                a.wait_ge(ln_turned, n + 1)
                a.activation(XLT[:, 512 * n:512 * n + 512], bank[n][:, :], ACT.Copy).then_inc(ln_copied, 1)

            def scale_queries(n):
                a.wait_ge(q_ready, n + 1)
                a.activation(XL[:, 4 * n:4 * n + 4, :].rearrange("p t d -> p (t d)"), bank[n][:, :], ACT.Copy,
                             scale=XD ** -0.5).then_inc(q_scaled, 1)

            normed_out(0)
            for n in range(1, 4):
                normed_out(n)
                scale_queries(n - 1)
            scale_queries(3)

            def k_high(k, j):
                a.wait_ge(k_proj, k + 1)
                if counts(4 * k - 4):
                    a.wait_ge(scores, 4 * k - 4)
                a.activation(KH[:, j % 2, :], bank[7][:, 0:SP], ACT.Copy).then_inc(k_hi, 1)

            def v_copy(k, j):
                a.wait_ge(v_proj, k + 1)
                if counts(k - 3):
                    a.wait_ge(pv_done, k - 3)
                a.activation(V[:, j, :, :], PS[0:KC, 0:3, 384:512], ACT.Copy).then_inc(v_copied, 1)

            def exps(k, j):
                if counts(3 * k - 3):
                    a.wait_ge(p_turned, 3 * k - 3)
                for gr in range(G):
                    a.wait_ge(max_ready, 4 * k + gr + 1)
                    if gr == 0:
                        if counts(k):
                            a.wait_ge(sums_inv, k)
                    a.activation(PR[:, j % 2, gr, 0:S], bank[gr][:, 0:S], ACT.Exp, bias=nmax[:, gr:gr + 1],
                                 accum_out=rsum[:, gr:gr + 1]).then_inc(exped, 1)

            def turned_copy(k, ch):
                a.wait_ge(p_turned, 3 * k + ch + 1)
                if counts(k):
                    a.wait_ge(pv_done, k)
                a.activation(PT[:, ch, :], bank[4 + ch][0:KC, :], ACT.Copy).then_inc(pt_act, 1)

            def step(k, j, last=False):
                if not isinstance(k, int) or k >= 1:
                    turned_copy(k - 1, 2)
                if not last or k + 1 < B:
                    exps(k + 1, j + 1)
                turned_copy(k, 0)
                if not last or k + 2 < B:
                    v_copy(k + 2, (j + 2) % 4)
                if not last or k + 3 < B:
                    k_high(k + 3, j + 3)

            for k in range(2):
                k_high(k, k)
                v_copy(k, k)
            exps(0, 0)
            k_high(2, 2)
            for k in range(4):
                step(k, k)
            with a.Fori(1, T - 1) as i:
                for j in range(4):
                    step(4 * i + j, j)
            for k in range(B - 4, B):
                step(k, k % 4, True)
            turned_copy(B - 1, 2)

            root(a, 1)

            def normed_turned(i):
                for s in range(2):
                    a.wait_ge(b["turned"], first_of(i, s))
                    a.activation(xlT[:, s, :], bank[s][:, 0:128], ACT.Copy).then_inc(b["xlT"], 1)

            def softmax_exp(i):
                for s in range(2):
                    a.wait_ge(b["sub"], second_of(i, s))
                    a.activation(SE[:, s, :, :], SD[:, s, :, :], ACT.Exp, scale=(DH + DR) ** -0.5).then_inc(b["se"], 1)

            def softplus_exp(i):
                for s in range(2):
                    w = first_of(i, s)
                    q = bank[2 + s][:, :].rearrange("p (h c d) -> p h c d", c=2, d=32)
                    a.wait_ge(b["q"], w)
                    a.activation(RR[:, s, 0:8, :], q[:, :, 1, :], ACT.Copy).then_inc(b["rr"], 1)
                    a.wait_ge(b["rr"], w)
                    a.wait_ge(b["kr"], w)
                    a.activation(AB[:, s, :, :], RR[:, s, :, :], ACT.Abs).then_inc(b["abs"], 1)
                    a.wait_ge(b["abs"], w)
                    a.activation(EX[:, s, :, :], AB[:, s, :, :], ACT.Exp, scale=-1.0).then_inc(b["exp"], 1)

            def softplus_log(i):
                for s in range(2):
                    w = first_of(i, s)
                    a.wait_ge(b["exp"], w)
                    a.activation(LG[:, s, :, :], EX[:, s, :, :], ACT.Ln, bias=1.0).then_inc(b["ln"], 1)
                for s in range(2):
                    q = bank[2 + s][:, :].rearrange("p (h c d) -> p h c d", c=2, d=32)
                    a.activation(TT[:, s, 0:8, 0, :], q[:, :, 0, :], ACT.Copy).then_inc(b["copied"], 1)

            def rotated(i):
                for s in range(2):
                    a.wait_ge(b["T"], first_of(i, s))
                    a.activation(XT[:, s, 0:4, :].rearrange("p a n -> p (a n)"), bank[2 + s][:, :], ACT.Copy).then_inc(b["xt_a"], 1)

            def step(i, before=True, after=True):
                if before:
                    softmax_exp(i)
                softplus_exp(i)
                if after:
                    normed_turned(i + 1)
                softplus_log(i)
                rotated(i)

            normed_turned(0)
            step(0, before=False)
            with a.Fori(1, PAIRS - 1) as i:
                step(i)
            step(PAIRS - 1, after=False)
            softmax_exp(PAIRS)

            root(a, 2)
            def whole(n):
                a.wait_ge(c["turned"], n + 1)
                a.activation(xeT[:, 512 * n:512 * n + 512], bank[n][:, :], ACT.Copy).then_inc(c["xeT"], 1)

            def upper(n):
                a.activation(xeH[:, 512 * n:512 * n + 512], bank[n][:, :], ACT.Copy).then_inc(c["xeH"], 1)

            whole(0)
            upper(0)
            for n in range(1, 4):
                whole(n)
                if n > 1:
                    upper(n - 1)
            upper(3)
            a.wait_ge(c["tk"], 11)
            a.activation(tm[:, 6, :], tm[:, 4, :], ACT.Sigmoid).then_inc(c["pair"], 1)
            a.activation(tm[:, 7, :], tm[:, 4, :], ACT.Sigmoid, scale=-1.0).then_inc(c["pair"], 1)

            def gated(tb, n):
                at = U * tb + n
                a.wait_ge(c["gate"], at + 1)
                if counts(at - 1):
                    a.wait_ge(c["hu"], at - 1)
                a.activation(sg[:, n % 2, :], bank[n % 2][:, :], ACT.Silu).then_inc(c["silu"], 1)

            def spread(tb, q):
                a.wait_ge(c["cbm"], Q * tb + q + 1)
                used = U * tb + (STARTS[q - 1] if q else STARTS[Q - 1] - U)
                if counts(used):
                    a.wait_ge(c["hc"], used)
                a.activation(CB[:, q % 2, :], bank[7][:, :], ACT.Copy).then_inc(c["cb"], 1)

            def hidden_high(tb, n):
                at = U * tb + n
                o = (n - 2) % U
                a.wait_ge(c["hc"], at - 1)
                if counts(at - 5):
                    a.wait_ge(c["down"], at - 5)
                a.activation(hH[:, slot(o), :], hc[:, o % 2, :], ACT.Copy).then_inc(c["hH"], 1)

            def summed(tb):
                a.wait_ge(c["down"], U * tb)
                a.activation(YS[:, :], bank[6][:, :], ACT.Copy).then_inc(c["ys"], 1)

            def block_of(tb, first=False):
                for n in range(U):
                    if n in STARTS and not (first and n == 0):
                        spread(tb, run_of(n))
                    gated(tb, n)
                    if n == 3 and not first:
                        summed(tb)
                    if first and n in (1, 2):
                        for m in (2 * n - 2, 2 * n - 1):
                            a.wait_ge(c["combT"], m + 1)
                            a.activation(CT[:, 512 * m:512 * m + 512], bank[4 + m % 2][0:32, :], ACT.Copy).then_inc(c["ct"], 1)
                        if n == 1:
                            spread(tb, 0)
                    if n >= 2 or not first:
                        hidden_high(tb, n)

            block_of(0, True)
            with a.Fori(1, TB) as tb:
                block_of(tb)
            for n in range(2):
                hidden_high(TB, n)
            summed(TB)

        @block.vector
        def _(v):
            v.wait_ge(in_rot, 64)
            v.wait_ge(rot_act, 1)
            sm = lambda n: small[:, n, :]
            v.tensor_scalar(sm(1), sm(1), 1.0, None, ALU.add).then_inc(rot_step, 1)
            v.wait_ge(rot_step, 1)
            v.reciprocal(sm(2), sm(1)).then_inc(rot_step, 1)
            v.wait_ge(rot_step, 2)
            v.tensor_scalar(sm(2), sm(2), -math.pi, math.pi / 2, ALU.mult, ALU.add).then_inc(rot_step, 1)
            v.wait_ge(rot_step, 3)
            v.scalar_tensor_tensor(out=sm(4), in0=sm(2), scalar=-1.0, in1=sm(2), op0=ALU.mult, op1=ALU.max).then_inc(rot_step, 1)
            v.wait_ge(rot_step, 4)
            v.tensor_scalar(sm(4), sm(4), -1.0, math.pi / 2, ALU.mult, ALU.add).then_inc(rot_step, 1)
            v.wait_ge(rot_act, 3)
            v.scalar_tensor_tensor(out=sm(1), in0=sm(3), scalar=-2.0, in1=sm(5), op0=ALU.mult, op1=ALU.mult).then_inc(rot_step, 1)
            v.scalar_tensor_tensor(out=sm(2), in0=sm(3), scalar=2.0, in1=sm(3), op0=ALU.mult, op1=ALU.mult).then_inc(rot_step, 1)
            v.wait_ge(rot_step, 7)
            v.tensor_scalar(sm(2), sm(2), 1.0, None, ALU.subtract).then_inc(rot_step, 1)
            v.wait_ge(rot_step, 8)
            v.tensor_tensor(cosT[:, :], cpos[:, :], sm(2), ALU.mult).then_inc(rot_step, 1)
            v.tensor_tensor(sm(0), spos[:, :], sm(1), ALU.mult).then_inc(rot_step, 1)
            v.tensor_tensor(sinT[:, :], spos[:, :], sm(2), ALU.mult).then_inc(rot_step, 1)
            v.tensor_tensor(sm(3), cpos[:, :], sm(1), ALU.mult).then_inc(rot_step, 1)
            v.wait_ge(rot_step, 12)
            v.tensor_tensor(cosT[:, :], cosT[:, :], sm(0), ALU.subtract).then_inc(rot_step, 1)
            v.tensor_tensor(sinT[:, :], sinT[:, :], sm(3), ALU.add).then_inc(rot_step, 1)
            for t in range(T):
                if t % 4 == 0:
                    v.wait_ge(in_x[t // 4], 16)
                v.bn_stats(ST[:, t, :], X[:, t, :]).then_inc(x1_stats, 1)
            v.wait_ge(x1_stats, T)
            finish_norm(v, 0)
            for t in range(T):
                v.tensor_scalar(XL[:, t, :], X[:, t, :], mean[:, t:t + 1], rstd[:, t:t + 1], ALU.subtract, ALU.mult).then_inc(ln_out, 1)
            v.wait_ge(w_split, 2)
            v.tensor_tensor(WkL[:, :], WkS[:, :], f(WkH[:, :]), ALU.subtract).then_inc(w_split, 1)
            v.tensor_tensor(WvL[:, :], WvS[:, :], f(WvH[:, :]), ALU.subtract).then_inc(w_split, 1)
            for n in range(4):
                v.wait_ge(q_scaled, n + 1)
                qs = XL[:, 4 * n:4 * n + 4, :].rearrange("p t d -> p (t d)")
                v.tensor_copy(QH[:, 512 * n:512 * n + 512], qs).then_inc(q_hi, 1)
                v.wait_ge(q_hi, n + 1)
                v.tensor_tensor(QL[:, 512 * n:512 * n + 512], qs, f(QH[:, 512 * n:512 * n + 512]), ALU.subtract).then_inc(q_lo, 1)

            def k_low(k, j):
                v.wait_ge(k_hi, k + 1)
                v.tensor_tensor(KL[:, j % 2, :], bank[7][:, 0:SP], f(KH[:, j % 2, :]), ALU.subtract).then_inc(k_lo, 1)

            def maxima(k):
                if counts(4 * k):
                    v.wait_ge(exped, 4 * k)
                for gr in range(G):
                    v.wait_ge(scores, 4 * k + gr + 1)
                    v.tensor_reduce(nmax[:, gr:gr + 1], bank[gr][:, 0:S], AX.X, ALU.max, negate=True).then_inc(max_ready, 1)

            def normalise(k, j):
                v.wait_ge(exped, 4 * k + 4)
                if counts(2 * k):
                    v.wait_ge(pool_normed, 2 * k)
                v.reciprocal(rinv[:, :], rsum[:, :]).then_inc(sums_inv, 1)
                v.wait_ge(sums_inv, k + 1)
                for gr in range(2):
                    v.tensor_scalar(PR[:, j % 2, gr, 0:S], PR[:, j % 2, gr, 0:S], rinv[:, gr:gr + 1], None,
                                    ALU.mult).then_inc(normed, 1)

            def turned_copy(k):
                v.wait_ge(p_turned, 3 * k + 2)
                if counts(k):
                    v.wait_ge(pv_done, k)
                v.tensor_copy(PT[:, 1, :], bank[5][0:KC, :]).then_inc(pt_dve, 1)

            def own_blocks(k, j, unit):
                v.wait_ge(pv_done, k + 1)
                if counts(k):
                    v.wait_ge(o_summed, k)
                o = bank[7][:, 384:512].rearrange("p (h q) -> p h q", h=G)
                v.tensor_tensor(OM[:, :, :], o, bc(HM[:, :].unsqueeze(2), [128, G, L]), ALU.mult).then_inc(o_masked, 1)
                v.wait_ge(o_masked, k + 1)
                if j == 0:
                    if counts(unit):
                        v.wait_ge(wo_done, unit)
                v.tensor_reduce(OT[:, L * j:L * j + L], OM[:, :, :].rearrange("p h q -> p q h"), AX.X, ALU.add).then_inc(o_summed, 1)

            def residual(unit):
                v.wait_ge(wo_done, unit + 1)
                xt = X[:, bass.ds(unit, 1), :].rearrange("p t d -> p (t d)")
                v.tensor_tensor(xt, bank[3][:, 384:512], xt, ALU.add).then_inc(x1_ready, 1)
                v.wait_ge(x1_ready, unit + 1)
                v.bn_stats(ST[:, bass.ds(unit, 1), :].rearrange("p t s -> p (t s)"), xt).then_inc(x1_stats, 1)

            def step(k, j, unit, last=False):
                if not last or k + 1 < B:
                    maxima(k + 1)
                if not isinstance(k, int) or k >= 1:
                    own_blocks(k - 1, (j - 1) % 4, unit - (j == 0))
                if not last or k + 1 < B:
                    normalise(k + 1, j + 1)
                turned_copy(k)
                if j == 0 and (not isinstance(unit, int) or unit >= 1):
                    residual(unit - 1)
                if not last or k + 3 < B:
                    k_low(k + 3, j + 3)

            k_low(0, 0)
            k_low(1, 1)
            maxima(0)
            v.wait_ge(absorbed, 1)
            v.tensor_copy(WA[:, :, 0, :], bank[5][0:CQ, 0:NH * 32].rearrange("p (h d) -> p h d", h=NH)).then_inc(absorbed_out, 1)
            v.wait_ge(absorbed, 2)
            v.tensor_copy(Wvo[:, :, :].rearrange("p r n -> p (r n)"), bank[6][:, 0:256]).then_inc(absorbed_out, 1)
            normalise(0, 0)
            k_low(2, 2)
            v.wait_ge(x_biased, 4)
            for k in range(4):
                step(k, k, 0)
            with v.Fori(1, T - 1) as i:
                for j in range(4):
                    step(4 * i + j, j, i)
            for k in range(B - 4, B):
                step(k, k % 4, T - 1, True)
            own_blocks(B - 1, 3, T - 1)
            residual(T - 1)

            v.wait_ge(x1_stats, 2 * T)
            finish_norm(v, 1)

            def normed_tiles(i):
                for s in range(2):
                    t = 2 * i + s
                    v.tensor_scalar(xl[:, s, :], X[:, bass.ds(t, 1), :].rearrange("p t d -> p (t d)"),
                                    mean[:, bass.ds(t, 1)], rstd[:, bass.ds(t, 1)], ALU.subtract, ALU.mult).then_inc(b["xl"], 1)

            def centred_scores(i):
                for s in range(2):
                    w = second_of(i, s)
                    v.wait_ge(b["s"], w)
                    for r in range(2):
                        v.transpose(SS[:, s, 4 * r:4 * r + 4, :].rearrange("p h k -> p (h k)"), bank[4 + 2 * r + s][:, 0:128]).then_inc(b["ss"], 1)
                    v.wait_ge(b["ss"], 2 * w)
                    v.tensor_reduce(nm8[:, s, :], SS[:, s, :, :], AX.X, ALU.max).then_inc(b["max"], 1)
                    v.wait_ge(b["max"], w)
                    v.tensor_tensor(SD[:, s, :, :], SS[:, s, :, :], bc(nm8[:, s, :].unsqueeze(2), [128, 8, 32]), ALU.subtract).then_inc(b["sub"], 1)

            def compressed(i):
                for s in range(2):
                    v.wait_ge(b["kv"], first_of(i, s))
                    v.tensor_copy(cqT[:, s, :], bank[s][0:CQ, 128:256]).then_inc(b["cqT"], 1)

            def keys_and_values(i):
                for s in range(2):
                    v.tensor_copy(RR[:, s, 8, :], bank[s][:, 256 + CKV:256 + CKV + DR]).then_inc(b["kr"], 1)
                    v.tensor_copy(TT[:, s, 8:10, 0, :], bc(bank[s][:, 256:256 + CKV].unsqueeze(1), [128, 2, 32])).then_inc(b["ckv"], 1)

            def probabilities(i):
                for s in range(2):
                    w = second_of(i, s)
                    v.wait_ge(b["se"], w)
                    v.tensor_reduce(s8[:, s, :], SE[:, s, :, :], AX.X, ALU.add).then_inc(b["sum"], 1)
                    v.wait_ge(b["sum"], w)
                    v.reciprocal(r8[:, s, :], s8[:, s, :]).then_inc(b["inv"], 1)
                    v.wait_ge(b["inv"], w)
                    v.tensor_tensor(SN[:, s, :, :], SE[:, s, :, :], bc(r8[:, s, :].unsqueeze(2), [128, 8, 32]), ALU.mult).then_inc(b["norm"], 1)
                    v.wait_ge(b["norm"], w)
                    v.transpose(PTb[:, s, :, :].rearrange("p h k -> p (h k)"), SN[:, s, :, :].rearrange("p h k -> p (h k)")).then_inc(b["pt"], 1)

            def weighted_turned(i):
                for s in range(2):
                    v.wait_ge(b["pv"], second_of(i, s))
                    v.transpose(OS[:, s, :, :].rearrange("p r n -> p (r n)"), bank[4 + s][:, 256:512]).then_inc(b["os"], 1)

            def rotate(i):
                for s in range(2):
                    w = first_of(i, s)
                    v.wait_ge(b["ln"], w)
                    v.scalar_tensor_tensor(out=SPL[:, s, :, :, :].rearrange("p h a d -> p h (a d)"), in0=RR[:, s, :, :], scalar=0.0,
                                           in1=LG[:, s, :, :], op0=ALU.max, op1=ALU.add).then_inc(b["sp"], 1)
                for s in range(2):
                    v.wait_ge(b["sp"], first_of(i, s))
                    full = [128, 9, 2, 16]
                    v.tensor_tensor(MC[:, s, :, :, :], SPL[:, s, :, :, :], bc(cosT[:, :].unsqueeze(1).unsqueeze(1), full), ALU.mult).then_inc(b["mc"], 1)
                for s in range(2):
                    w = first_of(i, s)
                    v.wait_ge(b["mc"], w)
                    v.wait_ge(b["ms"], w)
                    v.tensor_tensor(TT[:, s, 0:9, 1, 0:16], MC[:, s, :, 0, :], MS[:, s, :, 1, :], ALU.subtract).then_inc(b["rot"], 1)
                    v.tensor_tensor(TT[:, s, 0:9, 1, 16:32], MS[:, s, :, 0, :], MC[:, s, :, 1, :], ALU.add).then_inc(b["rot"], 1)
                    v.wait_ge(b["rot"], 2 * w)
                    v.tensor_copy(TT[:, s, 9, 1, :], TT[:, s, 8, 1, :]).then_inc(b["dup"], 1)

            def residual2(i):
                for s in range(2):
                    v.wait_ge(b["o"], second_of(i, s))
                    xt = X[:, bass.ds(2 * i + s - 2, 1), :].rearrange("p t d -> p (t d)")
                    v.tensor_tensor(xt, bank[6 + s][:, 128:256], xt, ALU.add).then_inc(b["x2"], 1)
                for s in range(2):
                    v.wait_ge(b["x2"], second_of(i, s))
                    xt = X[:, bass.ds(2 * i + s - 2, 1), :].rearrange("p t d -> p (t d)")
                    v.bn_stats(ST[:, bass.ds(2 * i + s - 2, 1), :].rearrange("p t s -> p (t s)"), xt).then_inc(x2_stats, 1)

            def rotated_keys(i):
                for s in range(2):
                    v.wait_ge(b["T"], first_of(i, s))
                    v.tensor_copy(XT[:, s, 4, :], bank[4 + s][:, 128:256]).then_inc(b["xt_v"], 1)

            def step(i, before=True, after=True):
                keys_and_values(i)
                if after:
                    normed_tiles(i + 1)
                if before:
                    centred_scores(i)
                    probabilities(i)
                if before:
                    weighted_turned(i)
                rotate(i)
                if after:
                    compressed(i + 1)
                if before:
                    residual2(i)
                rotated_keys(i)

            normed_tiles(0)
            compressed(0)
            step(0, before=False)
            with v.Fori(1, PAIRS - 1) as i:
                step(i)
            step(PAIRS - 1, after=False)
            centred_scores(PAIRS)
            probabilities(PAIRS)
            weighted_turned(PAIRS)
            residual2(PAIRS)

            v.wait_ge(x2_stats, T)
            finish_norm(v, 2)
            for t in range(T):
                v.tensor_scalar(xe[:, t, :], X[:, t, :], mean[:, t:t + 1], rstd[:, t:t + 1], ALU.subtract, ALU.mult).then_inc(c["xe"], 1)
            for n in range(4):
                s = slice(512 * n, 512 * n + 512)
                v.wait_ge(c["xeH"], n + 1)
                v.tensor_tensor(xeL[:, s], bank[n][:, :], f(xeH[:, s]), ALU.subtract).then_inc(c["xeL"], 1)
            n = [0]

            def did(ins):
                n[0] += 1
                ins.then_inc(c["tk"], 1)
                return n[0]

            def small_step(ins):
                v.wait_ge(c["tk"], did(ins))

            lg = bank[4][:, 0:T * E].rearrange("p (t e) -> p t e", t=T)
            rk = bc(rank[:, :].unsqueeze(1), [128, T, E])
            wide = lambda ap: bc(ap.unsqueeze(2), [128, T, E])
            K = lambda m: tk[:, m, :, :]
            v.wait_ge(c["logits"], 4)
            small_step(v.tensor_reduce(tm[:, 0, :], lg, AX.X, ALU.max))
            small_step(v.tensor_tensor(K(0), lg, wide(tm[:, 0, :]), ALU.is_equal))
            small_step(v.tensor_tensor(K(1), K(0), rk, ALU.mult))
            small_step(v.tensor_reduce(tm[:, 1, :], K(1), AX.X, ALU.max))
            small_step(v.tensor_tensor(K(2), K(1), wide(tm[:, 1, :]), ALU.is_equal))
            small_step(v.scalar_tensor_tensor(out=K(3), in0=K(2), scalar=-BIG, in1=lg, op0=ALU.mult, op1=ALU.add))
            small_step(v.tensor_reduce(tm[:, 2, :], K(3), AX.X, ALU.max))
            small_step(v.tensor_tensor(K(4), K(3), wide(tm[:, 2, :]), ALU.is_equal))
            small_step(v.tensor_tensor(K(5), K(4), rk, ALU.mult))
            small_step(v.tensor_reduce(tm[:, 3, :], K(5), AX.X, ALU.max))
            did(v.tensor_tensor(tm[:, 4, :], tm[:, 2, :], tm[:, 0, :], ALU.subtract))
            small_step(v.tensor_tensor(K(6), K(5), wide(tm[:, 3, :]), ALU.is_equal))
            m = [0]

            def comb_step(ins):
                m[0] += 1
                ins.then_inc(c["comb"], 1)
                v.wait_ge(c["comb"], m[0])

            v.wait_ge(c["pair"], 2)
            comb_step(v.tensor_tensor(K(7), K(2), wide(tm[:, 7, :]), ALU.mult))
            comb_step(v.tensor_tensor(K(8), K(6), wide(tm[:, 6, :]), ALU.mult))
            comb_step(v.tensor_tensor(K(9), K(7), K(8), ALU.add))
            comb_step(v.tensor_copy(cHi[:, :, :], K(9)))
            v.tensor_copy(comb[:, :, 0:E], f(cHi[:, :, :])).then_inc(c["xeL"], 1)
            comb_step(v.tensor_tensor(comb[:, :, E:2 * E], K(9), f(cHi[:, :, :]), ALU.subtract))

            def multiplied(tb, n):
                at = U * tb + n
                v.wait_ge(c["silu"], at + 1)
                v.wait_ge(c["up"], at + 1)
                if counts(at - 1):
                    v.wait_ge(c["hc"], at - 1)
                v.tensor_tensor(hu[:, n % 2, :], bank[2 + n % 2][:, :], sg[:, n % 2, :], ALU.mult).then_inc(c["hu"], 1)

            def hidden_low(tb, n):
                at = U * tb + n
                o = (n - 2) % U
                v.wait_ge(c["hH"], at - 1)
                v.tensor_tensor(hL[:, slot(o), :], hc[:, o % 2, :], f(hH[:, slot(o), :]), ALU.subtract).then_inc(c["hL"], 1)

            def result(tb):
                v.wait_ge(c["yT"], tb)
                v.wait_ge(out_free, tb)
                for n in range(4):
                    v.tensor_tensor(OUT[:, n, :], bank[5][:, 128 * n:128 * n + 128],
                                    X[:, bass.ds(4 * (tb - 1) + n, 1), :].rearrange("p t d -> p (t d)"), ALU.add).then_inc(c["out"], 1)

            for n in range(U):
                multiplied(0, n)
                if n >= 2:
                    hidden_low(0, n)
            with v.Fori(1, TB) as tb:
                for n in range(U):
                    multiplied(tb, n)
                    hidden_low(tb, n)
                    if n == 8:
                        result(tb)
            for n in range(2):
                hidden_low(TB, n)
            result(TB)

        @block.tensor
        def _(t):
            t.wait_ge(in_ident, 16)

            def turn_x(n):
                for m in range(4):
                    t.wait_ge(ln_out, 4 * n + m + 1)
                    ins = t.transpose(bank[n][:, 128 * m:128 * m + 128], XL[:, 4 * n + m, :], I128[:, :])
                ins.then_inc(ln_turned, 1)

            def project_queries(n):
                t.wait_ge(ln_copied, n + 1)
                t.matmul(bank[n][:, :], WqS[:, :], XLT[:, 512 * n:512 * n + 512], start=True, stop=True).then_inc(q_ready, 1)

            turn_x(0)
            t.wait_ge(in_wqk, 96)
            for n in range(1, 4):
                turn_x(n)
                project_queries(n - 1)
            project_queries(3)

            def absorb():
                t.wait_ge(in_attn, 16 * 6)
                for h in range(NH):
                    ins = t.matmul(bank[5][0:CQ, 32 * h:32 * h + 32], uqT[:, h, :], ukT[:, h, :], start=True, stop=True)
                ins.then_inc(absorbed, 1)
                for h in range(NH):
                    hp, r = h // 2, h % 2
                    ins = t.matmul(bank[6][32 * hp:32 * hp + 32, 128 * r:128 * r + 128], uvT[:, h, :], woutS[:, h, :], start=True, stop=True)
                ins.then_inc(absorbed, 1)

            def project_keys(k, j):
                t.wait_ge(ctx_lo, k + 1)
                if counts(k):
                    t.wait_ge(k_lo, k)
                if counts(k - 3):
                    t.wait_ge(o_masked, k - 3)
                hi, lo = CHi[:, j, :], CLo[:, j, :]
                for n, (w, c_) in enumerate(((WkH, hi), (WkL, hi), (WkH, lo))):
                    ins = t.matmul(bank[7][:, 0:SP], w[:, :], c_, start=(n == 0), stop=(n == 2))
                ins.then_inc(k_proj, 1)

            def project_values(k, j, scored=True):
                hi, lo = CHi[:, j, :], CLo[:, j, :]
                if counts(k):
                    t.wait_ge(v_copied, k)
                for ch in range(3):
                    s = slice(KC * ch, KC * ch + KC)
                    if scored:
                        t.wait_ge(exped, 4 * k - 3 + ch)
                    for n, (w, c_) in enumerate(((WvH, hi), (WvL, hi), (WvH, lo))):
                        ins = t.matmul(bank[ch][0:KC, 384:512], c_[:, s], w[:, :], start=(n == 0), stop=(n == 2))
                ins.then_inc(v_proj, 1)

            def score(k, j, done=0):
                t.wait_ge(qm_lo, k + 1)
                t.wait_ge(k_lo, k + 1)
                t.wait_ge(v_copied, 2 if isinstance(k, int) and k == 0 else k + 1)
                for gr in range(G):
                    rows = slice(32 * gr, 32 * gr + 32)
                    if isinstance(k, int) and k == 1 and gr == 0:
                        t.wait_ge(exped, 4)
                    if gr == 3 and counts(done):
                        t.wait_ge(x1_ready, done)
                    qh, ql = (q[rows, j % 4, :, :].rearrange("p h q -> p (h q)") for q in (QMH, QML))
                    kh, kl = KH[rows, j % 2, :], KL[rows, j % 2, :]
                    for n, (q, kk) in enumerate(((qh, kh), (ql, kh), (qh, kl))):
                        ins = t.matmul(bank[gr][:, 0:SP], q, kk, start=(n == 0), stop=(n == 2))
                    ins.then_inc(scores, 1)

            def turn(k, j, ch):
                if ch == 1:
                    if counts(k):
                        t.wait_ge(pt_dve, k)
                else:
                    if counts(2 * k - 1 + ch // 2):
                        t.wait_ge(pt_act, 2 * k - 1 + ch // 2)
                for gr in range(G):
                    if ch == 0 and gr % 2 == 0:
                        if gr == 0:
                            t.wait_ge(normed, 2 * k + 2)
                        else:
                            t.wait_ge(pool_normed, 2 * k + 2)
                    ins = t.transpose(bank[4 + ch][0:KC, 128 * gr:128 * gr + 128],
                                      PR[:, j % 2, gr, KC * ch:KC * ch + KC], I128[:, :])
                ins.then_inc(p_turned, 1)

            def weigh(k, j):
                t.wait_ge(k_lo, min(k + 4, B) if isinstance(k, int) else k + 4)
                if counts(k):
                    t.wait_ge(o_masked, k)
                for ch in range(3):
                    if ch == 1:
                        t.wait_ge(pt_dve, k + 1)
                    else:
                        t.wait_ge(pt_act, 2 * k + 1 + ch // 2)
                    for gr in range(G):
                        ins = t.matmul(bank[7][32 * gr:32 * gr + 32, 384:512], V[:, j, ch, 32 * gr:32 * gr + 32],
                                       PT[:, ch, 128 * gr:128 * gr + 128], start=(ch == 0), stop=(ch == 2))
                ins.then_inc(pv_done, 1)

            def project_out(unit):
                t.wait_ge(o_summed, 4 * unit + 4)
                t.wait_ge(exped, min(16 * unit + 24, 4 * B) if isinstance(unit, int) else 16 * unit + 24)
                t.matmul(bank[3][:, 384:512], OT[:, :], WoS[:, :], start=True, stop=True).then_inc(wo_done, 1)

            def step(k, j, unit, last=False):
                if not last or k + 1 < B:
                    score(k + 1, j + 1, done=unit if j == 1 else 0)
                if not isinstance(k, int) or k >= 1:
                    weigh(k - 1, (j - 1) % 4)
                turn(k, j, 0)
                turn(k, j, 1)
                if not last or k + 2 < B:
                    project_values(k + 2, (j + 2) % 4)
                if not last or k + 3 < B:
                    project_keys(k + 3, (j + 3) % 4)
                turn(k, j, 2)
                if j == 0 and (not isinstance(unit, int) or unit >= 1):
                    project_out(unit - 1)

            t.wait_ge(w_split, 4)
            t.wait_ge(pad_set, 3)
            for k in range(2):
                project_keys(k, k)
                if k == 0:
                    t.wait_ge(q_scaled, 4)
                project_values(k, k, False)
            score(0, 0)
            project_keys(2, 2)
            absorb()
            for k in range(4):
                if k == 0:
                    t.wait_ge(absorbed_out, 2)
                step(k, k, 0)
            with t.Fori(1, T - 1) as i:
                for j in range(4):
                    step(4 * i + j, j, i)
            for k in range(B - 4, B):
                step(k, k % 4, T - 1, True)
            weigh(B - 1, 3)
            project_out(T - 1)

            t.wait_ge(wqr_in, 16)
            t.wait_ge(x1_ready, T)

            def turn_normed(i):
                for s in range(2):
                    t.wait_ge(b["xl"], first_of(i, s))
                    t.transpose(bank[s][:, 0:128], xl[:, s, :], I128[:, :]).then_inc(b["turned"], 1)

            def latent_scores(i):
                for s in range(2):
                    w = second_of(i, s)
                    t.wait_ge(b["xt_a"], w)
                    t.wait_ge(b["xt_v"], w)
                    t.sem_inc(b["pe_ready"], 1)
                    for j in range(4):
                        for r in range(2):
                            rows, q = slice(64 * r, 64 * r + 64), slice(32 * j, 32 * j + 32)
                            ins = t.matmul(bank[4 + 2 * r + s][32 * j:32 * j + 32, 0:128],
                                           XT[rows, s, 4, q], XT[rows, s, 0:4, q], start=True, stop=True)
                    ins.then_inc(b["s"], 1)

            def compress(i):
                for s in range(2):
                    t.wait_ge(b["xlT"], first_of(i, s))
                    t.matmul(bank[s][0:CQ, 128:256], WdqS[:, :], xlT[:, s, :], start=True, stop=True)
                    t.matmul(bank[s][:, 256:256 + CKV + DR], xlT[:, s, :], WkvS[:, :], start=True, stop=True).then_inc(b["kv"], 1)

            def queries(i):
                for s in range(2):
                    t.wait_ge(b["cqT"], first_of(i, s))
                    t.matmul(bank[2 + s][:, :], cqT[:, s, :], WA[:, :, :, :].rearrange("p h c d -> p (h c d)"),
                             start=True, stop=True).then_inc(b["q"], 1)

            def weigh_compressed(i):
                for s in range(2):
                    t.wait_ge(b["blocks"], second_of(i, s))
                    t.wait_ge(b["pt"], second_of(i, s))
                    for r in range(2):
                        probs = PTb[:, s, 4 * r:4 * r + 4, :].rearrange("p h q -> p (h q)")
                        ins = t.matmul(bank[4 + s][:, 256 + 128 * r:384 + 128 * r], probs,
                                       CKB[:, s, :, :].rearrange("p j d -> p (j d)"), start=True, stop=True)
                    ins.then_inc(b["pv"], 1)

            def latent_out(i):
                for s in range(2):
                    t.wait_ge(b["os"], second_of(i, s))
                    for r in range(2):
                        ins = t.matmul(bank[6 + s][:, 128:256], OS[:, s, r, :], Wvo[:, r, :], start=(r == 0), stop=(r == 1))
                    ins.then_inc(b["o"], 1)

            def turn_rotated(i):
                for s in range(2):
                    t.wait_ge(b["dup"], first_of(i, s))
                    t.wait_ge(b["copied"], first_of(i, s))
                    for n in range(5):
                        src = TT[:, s, 2 * n:2 * n + 2, :, :].rearrange("p h c d -> p (h c d)")
                        dst = bank[2 + s][:, 128 * n:128 * n + 128] if n < 4 else bank[4 + s][:, 128:256]
                        ins = t.transpose(dst, src, I128[:, :])
                    ins.then_inc(b["T"], 1)

            def step(i, before=True, after=True):
                if before:
                    latent_scores(i)
                if after:
                    turn_normed(i + 1)
                queries(i)
                if before:
                    weigh_compressed(i)
                if after:
                    compress(i + 1)
                if before:
                    latent_out(i)
                turn_rotated(i)

            turn_normed(0)
            compress(0)
            step(0, before=False)
            with t.Fori(1, PAIRS - 1) as i:
                step(i)
            step(PAIRS - 1, after=False)
            latent_scores(PAIRS)
            weigh_compressed(PAIRS)
            latent_out(PAIRS)

            t.wait_ge(b["x2"], T)
            def route(n):
                t.wait_ge(c["xeT"], n + 1)
                for m in range(4 * n, 4 * n + 4):
                    ins = t.matmul(bank[4][:, E * m:E * m + E], xeT[:, 128 * m:128 * m + 128], wrT[:, :], start=True, stop=True)
                ins.then_inc(c["logits"], 1)

            for n in range(4):
                for m in range(4):
                    t.wait_ge(c["xe"], 4 * n + m + 1)
                    ins = t.transpose(bank[n][:, 128 * m:128 * m + 128], xe[:, 4 * n + m, :], I128[:, :])
                ins.then_inc(c["turned"], 1)
            for n in range(4):
                route(n)

            def spread(tb, q):
                if counts(Q * tb + q):
                    t.wait_ge(c["cb"], Q * tb + q)
                t.sem_inc(b["pe_ready"], 1)
                t.matmul(bank[7][:, :], SELr[:, q, :], CT[:, bass.ds(512 * tb, 512)], start=True, stop=True).then_inc(c["cbm"], 1)

            def gate_and_up(tb, n):
                at = U * tb + n
                xh, xl_ = xeH[:, bass.ds(512 * tb, 512)], xeL[:, bass.ds(512 * tb, 512)]
                for name, wh, wl, bk in (("gate", GH, GL, n % 2), ("up", UH, UL, 2 + n % 2)):
                    if counts(at - 1):
                        t.wait_ge(c["silu"] if name == "gate" else c["hu"], at - 1)
                    for q, (w_, x_) in enumerate(((wh, xh), (wl, xh), (wh, xl_))):
                        ins = t.matmul(bank[bk][:, :], w_[:, n, :], x_, start=(q == 0), stop=(q == 2))
                    ins.then_inc(c[name], 1)

            def down(tb, n):
                at = U * tb + n
                o = (n - 3) % U
                t.wait_ge(c["hH"], at - 2)
                t.wait_ge(c["hL"], at - 2)
                if o == 0 and counts(tb):
                    t.wait_ge(c["ys"], tb)
                for q, (w_, h_) in enumerate(((WH, hH), (WL, hH), (WH, hL))):
                    ins = t.matmul(bank[6][:, :], w_[:, o, :], h_[:, slot(o), :], start=(o == 0 and q == 0),
                                   stop=(o == U - 1 and q == 2))
                ins.then_inc(c["down"], 1)

            def turn_back(tb):
                t.wait_ge(c["ys"], tb)
                t.wait_ge(out_free, tb)
                for n in range(4):
                    ins = t.transpose(bank[5][:, 128 * n:128 * n + 128], YS[:, 128 * n:128 * n + 128], I128[:, :])
                ins.then_inc(c["yT"], 1)

            def block_of(tb, first=False):
                for n in range(U):
                    if n in STARTS and not (first and n == 0):
                        spread(tb, run_of(n))
                    gate_and_up(tb, n)
                    if first and n == 1:
                        t.wait_ge(c["comb"], 5)
                        t.wait_ge(c["zero"], 1)
                        turn_weights(0)
                        turn_weights(1)
                        t.wait_ge(c["ct"], 1)
                        spread(tb, 0)
                    if first and n == 2:
                        for m in (2, 3):
                            t.wait_ge(c["ct"], m - 1)
                            turn_weights(m)
                    if n >= 3 or not first:
                        down(tb, n)
                    if n == 6 and not first:
                        turn_back(tb)

            def turn_weights(m):
                for n in range(4):
                    ins = t.transpose(bank[4 + m % 2][0:32, 128 * n:128 * n + 128], comb[:, 4 * m + n, :], I128[:, :])
                ins.then_inc(c["combT"], 1)

            t.wait_ge(c["w_lo"], PARTS * E)
            t.wait_ge(sel_ready, 1)
            t.wait_ge(c["xeL"], 4)
            block_of(0, True)
            with t.Fori(1, TB) as tb:
                block_of(tb)
            for n in range(3):
                down(TB, n)
            turn_back(TB)


def kernel(x, ctx_1024, L0_xattn_Wv, L0_xattn_Wk, L0_xattn_Wq, L0_xattn_Wo, L0_xattn_bo, L0_attn_W_dkv, L0_attn_W_uk,
           L0_attn_W_uv, L0_attn_W_dq, L0_attn_W_uq, L0_attn_W_qr, L0_attn_W_kr, L0_attn_W_out, L0_attn_idx_wq,
           L0_attn_idx_wk, L0_attn_idx_w, L0_attn_raw_delta, L0_ffn_w_router, L0_ffn_w_gate, L0_ffn_w_up, L0_ffn_w_down):
    import numpy as np
    import concourse.bacc as bacc
    from concourse.bass_utils import run_bass_kernel_spmd

    a = lambda v: np.asarray(v)
    p = np.arange(128)
    angle = (p[:, None] % L) * (1.0 / 10000.0 ** (2.0 * np.arange(16) / DR))[None, :]
    chosen = np.zeros((32, Q, 128), np.float32)
    for q, n in enumerate(STARTS):
        e = (128 * n + p) // I
        chosen[e, q, p] = chosen[E + e, q, p] = 1.0
    arrays = {
        "x": a(x).reshape(B * L, D),
        "ctxT": a(ctx_1024).transpose(2, 0, 1).reshape(D, B * S),
        "wq": a(L0_xattn_Wq).T, "wk": a(L0_xattn_Wk).T, "wv": a(L0_xattn_Wv).T, "wo": a(L0_xattn_Wo).T,
        "bo": a(L0_xattn_bo),
        "w_dq": a(L0_attn_W_dq),
        "w_kv": np.concatenate([a(L0_attn_W_dkv), a(L0_attn_W_kr)], axis=1),
        "w_uqT": a(L0_attn_W_uq).reshape(CQ, NH, DH).transpose(2, 1, 0),
        "w_ukT": a(L0_attn_W_uk).reshape(CKV, NH, DH).transpose(2, 1, 0),
        "w_uvT": a(L0_attn_W_uv).reshape(CKV, NH, DH).transpose(2, 1, 0),
        "w_qr": a(L0_attn_W_qr).reshape(CQ, NH, DR),
        "w_out": a(L0_attn_W_out).reshape(NH, DH, D).transpose(1, 0, 2),
        "raw_delta": a(L0_attn_raw_delta),
        "w_router": a(L0_ffn_w_router).T,
        "w_gate": a(L0_ffn_w_gate).transpose(2, 0, 1).reshape(D, U, 128),
        "w_up": a(L0_ffn_w_up).transpose(2, 0, 1).reshape(D, U, 128),
        "w_down": a(L0_ffn_w_down).transpose(0, 2, 1).reshape(U, 128, D).transpose(1, 0, 2),
        "ident": np.eye(128, dtype=np.float32),
        "head_mask": ((p[:, None] // XD) % G == np.arange(G)[None, :]).astype(np.float32),
        "cos_pos": np.cos(angle).astype(np.float32),
        "sin_pos": np.sin(angle).astype(np.float32),
        "own_sequence": (p[:, None] // L == np.arange(4)[None, :]).astype(np.float32),
        "expert_rank": np.tile(E - np.arange(E, dtype=np.float32), (128, 1)),
        "expert_sel": chosen,
    }
    arrays = {n: np.ascontiguousarray(v) for n, v in arrays.items()}
    nc = bacc.Bacc("TRN2", target_bir_lowering=False, num_devices=1)
    aps = {n: nc.dram_tensor(n, v.shape, mybir.dt.from_np(v.dtype), kind="ExternalInput").ap() for n, v in arrays.items()}
    aps["out"] = nc.dram_tensor("out", (B * L, D), F32, kind="ExternalOutput").ap()
    build(nc, **aps)
    r = run_bass_kernel_spmd(nc, [arrays], core_ids=[0])
    return r.results[0]["out"].reshape(B, L, D)
```
